# Optimizing a Trainium2 kernel written in Bass

```python
import numpy as np
import jax
import jax.numpy as jnp

def _softmax(x, axis=-1):
    return jax.nn.softmax(x, axis=axis)
def _gelu(x):
    return jax.nn.gelu(x, approximate=True)
def _silu(x):
    return jax.nn.silu(x)
def _sigmoid(x):
    return jax.nn.sigmoid(x)
def _layernorm(x, axis=-1, eps=1e-5):
    m = jnp.mean(x, axis=axis, keepdims=True)
    v = jnp.var(x, axis=axis, keepdims=True)
    return (x - m) / jnp.sqrt(v + eps)
def _scatter_add(tgt, idx, src, axis=0):
    return tgt.at[idx].add(src)
def _segment_sum(src, seg, n):
    return jax.ops.segment_sum(src, seg, n)

kernel_name = 'mk_adj_preln_d1_adj_256_1eaeac'

def setup_inputs(seed: int = 0):
    np.random.seed(seed)
    _w = jnp.asarray
    def _rec_inputs():
        import jax
        import jax.numpy as jnp
        _gk = jax.random.key(seed)
        x = -0.0005207 + 1.001 * jax.random.normal(jax.random.fold_in(_gk, 1), (8, 2048, 256), jnp.float32)
        _w = (1.0 + jnp.arange(2048, dtype=jnp.float32)) ** -0.5
        _w = _w / _w.mean()
        _pij = jnp.clip(0.00390625 * _w[:, None] * _w[None, :], 0.0, 1.0)
        _a = jax.random.uniform(jax.random.fold_in(_gk, 2), (8, 2048, 2048)) < _pij
        adj = _a.astype(jnp.int32)
        return x, adj
    x, adj = _rec_inputs()
    def _L0_gnn_setup():
        import jax, jax.numpy as jnp
        import numpy as np
        B, N, D = (8, 1024, 256)
        H, HO = (4, 64)
        T = 5
        NEG = -1000000000.0
        EPS = 1e-06
        key = jax.random.key(seed)
        ks = jax.random.split(key, 6)
        nodes_embed = jax.random.normal(ks[0], (B, N, D), dtype=jnp.float32)
        node_adj = jax.random.randint(ks[1], (B, N, N), 0, T + 1)
        W = jax.random.normal(ks[2], (H, D, HO), dtype=jnp.float32) * (1.0 / np.sqrt(D))
        a_src = jax.random.normal(ks[3], (H, T, HO), dtype=jnp.float32) * 0.1
        a_dst = jax.random.normal(ks[4], (H, T, HO), dtype=jnp.float32) * 0.1
        bias = jnp.zeros((H, HO), dtype=jnp.float32)
        ln_gamma = jnp.ones((H, HO), dtype=jnp.float32)
        ln_beta = jnp.zeros((H, HO), dtype=jnp.float32)
        return {'nodes_embed': nodes_embed, 'node_adj': node_adj, 'W': W, 'a_src': a_src, 'a_dst': a_dst, 'bias': bias, 'ln_gamma': ln_gamma, 'ln_beta': ln_beta}
    _L0_gnn_all = _L0_gnn_setup()
    _L0_gnn_in = {k: v for k, v in _L0_gnn_all.items() if k in ('W', 'a_src', 'a_dst', 'bias', 'ln_gamma', 'ln_beta', )}
    del _L0_gnn_all

    return {
        "x": x,
        "adj": adj,
        "L0_gnn_W": _L0_gnn_in["W"],
        "L0_gnn_a_src": _L0_gnn_in["a_src"],
        "L0_gnn_a_dst": _L0_gnn_in["a_dst"],
        "L0_gnn_bias": _L0_gnn_in["bias"],
        "L0_gnn_ln_gamma": _L0_gnn_in["ln_gamma"],
        "L0_gnn_ln_beta": _L0_gnn_in["ln_beta"],
    }

def reference(x, adj, L0_gnn_W, L0_gnn_a_src, L0_gnn_a_dst, L0_gnn_bias, L0_gnn_ln_gamma, L0_gnn_ln_beta):
    import jax
    import jax.numpy as jnp
    def _L0_gnn_ref(nodes_embed, node_adj, W, a_src, a_dst, bias, ln_gamma, ln_beta):
        import jax, jax.numpy as jnp
        import numpy as np
        B, N, D = (8, 1024, 256)
        H, HO = (4, 64)
        T = 5
        NEG = -1000000000.0
        EPS = 1e-06
        h = jnp.einsum('bnd,hde->bhne', nodes_embed, W)
        e_src = jnp.einsum('bhne,hte->bhtn', h, a_src)
        e_dst = jnp.einsum('bhne,hte->bhtn', h, a_dst)
        n_types = a_src.shape[1]
        weight = jnp.zeros(h.shape[:2] + (h.shape[2], h.shape[2]), dtype=h.dtype)
        for t in range(n_types):
            mask = (node_adj == t + 1).astype(h.dtype)[:, None]
            weight = weight + mask * (e_src[:, :, t, :, None] + e_dst[:, :, t, None, :])
        weight = jax.nn.leaky_relu(weight, negative_slope=0.01)
        weight = jnp.where(node_adj[:, None] == 0, NEG, weight)
        attention = jax.nn.softmax(weight, axis=-1)
        dst = jnp.einsum('bhij,bhje->bhie', attention, h) + bias[None, :, None, :]
        out = jax.nn.relu(dst) + h
        mu = out.mean(axis=-1, keepdims=True)
        var = out.var(axis=-1, keepdims=True)
        out = (out - mu) / jnp.sqrt(var + EPS) * ln_gamma[None, :, None, :] + ln_beta[None, :, None, :]
        b, hh, n, e = out.shape
        return out.transpose(0, 2, 1, 3).reshape(b, n, hh * e)

    h = jnp.maximum(_layernorm(x, axis=-1), 0.0)
    x = x + _L0_gnn_ref(h, adj, L0_gnn_W, L0_gnn_a_src, L0_gnn_a_dst, L0_gnn_bias, L0_gnn_ln_gamma, L0_gnn_ln_beta)
    return x


_drawn_inputs = setup_inputs


def setup_inputs(seed=0):
    import zlib

    import numpy as np

    out = dict(_drawn_inputs(seed))
    spreads = {'L0_gnn_bias': (0.0, 0.1), 'L0_gnn_ln_gamma': (1.0, 0.2), 'L0_gnn_ln_beta': (0.0, 0.1)}
    factors = {}
    for name, (base, spread) in spreads.items():
        noise = np.random.default_rng([zlib.crc32(name.encode()), seed]).standard_normal(out[name].shape)
        drawn = base * np.exp(spread * noise) if base else spread * noise
        out[name] = jnp.asarray(drawn.astype(out[name].dtype))
    for name, factor in factors.items():
        out[name] = (out[name] * factor).astype(out[name].dtype)
    return out
```

```python
from contextlib import ExitStack

import concourse.bass as bass
from concourse import mybir

P = 128
HEADS, HEAD_DIM, TYPES = 4, 64, 5
DIM = HEADS * HEAD_DIM
KC = DIM // P
AUG = HEAD_DIM + 1
PROJ = 2 * HEADS * TYPES
SRC, DST = 0, HEADS * TYPES
GCOLS = HEADS * 4 * AUG
UNIT_TILES = 4
UNIT = UNIT_TILES * P
SCALE = 64.0
LN_EPS, HEAD_EPS = 1e-5, 1e-6
NO_EDGE = -1e9
MAX_DST, MAX_SRC, MAX_H, MIN_H = 4.0, 40.0, 16.0, 0.25

START = 6


def done(n):
    return n + START + 1


def freed(n, depth):
    return n + START + 1 - depth


def wait_apart(engine, semaphore, value, passed):
    engine.wait_ge(semaphore, value)
    engine.sem_inc(passed, 1)


F32, F16, F8, I32 = mybir.dt.float32, mybir.dt.float16, mybir.dt.float8e4, mybir.dt.int32
ALU = mybir.AluOpType
ACT = mybir.ActivationFunctionType
AX = mybir.AxisListType


def build(nc, x, adj, W, a_src, a_dst, bias, gamma, beta, out):
    batches, nodes, _ = x.shape
    tiles = nodes // P
    all_tiles = batches * tiles
    units = all_tiles // UNIT_TILES
    batch_units = tiles // UNIT_TILES
    groups = tiles // 4

    x_rows = x.rearrange("b n d -> (b n) d")
    adj_rows = adj.rearrange("b n m -> (b n) m")
    out_rows = out.rearrange("b n d -> (b n) d")
    h_dram = nc.dram_tensor("h_rows", (batches * nodes, DIM), F32).ap()
    uv_dram = nc.dram_tensor("uv_rows", (batches * nodes, GCOLS), F16).ap()
    score_dram = nc.dram_tensor("score_rows", (batches * nodes, PROJ), F32).ap()
    scoreT_dram = nc.dram_tensor("score_cols", (PROJ, batches * nodes), F32).ap()
    hmean_dram = nc.dram_tensor("h_mean", (batches, DIM), F32).ap()

    keep = ExitStack()
    with keep:
        def sb(stack, name, shape, dt):
            return stack.enter_context(nc.sbuf_tensor(name, shape, dt))

        def ps(stack, name, shape, dt):
            return stack.enter_context(nc.psum_tensor(name, shape, dt))

        def sem(stack, name):
            return stack.enter_context(nc.semaphore(name))

        ident16 = sb(keep, "ident16", [P, P], F16)
        ident32 = sb(keep, "ident32", [P, P], F32)
        bias_b = sb(keep, "bias_b", [P, DIM], F32)
        gamma_b = sb(keep, "gamma_b", [P, DIM], F32)
        beta_b = sb(keep, "beta_b", [P, DIM], F32)
        rho = sb(keep, "rho", [P, all_tiles, HEADS], F32)
        neg_d = sb(keep, "neg_d", [P, batches * HEADS * tiles], F32)
        eps = sb(keep, "eps", [P, 2], F32)
        extremes = sb(keep, "extremes", [P, 3, HEADS], F32)
        sum_a = sb(keep, "sum_a", [P, UNIT_TILES * (units + 2)], F32)
        sum_aa = sb(keep, "sum_aa", [P, 2 * UNIT_TILES], F32)
        verdict = sb(keep, "verdict", [P, 1], I32)

        with ExitStack() as early:
            wx = sb(early, "wx", [P, KC, DIM + PROJ], F32)
            setup_block(nc, sb, ps, sem, W, a_src, a_dst, bias, gamma, beta, wx, ident16, ident32,
                        bias_b, gamma_b, beta_b, eps, extremes, sum_aa)
            rows_block(nc, sb, ps, sem, batches, tiles, groups, x_rows, wx, ident32, rho, neg_d,
                       eps, extremes, h_dram, uv_dram, score_dram, scoreT_dram, hmean_dram)
        edges_block(nc, sb, ps, sem, batches, tiles, units, batch_units, x_rows, adj_rows, out_rows,
                    h_dram, uv_dram, scoreT_dram, hmean_dram, ident16, bias_b, gamma_b, beta_b,
                    rho, neg_d, eps, sum_a, sum_aa)
        verdict_block(nc, sb, ps, sem, all_tiles, extremes, sum_a, sum_aa, verdict)
        general_block(nc, sb, ps, sem, batches, tiles, all_tiles, x_rows, adj_rows, out_rows, h_dram,
                      score_dram, scoreT_dram, ident32, bias_b, gamma_b, beta_b, eps, verdict)


def setup_block(nc, sb, ps, sem, W, a_src, a_dst, bias, gamma, beta, wx, ident16, ident32,
                bias_b, gamma_b, beta_b, eps, extremes, sum_aa):
    with ExitStack() as s:
        a_t = sb(s, "a_t", [P, HEADS // 2, PROJ], F32)
        w_t = sb(s, "w_t", [P, HEADS // 2, KC, P], F32)
        w_ps = ps(s, "w_ps", [P, HEADS // 2, KC, P], F32)
        v_ps = ps(s, "v_ps", [P, KC, 256], F32)
        loaded, broadcast = sem(s, "loaded"), sem(s, "broadcast")
        a_loaded, a_clear = sem(s, "a_loaded"), sem(s, "a_clear")
        made, transposed, w_ready = sem(s, "made"), sem(s, "transposed"), sem(s, "w_ready")
        projected = sem(s, "projected")
        with nc.Block() as block:

            @block.sync
            def _(sp):
                for h in range(HEADS):
                    sp.dma_start(wx[:, :, h * HEAD_DIM:(h + 1) * HEAD_DIM],
                                 W[h].rearrange("(k p) e -> p k e", p=P)).then_inc(loaded, 16)
                sp.wait_ge(a_clear, 1)
                for first, a in ((SRC, a_src), (DST, a_dst)):
                    for h in range(HEADS):
                        row, col = (h % 2) * HEAD_DIM, first + h * TYPES
                        with nc.allow_non_contiguous_dma(reason="1280 numbers, once"):
                            sp.dma_start(a_t[row:row + HEAD_DIM, h // 2, col:col + TYPES],
                                         a[h].rearrange("t e -> e t")).then_inc(a_loaded, 16)
                for row, to in ((bias, bias_b), (gamma, gamma_b), (beta, beta_b)):
                    flat = row.rearrange("h e -> (h e)").rearrange("(o n) -> o n", o=1)
                    sp.dma_start(to[:, :], flat.to_broadcast([P, DIM])).then_inc(broadcast, 16)
                sp.wait_ge(broadcast, 48)

            @block.gpsimd
            def _(pool):
                nc.gpsimd.memset(a_t[:], 0.0).then_inc(a_clear, 1)
                nc.gpsimd.memset(eps[:, 0:1], LN_EPS)
                nc.gpsimd.memset(eps[:, 1:2], HEAD_EPS)
                nc.gpsimd.memset(extremes[:], 0.0)
                nc.gpsimd.memset(sum_aa[:], 0.0)
                nc.gpsimd.memset(ident16[:], 0.0)
                nc.gpsimd.memset(ident32[:], 0.0).then_inc(made, 1)
                pool.wait_ge(made, 1)
                for ident in (ident16, ident32):
                    nc.gpsimd.affine_select(out=ident[:], in_=ident[:], compare_op=ALU.not_equal,
                                            fill=1.0, base=0, pattern=[[-1, P]],
                                            channel_multiplier=1).then_inc(made, 1)

            @block.tensor
            def _(pe):
                pe.wait_ge(loaded, 16 * HEADS)
                pe.wait_ge(made, 3)
                for pair in range(HEADS // 2):
                    for k in range(KC):
                        last = nc.tensor.transpose(w_ps[:, pair, k, :],
                                                   wx[:, k, pair * P:(pair + 1) * P], ident32[:])
                last.then_inc(transposed, 1)
                pe.wait_ge(w_ready, 1)
                pe.wait_ge(a_loaded, 16 * 2 * HEADS)
                for k in range(KC):
                    for pair in range(HEADS // 2):
                        last = nc.tensor.matmul(v_ps[:, k, 0:PROJ], w_t[:, pair, k, :],
                                                a_t[:, pair, :], start=pair == 0,
                                                stop=pair == HEADS // 2 - 1)
                last.then_inc(projected, 1)

            @block.vector
            def _(dve):
                dve.wait_ge(transposed, 1)
                nc.vector.tensor_copy(w_t[:], w_ps[:]).then_inc(w_ready, 1)
                dve.wait_ge(projected, 1)
                nc.vector.tensor_copy(wx[:, :, DIM:DIM + PROJ], v_ps[:, :, 0:PROJ])


def rows_block(nc, sb, ps, sem, batches, tiles, groups, x_rows, wx, ident32, rho, neg_d, eps,
               extremes, h_dram, uv_dram, score_dram, scoreT_dram, hmean_dram):
    pairs = tiles // 2
    span = tiles * P
    with ExitStack() as s:
        xt = [sb(s, f"xt{q}", [P, tiles, DIM], F32) for q in (0, 1)]
        haug = [sb(s, f"haug{q}", [P, tiles, HEADS, AUG], F32) for q in (0, 1)]
        score = [sb(s, f"score{q}", [P, tiles, PROJ], F32) for q in (0, 1)]
        scoreT = [sb(s, f"scoreT{q}", [PROJ, span], F32) for q in (0, 1)]
        stats = sb(s, "stats", [P, tiles, 6], F32)
        mean_var = sb(s, "mean_var", [P, tiles, 2], F32)
        deviation = sb(s, "deviation", [P, tiles], F32)
        rstd = sb(s, "rstd", [P, tiles], F32)
        shift = sb(s, "shift", [P, tiles], F32)
        normed = [sb(s, f"normed{i}", [P, DIM], F32) for i in range(4)]
        normed_t = [sb(s, f"normed_t{i}", [P, KC, 4 * P], F32) for i in (0, 1)]
        u_exp = sb(s, "u_exp", [P, tiles, HEADS], F32)
        v_exp = sb(s, "v_exp", [P, tiles, HEADS], F32)
        whole = [sb(s, f"whole{i}", [P, HEADS, 2, AUG], F32) for i in range(4)]
        parts = [sb(s, f"parts{i}", [P, 4, HEADS, 2, 2, AUG], F16) for i in (0, 1)]
        ones = sb(s, "ones", [P, 1], F32)
        hmean = sb(s, "hmean", [1, DIM], F32)
        batch_max = sb(s, "batch_max", [P, 3, HEADS], F32)
        t_ps = [ps(s, f"t_ps{i}", [P, KC, 2 * P], F32) for i in (0, 1)]
        h_ps = [ps(s, f"h_ps{i}", [P, 512], F32) for i in (0, 1)]
        sT_ps = [ps(s, f"sT_ps{i}", [P, 4 * P], F32) for i in (0, 1)]
        mean_ps = ps(s, "mean_ps", [P, 512], F32)

        ones_made = sem(s, "ones_made")
        stats_done, mv_done, dev_done = sem(s, "stats_done"), sem(s, "mv_done"), sem(s, "dev_done")
        rstd_done, shift_done = sem(s, "rstd_done"), sem(s, "shift_done")
        normed_done, transposed = sem(s, "normed_done"), sem(s, "transposed")
        t_copied, h_made, h_copied = sem(s, "t_copied"), sem(s, "h_made"), sem(s, "h_copied")
        e_copied, sT_made, sT_copied = sem(s, "e_copied"), sem(s, "sT_made"), sem(s, "sT_copied")
        mean_made, mean_copied = sem(s, "mean_made"), sem(s, "mean_copied")
        exps_done, whole_done = sem(s, "exps_done"), sem(s, "whole_done")
        hi_done, lo_done, max_done = sem(s, "hi_done"), sem(s, "lo_done"), sem(s, "max_done")
        x_loaded = [sem(s, f"x_loaded{q}") for q in (0, 1)]
        rows_stored = [sem(s, f"rows_stored{q}") for q in (0, 1)]
        uv_stored = [sem(s, f"uv_stored{i}") for i in (0, 1)]
        mean_stored, passed = sem(s, "mean_stored"), sem(s, "passed")
        STORES = HEADS + 2

        with nc.Block() as block:

            @block.gpsimd
            def _(pool):
                for one in (stats_done, mv_done, dev_done, rstd_done, shift_done, normed_done,
                            transposed, t_copied, h_made, h_copied, e_copied, sT_made, sT_copied,
                            mean_made, mean_copied, exps_done, whole_done, hi_done, lo_done):
                    pool.sem_inc(one, START)
                for one in (*x_loaded, *rows_stored, *uv_stored, mean_stored):
                    pool.sem_inc(one, 16 * START)
                nc.gpsimd.memset(ones[:], 1.0)
                for q in (0, 1):
                    last = nc.gpsimd.memset(haug[q][:, :, :, HEAD_DIM:AUG], 1.0)
                last.then_inc(ones_made, 1)
                with pool.Fori(0, batches) as b:
                    for t in range(tiles):
                        pool.wait_ge(hi_done, done(tiles * b + t))
                        nc.gpsimd.tensor_tensor(parts[t // 4 % 2][:, t % 4, :, :, 1, :], whole[t % 4][:],
                                                parts[t // 4 % 2][:, t % 4, :, :, 0, :],
                                                ALU.subtract).then_inc(lo_done, 1)

            @block.sync
            def _(sp):
                def load(b, q):
                    rows = x_rows[bass.ds(b * span, span), :].rearrange("(t p) d -> p t d", p=P)
                    sp.dma_start(xt[q][:], rows).then_inc(x_loaded[q], 16)

                def store(i, q):
                    b = 2 * i + q
                    rows = bass.ds(b * span, span)
                    sp.wait_ge(h_copied, done(tiles * b + tiles - 1))
                    for h in range(HEADS):
                        cols = slice(h * HEAD_DIM, (h + 1) * HEAD_DIM)
                        sp.dma_start(h_dram[rows, cols].rearrange("(t p) e -> p t e", p=P),
                                     haug[q][:, :, h, 0:HEAD_DIM]).then_inc(rows_stored[q], 16)
                    sp.wait_ge(e_copied, done(tiles * b + tiles - 1))
                    sp.dma_start(score_dram[rows, :].rearrange("(t p) c -> p t c", p=P),
                                 score[q][:]).then_inc(rows_stored[q], 16)
                    wait_apart(sp, sT_copied, done(groups * b + groups - 1), passed)
                    sp.dma_start(scoreT_dram[:, rows], scoreT[q][:]).then_inc(rows_stored[q], 16)
                    sp.wait_ge(mean_copied, done(b))
                    sp.dma_start(hmean_dram[bass.ds(b, 1), :], hmean[:]).then_inc(mean_stored, 16)
                    for g in range(groups):
                        sp.wait_ge(lo_done, done(tiles * b + 4 * g + 3))
                        four = uv_dram[bass.ds(b * span + g * 4 * P, 4 * P), :]
                        sp.dma_start(four.rearrange("(t p) c -> p t c", p=P),
                                     parts[g % 2][:].rearrange("p t h u l e -> p t (h u l e)")
                                     ).then_inc(uv_stored[g % 2], 16)

                for q in (0, 1):
                    load(q, q)
                if batches > 2:
                    with sp.Fori(0, batches // 2 - 1) as i:
                        for q in (0, 1):
                            sp.wait_ge(normed_done, done(tiles * (2 * i + q) + tiles - 1))
                            load(2 * i + q + 2, q)
                            store(i, q)
                for q in (0, 1):
                    store(batches // 2 - 1, q)
                for q in (0, 1):
                    sp.wait_ge(rows_stored[q], 16 * (START + STORES * (batches // 2)))
                    sp.wait_ge(uv_stored[q], 16 * (START + batches * groups // 2))
                sp.wait_ge(mean_stored, 16 * (START + batches))

            @block.scalar
            def _(act):
                with act.Fori(0, batches // 2) as i:
                    for q in (0, 1):
                        b = 2 * i + q
                        act.wait_ge(mv_done, done(b))
                        nc.scalar.activation(deviation[:], mean_var[:, :, 1], ACT.Sqrt,
                                             bias=eps[:, 0:1]).then_inc(dev_done, 1)
                        act.wait_ge(shift_done, done(b))

                        def norm(t):
                            act.wait_ge(transposed, freed(pairs * b + t // 2, 2))
                            nc.scalar.activation(normed[t % 4][:], xt[q][:, t, :], ACT.Relu,
                                                 scale=rstd[:, t:t + 1], bias=shift[:, t:t + 1]
                                                 ).then_inc(normed_done, 1)

                        def copy_h(t):
                            if t == 0:
                                act.wait_ge(rows_stored[q], 16 * (STORES * i + START))
                                act.wait_ge(mean_made, freed(b, 2))
                            act.wait_ge(h_made, done(tiles * b + t))
                            nc.scalar.activation(
                                haug[q][:, t, :, 0:HEAD_DIM],
                                h_ps[t % 2][:, 0:DIM].rearrange("p (h e) -> p h e", h=HEADS),
                                ACT.Copy).then_inc(h_copied, 1)

                        for t in range(tiles + 4):
                            if t < tiles:
                                norm(t)
                            if t >= 4:
                                copy_h(t - 4)
                        act.wait_ge(e_copied, done(tiles * b + tiles - 1))
                        act.wait_ge(whole_done, freed(tiles * b, 1))
                        for first, scale, to in ((DST, 1.0, u_exp[:]), (DST, 0.01, v_exp[:]),
                                                 (SRC, 0.99, rho[:, bass.ds(b * tiles, tiles), :])):
                            last = nc.scalar.activation(
                                to, score[q][:, :, first:first + HEADS * TYPES:TYPES], ACT.Exp,
                                scale=scale)
                        last.then_inc(exps_done, 1)
                        for t in range(tiles):
                            if t % 4 == 0:
                                act.wait_ge(uv_stored[t // 4 % 2],
                                            16 * (groups // 2 * b + t // 8 + START))
                            act.wait_ge(whole_done, done(tiles * b + t))
                            nc.scalar.activation(parts[t // 4 % 2][:, t % 4, :, :, 0, :],
                                                 whole[t % 4][:], ACT.Copy).then_inc(hi_done, 1)

            @block.tensor
            def _(pe):
                pe.wait_ge(ones_made, 1)
                with pe.Fori(0, batches // 2) as i:
                    for q in (0, 1):
                        b = 2 * i + q

                        def transpose_pair(r):
                            pe.wait_ge(normed_done, done(tiles * b + 2 * r + 1))
                            pe.wait_ge(t_copied, freed(pairs * b + r, 2))
                            for t in (0, 1):
                                for k in range(KC):
                                    last = nc.tensor.transpose(
                                        t_ps[r % 2][:, k, t * P:(t + 1) * P],
                                        normed[(2 * r + t) % 4][:, k * P:(k + 1) * P], ident32[:])
                            last.then_inc(transposed, 1)

                        def product(t):
                            pe.wait_ge(t_copied, done(pairs * b + t // 2))
                            pe.wait_ge(e_copied, freed(tiles * b + t, 2))
                            for k in range(KC):
                                last = nc.tensor.matmul(
                                    h_ps[t % 2][:, 0:DIM + PROJ],
                                    normed_t[t // 4 % 2][:, k, t % 4 * P:(t % 4 + 1) * P],
                                    wx[:, k, :], start=k == 0, stop=k == KC - 1)
                            last.then_inc(h_made, 1)

                        def scores_across(g):
                            pe.wait_ge(sT_copied, freed(groups * b + g, 2))
                            for k in range(KC):
                                last = nc.tensor.matmul(sT_ps[g % 2][0:PROJ, :],
                                                        wx[:, k, DIM:DIM + PROJ],
                                                        normed_t[g % 2][:, k, :], start=k == 0,
                                                        stop=k == KC - 1)
                            last.then_inc(sT_made, 1)

                        for r in range(pairs + 1):
                            if r < pairs:
                                transpose_pair(r)
                            if r >= 1:
                                product(2 * r - 2)
                                product(2 * r - 1)
                                if r % 2 == 0:
                                    scores_across(r // 2 - 1)
                        pe.wait_ge(h_copied, done(tiles * b + tiles - 1))
                        pe.wait_ge(mean_copied, freed(b, 1))
                        for t in range(tiles):
                            last = nc.tensor.matmul(mean_ps[0:1, 0:HEADS * AUG], ones[:],
                                                    haug[q][:, t, :, :].rearrange("p h e -> p (h e)"),
                                                    start=t == 0, stop=t == tiles - 1)
                        last.then_inc(mean_made, 1)

            @block.vector
            def _(dve):
                with dve.Fori(0, batches // 2) as i:
                    for q in (0, 1):
                        b = 2 * i + q
                        dve.wait_ge(x_loaded[q], 16 * done(i))
                        for t in range(tiles):
                            last = nc.vector.bn_stats(stats[:, t, :], xt[q][:, t, :])
                        last.then_inc(stats_done, 1)
                        wait_apart(dve, stats_done, done(b), passed)
                        for t in range(tiles):
                            last = nc.vector.bn_aggr(mean_var[:, t, :], stats[:, t, :])
                        last.then_inc(mv_done, 1)
                        dve.wait_ge(dev_done, done(b))
                        dve.wait_ge(normed_done, freed(tiles * b, 1))
                        nc.vector.reciprocal(rstd[:], deviation[:]).then_inc(rstd_done, 1)
                        dve.wait_ge(rstd_done, done(b))
                        nc.vector.scalar_tensor_tensor(
                            out=shift[:], in0=mean_var[:, :, 0], scalar=-1.0, in1=rstd[:],
                            op0=ALU.mult, op1=ALU.mult).then_inc(shift_done, 1)

                        def copy_score(t):
                            if t == 0:
                                dve.wait_ge(rows_stored[q], 16 * (STORES * i + START))
                            dve.wait_ge(h_copied, done(tiles * b + t))
                            nc.vector.tensor_copy(score[q][:, t, :], h_ps[t % 2][:, DIM:DIM + PROJ]
                                                  ).then_inc(e_copied, 1)

                        for r in range(pairs + 1):
                            if r < pairs:
                                g = r // 2
                                dve.wait_ge(transposed, done(pairs * b + r))
                                dve.wait_ge(sT_made, freed(groups * b + g, 2))
                                nc.vector.tensor_copy(normed_t[g % 2][:, :, r % 2 * 2 * P:(r % 2 + 1) * 2 * P],
                                                      t_ps[r % 2][:]).then_inc(t_copied, 1)
                            if r >= 1:
                                copy_score(2 * r - 2)
                                copy_score(2 * r - 1)
                                if r % 2 == 0:
                                    g = r // 2 - 1
                                    dve.wait_ge(sT_made, done(groups * b + g))
                                    nc.vector.tensor_copy(scoreT[q][:, g * 4 * P:(g + 1) * 4 * P],
                                                          sT_ps[g % 2][0:PROJ, :]).then_inc(sT_copied, 1)
                        dve.wait_ge(e_copied, done(tiles * b + tiles - 1))
                        dve.wait_ge(h_copied, done(tiles * b + tiles - 1))
                        nc.vector.tensor_scalar(
                            neg_d[:, bass.ds(b * HEADS * tiles, HEADS * tiles)].rearrange(
                                "p (h t) -> p h t", h=HEADS),
                            score[q][:, :, DST:DST + HEADS * TYPES:TYPES].rearrange("p t h -> p h t"),
                            -1.0, None, ALU.mult)
                        nc.vector.tensor_reduce(
                            batch_max[:, 0, :], haug[q][:, :, :, 0:HEAD_DIM].rearrange("p t h e -> p h t e"),
                            axis=AX.XY, op=ALU.max, apply_absolute_value=True)
                        for n, first in ((1, DST), (2, SRC)):
                            last = nc.vector.tensor_reduce(
                                batch_max[:, n, :],
                                score[q][:, :, first:first + HEADS * TYPES:TYPES].rearrange("p t h -> p h t"),
                                axis=AX.X, op=ALU.max, apply_absolute_value=True)
                        last.then_inc(max_done, 1)
                        dve.wait_ge(max_done, 2 * b + 1)
                        nc.vector.tensor_tensor(extremes[:], extremes[:], batch_max[:], ALU.max
                                                ).then_inc(max_done, 1)
                        dve.wait_ge(max_done, 2 * b + 2)
                        dve.wait_ge(mean_made, done(b))
                        dve.wait_ge(mean_stored, 16 * (b + START))
                        nc.vector.tensor_scalar(
                            hmean[:].rearrange("o (h e) -> o h e", h=HEADS),
                            mean_ps[0:1, 0:HEADS * AUG].rearrange("o (h e) -> o h e", h=HEADS)[:, :, 0:HEAD_DIM],
                            1.0 / span, None, ALU.mult).then_inc(mean_copied, 1)
                        dve.wait_ge(exps_done, done(b))
                        for t in range(tiles):
                            dve.wait_ge(lo_done, freed(tiles * b + t, 4))
                            for n, factor in ((0, u_exp), (1, v_exp)):
                                last = nc.vector.scalar_tensor_tensor(
                                    out=whole[t % 4][:, :, n, :], in0=haug[q][:, t, :, :], scalar=SCALE,
                                    in1=factor[:, t, :].unsqueeze(2).to_broadcast([P, HEADS, AUG]),
                                    op0=ALU.mult, op1=ALU.mult)
                            last.then_inc(whole_done, 1)


def edges_block(nc, sb, ps, sem, batches, tiles, units, batch_units, x_rows, adj_rows, out_rows,
                h_dram, uv_dram, scoreT_dram, hmean_dram, ident16, bias_b, gamma_b, beta_b,
                rho, neg_d, eps, sum_a, sum_aa):
    all_tiles = UNIT_TILES * units
    last_tile = all_tiles - 1
    with ExitStack() as s:
        edge = [sb(s, f"edge{i}", [P, tiles * P], I32) for i in (0, 1)]
        a_row = [sb(s, f"a_row{i}", [P, tiles, P], F16) for i in (0, 1)]
        at = [sb(s, f"at{i}", [P, tiles, UNIT], F8) for i in (0, 1)]
        mask = [sb(s, f"mask{i}", [P, HEADS, tiles, UNIT], F8) for i in (0, 1)]
        uv = sb(s, "uv", [P, 2 * tiles, HEADS, 4 * AUG], F16)
        s_row = sb(s, "s_row", [P, HEADS, UNIT], F32)
        h_own = [sb(s, f"h_own{i}", [P, DIM], F32) for i in (0, 1)]
        x_own = [sb(s, f"x_own{i}", [P, DIM], F32) for i in (0, 1)]
        hmean_b = [sb(s, f"hmean_b{i}", [P, DIM], F32) for i in (0, 1)]
        seg = sb(s, "seg", [P, HEADS, 6 * AUG], F32)
        two = sb(s, "two", [P, HEADS, 2 * AUG], F32)
        num = sb(s, "num", [P, HEADS, AUG], F32)
        lone = sb(s, "lone", [P, HEADS], F32)
        rden = sb(s, "rden", [P, HEADS], F32)
        base = sb(s, "base", [P, DIM], F32)
        o = sb(s, "o", [P, DIM], F32)
        xb = sb(s, "xb", [P, DIM], F32)
        sq = sb(s, "sq", [P, DIM], F32)
        hstat = sb(s, "hstat", [P, 4, HEADS], F32)
        y = [sb(s, f"y{i}", [P, DIM], F32) for i in (0, 1)]
        squares = [sb(s, f"squares{i}", [P, 2 * UNIT_TILES], F32) for i in (0, 1)]
        neg_now = [sb(s, f"neg_now{i}", [P, HEADS * tiles], F32) for i in (0, 1)]
        acc = [ps(s, f"acc{i}", [P, 512], F32) for i in range(6)]
        a_ps = [ps(s, f"a_ps{i}", [P, 8, P], F16) for i in (0, 1)]

        edge_loaded = [sem(s, f"edge_loaded{i}") for i in (0, 1)]
        own_loaded = [sem(s, f"own_loaded{i}") for i in (0, 1)]
        s_loaded = [sem(s, f"s_loaded{h}") for h in range(HEADS)]
        uv_loaded, passed = sem(s, "uv_loaded"), sem(s, "passed")
        y_stored = [sem(s, f"y_stored{i}") for i in (0, 1)]
        cast_done, a_turned, at_done = sem(s, "cast_done"), sem(s, "a_turned"), sem(s, "at_done")
        masks_done, tile_done = sem(s, "masks_done"), sem(s, "tile_done")
        late_copied, seg_done = sem(s, "late_copied"), sem(s, "seg_done")
        fin_step, lone_done, base_done = sem(s, "fin_step"), sem(s, "lone_done"), sem(s, "base_done")
        folded, centred, squared = sem(s, "folded"), sem(s, "centred"), sem(s, "squared")
        var_done, dev_done, scaled = sem(s, "var_done"), sem(s, "dev_done"), sem(s, "scaled")
        pool_step, y_done, unit_ready = sem(s, "pool_step"), sem(s, "y_done"), sem(s, "unit_ready")

        def by_head(t):
            return t[:].rearrange("p (h e) -> p h e", h=HEADS)

        def over_head(t):
            return t.unsqueeze(2).to_broadcast([P, HEADS, HEAD_DIM])

        with nc.Block() as block:

            @block.gpsimd
            def _(pool):
                for one in (cast_done, a_turned, at_done, masks_done, tile_done, late_copied, seg_done,
                            lone_done, base_done, folded, centred, squared, var_done, dev_done,
                            scaled, y_done, unit_ready):
                    pool.sem_inc(one, START)
                for one in (*edge_loaded, *own_loaded, *s_loaded, uv_loaded, *y_stored):
                    pool.sem_inc(one, 16 * START)
                with pool.Fori(0, units) as k:
                    for it in range(UNIT_TILES):
                        n = UNIT_TILES * k + it
                        slot = it % 2
                        pool.wait_ge(lone_done, done(n))
                        pool.wait_ge(y_done, freed(n, 1))
                        pool.wait_ge(own_loaded[slot], 16 * (3 * (2 * k + it // 2 + 1) + START))
                        nc.gpsimd.tensor_tensor(by_head(base), by_head(hmean_b[slot]), over_head(lone[:]),
                                                ALU.mult)
                        nc.gpsimd.tensor_tensor(xb[:], x_own[slot][:], beta_b[:], ALU.add
                                                ).then_inc(pool_step, 1)
                        pool.wait_ge(pool_step, 2 * n + 1)
                        nc.gpsimd.tensor_tensor(base[:], base[:], bias_b[:], ALU.add).then_inc(base_done, 1)
                        pool.wait_ge(scaled, done(n))
                        nc.gpsimd.tensor_tensor(y[slot][:], y[slot][:], gamma_b[:], ALU.mult
                                                ).then_inc(pool_step, 1)
                        pool.wait_ge(pool_step, 2 * n + 2)
                        nc.gpsimd.tensor_tensor(y[slot][:], y[slot][:], xb[:], ALU.add).then_inc(y_done, 1)

            @block.sync
            def _(sp):
                def load_edges(m, slot):
                    sp.dma_start(edge[slot][:], adj_rows[bass.ds(m % all_tiles * P, P), :]
                                 ).then_inc(edge_loaded[slot], 16)

                def load_scores(k, h):
                    row = SRC + h * TYPES
                    cols = bass.ds(k % units * UNIT, UNIT)
                    sp.dma_start(s_row[:, h, :], scoreT_dram[row:row + 1, cols].to_broadcast([P, UNIT])
                                 ).then_inc(s_loaded[h], 16)

                def load_uv(g):
                    q, first = g // batch_units % 2, g % batch_units * UNIT_TILES
                    rows = uv_dram[bass.ds(g % units * UNIT, UNIT), :]
                    to = uv[:, bass.ds(q * tiles + first, UNIT_TILES), :, :]
                    sp.dma_start(to.rearrange("p t h c -> p t (h c)"),
                                 rows.rearrange("(t p) c -> p t c", p=P)).then_inc(uv_loaded, 16)

                def unit(k, first):
                    sp.wait_ge(tile_done, done(k // batch_units * tiles - 1))
                    sp.wait_ge(uv_loaded, 16 * (k + batch_units + START))
                    load_uv(k + batch_units)
                    for it in range(UNIT_TILES):
                        n = UNIT_TILES * k + it
                        slot = it % 2
                        sp.wait_ge(masks_done, done(n))
                        load_scores(k + 1, it)
                        sp.wait_ge(cast_done, done(n + 7))
                        load_edges(n + 9, (it + 1) % 2)
                        if not first or it >= 2:
                            store(n - 2, slot)
                        rows = bass.ds(n * P, P)
                        b = k // batch_units
                        for to, row in ((h_own, h_dram[rows, :]), (x_own, x_rows[rows, :]),
                                        (hmean_b, hmean_dram[bass.ds(b, 1), :].to_broadcast([P, DIM]))):
                            sp.dma_start(to[slot][:], row).then_inc(own_loaded[slot], 16)

                def store(n, slot):
                    sp.wait_ge(y_done, done(n))
                    sp.dma_start(out_rows[bass.ds(n * P, P), :], y[slot][:]).then_inc(y_stored[slot], 16)

                for h in range(HEADS):
                    load_scores(0, h)
                for m in range(2 * UNIT_TILES + 1):
                    if m >= 2:
                        sp.wait_ge(cast_done, done(m - 2))
                    load_edges(m, m % 2)
                    if m < batch_units:
                        load_uv(m)
                unit(0, True)
                with sp.Fori(1, units) as k:
                    unit(k, False)
                for n in (last_tile - 1, last_tile):
                    store(n, n % 2)
                for i in (0, 1):
                    sp.wait_ge(y_stored[i], 16 * (START + all_tiles // 2))

            @block.scalar
            def _(act):
                def cast(m, slot):
                    act.wait_ge(edge_loaded[slot], 16 * done(m // 2))
                    act.wait_ge(a_turned, freed(2 * m + 1, 4))
                    nc.scalar.activation(a_row[slot][:].rearrange("p t c -> p (t c)"), edge[slot][:],
                                         ACT.Copy, accum_out=sum_a[:, bass.ds(m, 1)]
                                         ).then_inc(cast_done, 1)

                def take_at(m, parity, it):
                    for half in range(tiles // 8):
                        wait_apart(act, a_turned, done(2 * m + half), passed)
                        nc.scalar.activation(
                            at[parity][:, 8 * half:8 * half + 8, it * P:(it + 1) * P], a_ps[half][:],
                            ACT.Square, accum_out=squares[parity][:, 2 * it + half:2 * it + half + 1],
                            saturate=False
                        ).then_inc(at_done, 1)

                def head_variance(n):
                    act.wait_ge(centred, done(n))
                    nc.scalar.activation(sq[:], o[:], ACT.Square).then_inc(squared, 1)
                    act.wait_ge(var_done, done(n))
                    nc.scalar.activation(hstat[:, 2, :], hstat[:, 1, :], ACT.Sqrt, bias=eps[:, 1:2],
                                         scale=1.0 / HEAD_DIM).then_inc(dev_done, 1)

                def copy_seg(n, it):
                    act.wait_ge(tile_done, done(n))
                    act.wait_ge(folded, freed(n, 1))
                    for h in (2, 3, 0, 1):
                        bank = acc[it % 2 * 2 + h if h < 2 else 2 + h]
                        nc.scalar.activation(seg[:, h, 0:2 * AUG], bank[:, 0:2 * AUG], ACT.Copy,
                                             scale=rho[:, bass.ds(n, 1), h])
                        last = nc.scalar.activation(seg[:, h, 2 * AUG:6 * AUG], bank[:, 2 * AUG:6 * AUG],
                                                    ACT.Copy)
                        if h == 3:
                            last.then_inc(late_copied, 1)
                    last.then_inc(seg_done, 1)

                def unit(k, parity, first):
                    for it in range(UNIT_TILES):
                        n = UNIT_TILES * k + it
                        cast(n + 2 * UNIT_TILES, it % 2)
                        if not first or it >= 1:
                            head_variance(n - 1)
                        copy_seg(n, it)
                        take_at(n + 2 * UNIT_TILES, parity, it)

                for m in range(2 * UNIT_TILES):
                    cast(m, m % 2)
                    take_at(m, m // UNIT_TILES, m % UNIT_TILES)
                unit(0, 0, True)
                unit(1, 1, False)
                with act.Fori(1, units // 2) as i:
                    for parity in (0, 1):
                        unit(2 * i + parity, parity, False)
                head_variance(last_tile)

            @block.tensor
            def _(pe):
                def turn(m, slot):
                    pe.wait_ge(cast_done, done(m))
                    for half in range(tiles // 8):
                        pe.wait_ge(at_done, freed(2 * m + half, 2))
                        for j in range(8):
                            last = nc.tensor.transpose(a_ps[half][:, j, :], a_row[slot][:, 8 * half + j, :],
                                                       ident16[:])
                        last.then_inc(a_turned, 1)

                def multiply(n, parity, it, q):
                    for j in range(tiles):
                        for h in range(HEADS):
                            if j == 0 and h == 0:
                                wait_apart(pe, seg_done, freed(n, 2), passed)
                            if j == 0 and h == 2:
                                wait_apart(pe, late_copied, freed(n, 1), passed)
                            bank = acc[it % 2 * 2 + h if h < 2 else 2 + h]
                            own = slice(it * P, (it + 1) * P)
                            nc.tensor.matmul(bank[:, 4 * AUG:6 * AUG], at[parity][:, j, own],
                                             uv[:, q * tiles + j, h, 2 * AUG:4 * AUG], start=j == 0,
                                             stop=j == tiles - 1, skip_group_check=True)
                            last = nc.tensor.matmul(bank[:, 0:4 * AUG], mask[parity][:, h, j, own],
                                                    uv[:, q * tiles + j, h, :], start=False,
                                                    stop=j == tiles - 1, skip_group_check=True)
                    last.then_inc(tile_done, 1)

                for m in range(2 * UNIT_TILES):
                    turn(m, m % 2)
                with pe.Fori(0, batches // 2) as i:
                    for q in (0, 1):
                        wait_apart(pe, uv_loaded, 16 * (batch_units * (2 * i + q + 1) + START), passed)
                        with pe.Fori(0, batch_units // 2) as u:
                            for parity in (0, 1):
                                k = batch_units * (2 * i + q) + 2 * u + parity
                                pe.wait_ge(masks_done, done(HEADS * k + HEADS - 1))
                                for it in range(UNIT_TILES):
                                    n = UNIT_TILES * k + it
                                    multiply(n, parity, it, q)
                                    turn(n + 2 * UNIT_TILES, it % 2)

            @block.vector
            def _(dve):
                def finish_steps(n, slot):
                    STEPS = 9

                    def own(done_steps):
                        dve.wait_ge(fin_step, STEPS * n + done_steps)

                    def fold_u():
                        dve.wait_ge(seg_done, done(n))
                        nc.vector.tensor_tensor(two[:], seg[:, :, 0:2 * AUG], seg[:, :, 2 * AUG:4 * AUG],
                                                ALU.subtract).then_inc(fin_step, 1)

                    def fold_v():
                        own(1)
                        nc.vector.tensor_tensor(two[:], two[:], seg[:, :, 4 * AUG:6 * AUG], ALU.add
                                                ).then_inc(folded, 1)

                    def fold_parts():
                        dve.wait_ge(folded, done(n))
                        nc.vector.tensor_tensor(num[:], two[:, :, 0:AUG], two[:, :, AUG:2 * AUG], ALU.add
                                                ).then_inc(fin_step, 1)

                    def find_lone():
                        own(2)
                        dve.wait_ge(base_done, freed(n, 1))
                        nc.vector.tensor_scalar(lone[:], num[:, :, HEAD_DIM], 0.0, None, ALU.is_equal
                                                ).then_inc(lone_done, 1)

                    def denominator():
                        dve.wait_ge(lone_done, done(n))
                        nc.vector.tensor_tensor(rden[:], num[:, :, HEAD_DIM], lone[:], ALU.add
                                                ).then_inc(fin_step, 1)

                    def invert():
                        own(3)
                        nc.vector.reciprocal(rden[:], rden[:]).then_inc(fin_step, 1)

                    def divide():
                        own(4)
                        nc.vector.tensor_tensor(by_head(o), num[:, :, 0:HEAD_DIM], over_head(rden[:]),
                                                ALU.mult).then_inc(fin_step, 1)

                    def add_base():
                        own(5)
                        dve.wait_ge(base_done, done(n))
                        nc.vector.tensor_tensor(o[:], o[:], base[:], ALU.add).then_inc(fin_step, 1)

                    def relu_add_h():
                        own(6)
                        dve.wait_ge(own_loaded[slot], 16 * (3 * (n // 2 + 1) + START))
                        nc.vector.scalar_tensor_tensor(out=o[:], in0=o[:], scalar=0.0, in1=h_own[slot][:],
                                                       op0=ALU.max, op1=ALU.add).then_inc(fin_step, 1)

                    def head_sum():
                        own(7)
                        nc.vector.tensor_reduce(hstat[:, 0, :], by_head(o), axis=AX.X, op=ALU.add
                                                ).then_inc(fin_step, 1)

                    def centre():
                        own(8)
                        nc.vector.scalar_tensor_tensor(out=by_head(o), in0=over_head(hstat[:, 0, :]),
                                                       scalar=1.0 / HEAD_DIM, in1=by_head(o),
                                                       op0=ALU.mult, op1=ALU.subtract).then_inc(centred, 1)

                    def variance():
                        dve.wait_ge(squared, done(n))
                        nc.vector.tensor_reduce(hstat[:, 1, :], by_head(sq), axis=AX.X, op=ALU.add
                                                ).then_inc(var_done, 1)

                    def invert_deviation():
                        dve.wait_ge(dev_done, done(n))
                        nc.vector.reciprocal(hstat[:, 3, :], hstat[:, 2, :]).then_inc(fin_step, 1)

                    def scale():
                        own(9)
                        dve.wait_ge(y_stored[slot], 16 * (n // 2 + START))
                        nc.vector.scalar_tensor_tensor(out=by_head(y[slot]), in0=by_head(o), scalar=-1.0,
                                                       in1=over_head(hstat[:, 3, :]), op0=ALU.mult,
                                                       op1=ALU.mult).then_inc(scaled, 1)

                    return [fold_u, fold_v, fold_parts, find_lone, denominator, invert, divide, None,
                            add_base, relu_add_h, head_sum, centre, None, variance, invert_deviation,
                            scale]

                def unit(k, parity, first_finish):
                    dve.wait_ge(tile_done, freed(UNIT_TILES * k - 1, UNIT_TILES))
                    dve.wait_ge(at_done, done(2 * (UNIT_TILES * k + UNIT_TILES - 1) + 1))
                    nc.vector.tensor_tensor(sum_aa[:], sum_aa[:], squares[parity][:], ALU.add)
                    nc.vector.tensor_copy(
                        neg_now[parity][:],
                        neg_d[:, bass.ds(k // batch_units * (HEADS * tiles), HEADS * tiles)]
                    ).then_inc(unit_ready, 1)
                    dve.wait_ge(unit_ready, done(k))
                    for h in range(HEADS):
                        wait_apart(dve, s_loaded[h], 16 * done(k), passed)
                        steps = [None] * tiles
                        if h >= first_finish:
                            n = UNIT_TILES * (k - 1) + h - 1
                            steps = finish_steps(n, (h + 1) % 2)
                        for j in range(tiles):
                            last = nc.vector.scalar_tensor_tensor(
                                out=mask[parity][:, h, j, :], in0=s_row[:, h, :],
                                scalar=neg_now[parity][:, h * tiles + j:h * tiles + j + 1],
                                in1=at[parity][:, j, :], op0=ALU.is_gt, op1=ALU.mult, saturate=False)
                            if j == tiles - 1:
                                last.then_inc(masks_done, 1)
                            if steps[j] is not None:
                                steps[j]()

                unit(0, 0, HEADS)
                unit(1, 1, 1)
                with dve.Fori(1, units // 2) as i:
                    for parity in (0, 1):
                        unit(2 * i + parity, parity, 0)
                for n in range(last_tile - UNIT_TILES, last_tile + 1):
                    for step in finish_steps(n, n % 2):
                        if step is not None:
                            step()


def verdict_block(nc, sb, ps, sem, all_tiles, extremes, sum_a, sum_aa, verdict):
    with ExitStack() as s:
        sums = sb(s, "sums", [P, 2], F32)
        total = sb(s, "total", [P, 2], F32)
        most = sb(s, "most", [P, 3, HEADS], F32)
        good = sb(s, "good", [P, 5, HEADS], F32)
        all_good = sb(s, "all_good", [P, 1], F32)
        summed, reduced, step = sem(s, "summed"), sem(s, "reduced"), sem(s, "verdict_step")
        with nc.Block() as block:

            @block.vector
            def _(dve):
                nc.vector.tensor_reduce(sums[:, 0:1], sum_a[:, 0:all_tiles], axis=AX.X, op=ALU.add)
                nc.vector.tensor_reduce(sums[:, 1:2], sum_aa[:], axis=AX.X, op=ALU.add).then_inc(summed, 1)
                dve.wait_ge(reduced, 1)
                for n, bound, op in ((0, MAX_H, ALU.is_le), (1, MAX_DST, ALU.is_le),
                                     (2, MAX_SRC, ALU.is_le)):
                    nc.vector.tensor_scalar(good[:, n, :], most[:, n, :], bound, None, op)
                nc.vector.tensor_scalar(good[:, 3, :], most[:, 0, :], MIN_H, None, ALU.is_ge)
                nc.vector.tensor_tensor(good[:, 4, :], total[:, 0:1].to_broadcast([P, HEADS]),
                                        total[:, 1:2].to_broadcast([P, HEADS]), ALU.is_equal
                                        ).then_inc(step, 1)
                dve.wait_ge(step, 1)
                nc.vector.tensor_reduce(all_good[:], good[:], axis=AX.XY, op=ALU.min).then_inc(step, 1)
                dve.wait_ge(step, 2)
                nc.vector.tensor_scalar(verdict[:], all_good[:], 0.0, None, ALU.is_equal)

            @block.gpsimd
            def _(pool):
                pool.wait_ge(summed, 1)
                nc.gpsimd.partition_all_reduce(most[:].rearrange("p a h -> p (a h)"),
                                               extremes[:].rearrange("p a h -> p (a h)"), P,
                                               bass.bass_isa.ReduceOp.max)
                nc.gpsimd.partition_all_reduce(total[:], sums[:], P, bass.bass_isa.ReduceOp.add
                                               ).then_inc(reduced, 1)


def general_block(nc, sb, ps, sem, batches, tiles, all_tiles, x_rows, adj_rows, out_rows, h_dram,
                  score_dram, scoreT_dram, ident32, bias_b, gamma_b, beta_b, eps, verdict):
    span = tiles * P
    with ExitStack() as s:
        edge = sb(s, "g_edge", [P, span], I32)
        target = sb(s, "g_target", [P, TYPES, span], F32)
        match = sb(s, "g_match", [P, span], F32)
        weight = sb(s, "g_weight", [P, span], F32)
        probs_t = sb(s, "g_probs_t", [P, tiles, P], F32)
        h_head = sb(s, "g_h_head", [P, tiles, HEAD_DIM], F32)
        source = sb(s, "g_source", [P, PROJ], F32)
        h_own = sb(s, "g_h_own", [P, DIM], F32)
        x_own = sb(s, "g_x_own", [P, DIM], F32)
        neg_max = sb(s, "g_neg_max", [P, 1], F32)
        row_sum = sb(s, "g_row_sum", [P, 1], F32)
        inv_sum = sb(s, "g_inv_sum", [P, 1], F32)
        o = sb(s, "g_o", [P, DIM], F32)
        sq = sb(s, "g_sq", [P, DIM], F32)
        hstat = sb(s, "g_hstat", [P, 4, HEADS], F32)
        t_ps = ps(s, "g_t_ps", [P, tiles, P], F32)
        o_ps = ps(s, "g_o_ps", [P, 512], F32)
        own_loaded, head_loaded = sem(s, "g_own_loaded"), sem(s, "g_head_loaded")
        weight_done, probs_done = sem(s, "g_weight_done"), sem(s, "g_probs_done")
        turned, turned_copied, product_done = (sem(s, "g_turned"), sem(s, "g_turned_copied"),
                                               sem(s, "g_product_done"))
        head_done, var_done, dev_done = sem(s, "g_head_done"), sem(s, "g_var_done"), sem(s, "g_dev_done")
        y_done, y_stored, chain = sem(s, "g_y_done"), sem(s, "g_y_stored"), sem(s, "g_chain")
        OWN, HEAD = 4, 2

        def by_head(t):
            return t[:].rearrange("p (h e) -> p h e", h=HEADS)

        def over_head(t):
            return t.unsqueeze(2).to_broadcast([P, HEADS, HEAD_DIM])

        with nc.Block() as block:

            @block.sync
            def _(sp):
                wrong = sp.value_load(verdict[0:1, 0:1], min_val=0, max_val=1)
                with sp.If(wrong > 0):
                    for one in (head_done, product_done):
                        sp.sem_inc(one, 1)
                    sp.sem_inc(y_stored, 16)
                    with sp.Fori(0, all_tiles) as n:
                        rows = bass.ds(n * P, P)
                        b = n // tiles
                        sp.wait_ge(y_stored, 16 * n + 16)
                        for to, row in ((edge, adj_rows), (source, score_dram), (h_own, h_dram),
                                        (x_own, x_rows)):
                            sp.dma_start(to[:], row[rows, :]).then_inc(own_loaded, 16)
                        for h in range(HEADS):
                            sp.wait_ge(head_done, HEADS * n + h + 1)
                            first = DST + h * TYPES
                            sp.dma_start(target[:], scoreT_dram[first:first + TYPES,
                                                                bass.ds(b * span, span)]
                                         .rearrange("(o t) n -> o t n", o=1)
                                         .to_broadcast([P, TYPES, span])).then_inc(head_loaded, 16)
                            sp.dma_start(h_head[:],
                                         h_dram[bass.ds(b * span, span), h * HEAD_DIM:(h + 1) * HEAD_DIM]
                                         .rearrange("(t p) e -> p t e", p=P)).then_inc(head_loaded, 16)
                        sp.wait_ge(y_done, n + 1)
                        sp.dma_start(out_rows[rows, :], o[:]).then_inc(y_stored, 16)
                    sp.wait_ge(y_stored, 16 * all_tiles + 16)
                sp.nop()

            @block.scalar
            def _(act):
                wrong = act.value_load(verdict[0:1, 0:1], min_val=0, max_val=1)
                with act.If(wrong > 0):
                    with act.Fori(0, all_tiles) as n:
                        for h in range(HEADS):
                            act.wait_ge(weight_done, HEADS * n + h + 1)
                            nc.scalar.activation(weight[:], weight[:], ACT.Exp, bias=neg_max[:],
                                                 accum_out=row_sum[:]).then_inc(probs_done, 1)
                            act.wait_ge(turned, HEADS * n + h + 1)
                            for quarter in range(tiles // 4):
                                cols = slice(4 * quarter, 4 * quarter + 4)
                                last = nc.scalar.activation(probs_t[:, cols, :], t_ps[:, cols, :], ACT.Copy)
                            last.then_inc(turned_copied, 1)
                        act.wait_ge(var_done, n + 1)
                        nc.scalar.activation(hstat[:, 2, :], hstat[:, 1, :], ACT.Sqrt, bias=eps[:, 1:2],
                                             scale=1.0 / HEAD_DIM).then_inc(dev_done, 1)
                act.nop()

            @block.tensor
            def _(pe):
                wrong = pe.value_load(verdict[0:1, 0:1], min_val=0, max_val=1)
                with pe.If(wrong > 0):
                    with pe.Fori(0, all_tiles) as n:
                        for h in range(HEADS):
                            pe.wait_ge(probs_done, HEADS * n + h + 1)
                            for j in range(tiles):
                                last = nc.tensor.transpose(t_ps[:, j, :], weight[:, j * P:(j + 1) * P],
                                                           ident32[:])
                            last.then_inc(turned, 1)
                            pe.wait_ge(turned_copied, HEADS * n + h + 1)
                            pe.wait_ge(head_loaded, 16 * HEAD * (HEADS * n + h + 1))
                            pe.wait_ge(head_done, HEADS * n + h + 1)
                            for j in range(tiles):
                                last = nc.tensor.matmul(o_ps[:, 0:HEAD_DIM], probs_t[:, j, :],
                                                        h_head[:, j, :], start=j == 0,
                                                        stop=j == tiles - 1)
                            last.then_inc(product_done, 1)
                pe.nop()

            @block.vector
            def _(dve):
                CHAIN = 3 * TYPES + 3
                TAIL = 9
                wrong = dve.value_load(verdict[0:1, 0:1], min_val=0, max_val=1)
                with dve.If(wrong > 0):
                    with dve.Fori(0, all_tiles) as n:
                        links = [0]

                        def link(instruction):
                            links[0] += 1
                            instruction.then_inc(chain, 1)
                            dve.wait_ge(chain, (HEADS * CHAIN + TAIL) * n + links[0])

                        dve.wait_ge(own_loaded, 16 * OWN * (n + 1))
                        for h in range(HEADS):
                            dve.wait_ge(head_loaded, 16 * HEAD * (HEADS * n + h + 1))
                            for t in range(TYPES):
                                link(nc.vector.tensor_scalar(match[:], edge[:], float(t + 1), None,
                                                             ALU.is_equal))
                                col = SRC + h * TYPES + t
                                to = weight if t == 0 else target[:, t, :]
                                link(nc.vector.scalar_tensor_tensor(
                                    out=to[:] if t == 0 else to, in0=target[:, t, :],
                                    scalar=source[:, col:col + 1], in1=match[:], op0=ALU.add, op1=ALU.mult))
                                if t:
                                    link(nc.vector.tensor_tensor(weight[:], weight[:], target[:, t, :],
                                                                 ALU.add))
                            link(nc.vector.scalar_tensor_tensor(out=weight[:], in0=weight[:], scalar=0.01,
                                                                in1=weight[:], op0=ALU.mult, op1=ALU.max))
                            link(nc.vector.tensor_scalar(match[:], edge[:], 0.0, None, ALU.is_equal))
                            link(nc.vector.scalar_tensor_tensor(out=weight[:], in0=match[:],
                                                                scalar=NO_EDGE, in1=weight[:],
                                                                op0=ALU.mult, op1=ALU.add))
                            nc.vector.tensor_reduce(neg_max[:], weight[:], axis=AX.X, op=ALU.max,
                                                    negate=True).then_inc(weight_done, 1)
                            dve.wait_ge(product_done, HEADS * n + h + 2)
                            link(nc.vector.reciprocal(inv_sum[:], row_sum[:]))
                            nc.vector.tensor_scalar(o[:, h * HEAD_DIM:(h + 1) * HEAD_DIM],
                                                    o_ps[:, 0:HEAD_DIM], inv_sum[:], None, ALU.mult
                                                    ).then_inc(head_done, 1)
                        dve.wait_ge(head_done, HEADS * (n + 1) + 1)
                        link(nc.vector.tensor_tensor(o[:], o[:], bias_b[:], ALU.add))
                        link(nc.vector.scalar_tensor_tensor(out=o[:], in0=o[:], scalar=0.0, in1=h_own[:],
                                                            op0=ALU.max, op1=ALU.add))
                        link(nc.vector.tensor_reduce(hstat[:, 0, :], by_head(o), axis=AX.X, op=ALU.add))
                        link(nc.vector.scalar_tensor_tensor(
                            out=by_head(o), in0=over_head(hstat[:, 0, :]), scalar=-1.0 / HEAD_DIM,
                            in1=by_head(o), op0=ALU.mult, op1=ALU.add))
                        link(nc.vector.tensor_tensor(sq[:], o[:], o[:], ALU.mult))
                        nc.vector.tensor_reduce(hstat[:, 1, :], by_head(sq), axis=AX.X, op=ALU.add
                                                ).then_inc(var_done, 1)
                        dve.wait_ge(dev_done, n + 1)
                        link(nc.vector.reciprocal(hstat[:, 3, :], hstat[:, 2, :]))
                        link(nc.vector.tensor_tensor(by_head(o), by_head(o), over_head(hstat[:, 3, :]),
                                                     ALU.mult))
                        link(nc.vector.tensor_tensor(o[:], o[:], gamma_b[:], ALU.mult))
                        link(nc.vector.tensor_tensor(o[:], o[:], beta_b[:], ALU.add))
                        nc.vector.tensor_tensor(o[:], o[:], x_own[:], ALU.add).then_inc(y_done, 1)
                        assert links[0] == HEADS * CHAIN + TAIL
                dve.nop()


_INS = ("x", "adj", "L0_gnn_W", "L0_gnn_a_src", "L0_gnn_a_dst", "L0_gnn_bias", "L0_gnn_ln_gamma",
        "L0_gnn_ln_beta")


def kernel(**inputs):
    import numpy as _np
    import concourse.bacc as _bacc
    from concourse import mybir as _mybir
    from concourse.bass_utils import run_bass_kernel_spmd as _run

    nc = _bacc.Bacc("TRN2", target_bir_lowering=False, num_devices=1, dynamic_dma_scratch_size=1024)
    arrays, args = {}, []
    for name in _INS:
        a = _np.ascontiguousarray(inputs[name])
        arrays[name + "_dram"] = a
        args.append(nc.dram_tensor(name + "_dram", a.shape, _mybir.dt.from_np(a.dtype),
                                   kind="ExternalInput").ap())
    shape = inputs["x"].shape
    args.append(nc.dram_tensor("out_dram", shape, _mybir.dt.float32, kind="ExternalOutput").ap())
    build(nc, *args)
    return _run(nc, [arrays], core_ids=[0]).results[0]["out_dram"]
```

```python
from contextlib import ExitStack

import concourse.bass as bass
from concourse import mybir

P = 128
HEADS, HEAD_DIM, TYPES = 4, 64, 5
DIM = HEADS * HEAD_DIM
KC = DIM // P
AUG = HEAD_DIM + 1
PROJ = 2 * HEADS * TYPES
SRC, DST = 0, HEADS * TYPES
GCOLS = HEADS * 4 * AUG
UNIT_TILES = 4
UNIT = UNIT_TILES * P
SCALE = 64.0
LN_EPS, HEAD_EPS = 1e-5, 1e-6
NO_EDGE = -1e9
MAX_DST, MAX_SRC, MAX_H, MIN_H = 4.0, 40.0, 16.0, 0.25

START = 24


def done(n):
    return n + START + 1


def freed(n, depth):
    return n + START + 1 - depth


def wait_apart(engine, semaphore, value, passed):
    engine.wait_ge(semaphore, value)
    engine.sem_inc(passed, 1)


F32, F16, BF16, I32 = mybir.dt.float32, mybir.dt.float16, mybir.dt.bfloat16, mybir.dt.int32
STEP = 1e30
ALU = mybir.AluOpType
ACT = mybir.ActivationFunctionType
AX = mybir.AxisListType


def build(nc, x, adj, W, a_src, a_dst, bias, gamma, beta, out):
    batches, nodes, _ = x.shape
    tiles = nodes // P
    all_tiles = batches * tiles
    units = all_tiles // UNIT_TILES
    batch_units = tiles // UNIT_TILES
    groups = tiles // 4

    x_rows = x.rearrange("b n d -> (b n) d")
    adj_rows = adj.rearrange("b n m -> (b n) m")
    out_rows = out.rearrange("b n d -> (b n) d")
    h_dram = nc.dram_tensor("h_rows", (batches * nodes, DIM), F32).ap()
    uv_dram = nc.dram_tensor("uv_rows", (batches * nodes, GCOLS), F16).ap()
    score_dram = nc.dram_tensor("score_rows", (batches * nodes, PROJ), F32).ap()
    scoreT_dram = nc.dram_tensor("score_cols", (PROJ, batches * nodes), F32).ap()
    hsum_dram = nc.dram_tensor("h_sum", (batches, 2 * HEADS * AUG), F16).ap()

    keep = ExitStack()
    with keep:
        def sb(stack, name, shape, dt):
            return stack.enter_context(nc.sbuf_tensor(name, shape, dt))

        def ps(stack, name, shape, dt):
            return stack.enter_context(nc.psum_tensor(name, shape, dt))

        def sem(stack, name):
            return stack.enter_context(nc.semaphore(name))

        ident16 = sb(keep, "ident16", [P, P], BF16)
        ident32 = sb(keep, "ident32", [P, P], F32)
        bias_b = sb(keep, "bias_b", [P, DIM], F32)
        gamma_b = sb(keep, "gamma_b", [P, DIM], F32)
        beta_b = sb(keep, "beta_b", [P, DIM], F32)
        rho = sb(keep, "rho", [P, all_tiles, HEADS], F32)
        neg_d = sb(keep, "neg_d", [P, batches * HEADS * tiles], F32)
        eps = sb(keep, "eps", [P, 2], F32)
        extremes = sb(keep, "extremes", [P, 3, HEADS], F32)
        degree = sb(keep, "degree", [P, all_tiles + 8], F32)
        sum_aa = sb(keep, "sum_aa", [P, 2 * UNIT_TILES], F32)
        verdict = sb(keep, "verdict", [P, 1], I32)

        edge = [sb(keep, f"edge{i}", [P, tiles * P], I32) for i in (0, 1)]
        a_row = [sb(keep, f"a_row{i}", [P, tiles, P], BF16) for i in (0, 1)]
        edge_loaded = [sem(keep, f"edge_loaded{i}") for i in (0, 1)]
        cast_done, a_turned = sem(keep, "cast_done"), sem(keep, "a_turned")
        uv0 = sb(keep, "uv0", [P, tiles, HEADS, 4 * AUG], F16)
        casts = (edge, a_row, edge_loaded, cast_done, a_turned)
        with ExitStack() as early:
            wx = sb(early, "wx", [P, KC, DIM + PROJ], F32)
            xt = [sb(early, f"xt{q}", [P, tiles, DIM], F32) for q in (0, 1)]
            x_loaded = [sem(early, f"x_loaded{q}") for q in (0, 1)]
            setup_block(nc, sb, ps, sem, W, a_src, a_dst, bias, gamma, beta, wx, ident16, ident32,
                        bias_b, gamma_b, beta_b, eps, extremes, sum_aa, x_rows, xt, x_loaded)
            rows_block(nc, sb, ps, sem, batches, tiles, groups, x_rows, adj_rows, wx, ident32, rho,
                       neg_d, eps, extremes, h_dram, uv_dram, score_dram, scoreT_dram, hsum_dram,
                       xt, x_loaded, degree, casts, uv0)
        edges_block(nc, sb, ps, sem, batches, tiles, units, batch_units, x_rows, adj_rows, out_rows,
                    h_dram, uv_dram, scoreT_dram, hsum_dram, ident16, bias_b, gamma_b, beta_b,
                    rho, neg_d, eps, degree, sum_aa, casts, uv0)
        verdict_block(nc, sb, ps, sem, all_tiles, extremes, degree, sum_aa, verdict)
        general_block(nc, sb, ps, sem, batches, tiles, all_tiles, x_rows, adj_rows, out_rows, h_dram,
                      score_dram, scoreT_dram, ident32, bias_b, gamma_b, beta_b, eps, verdict)


def setup_block(nc, sb, ps, sem, W, a_src, a_dst, bias, gamma, beta, wx, ident16, ident32,
                bias_b, gamma_b, beta_b, eps, extremes, sum_aa, x_rows, xt, x_loaded):
    tiles = xt[0].shape[1]
    with ExitStack() as s:
        a_t = sb(s, "a_t", [P, HEADS // 2, PROJ], F32)
        w_t = sb(s, "w_t", [P, HEADS // 2, KC, P], F32)
        w_ps = ps(s, "w_ps", [P, HEADS // 2, KC, P], F32)
        v_ps = ps(s, "v_ps", [P, KC, 256], F32)
        loaded, broadcast = sem(s, "loaded"), sem(s, "broadcast")
        a_loaded, a_clear = sem(s, "a_loaded"), sem(s, "a_clear")
        made, transposed, w_ready = sem(s, "made"), sem(s, "transposed"), sem(s, "w_ready")
        projected = sem(s, "projected")
        with nc.Block() as block:

            @block.sync
            def _(sp):
                for h in range(HEADS):
                    sp.dma_start(wx[:, :, h * HEAD_DIM:(h + 1) * HEAD_DIM],
                                 W[h].rearrange("(k p) e -> p k e", p=P)).then_inc(loaded, 16)
                sp.dma_start(xt[0][:], x_rows[x_rows.shape[0] - tiles * P:, :].rearrange("(t p) d -> p t d", p=P)
                             ).then_inc(x_loaded[0], 16)
                sp.wait_ge(a_clear, 1)
                for first, a in ((SRC, a_src), (DST, a_dst)):
                    for h in range(HEADS):
                        row, col = (h % 2) * HEAD_DIM, first + h * TYPES
                        with nc.allow_non_contiguous_dma(reason="1280 numbers, once"):
                            sp.dma_start(a_t[row:row + HEAD_DIM, h // 2, col:col + TYPES],
                                         a[h].rearrange("t e -> e t")).then_inc(a_loaded, 16)
                for row, to in ((bias, bias_b), (gamma, gamma_b), (beta, beta_b)):
                    flat = row.rearrange("h e -> (h e)").rearrange("(o n) -> o n", o=1)
                    sp.dma_start(to[:, :], flat.to_broadcast([P, DIM])).then_inc(broadcast, 16)
                sp.wait_ge(broadcast, 48)

            @block.gpsimd
            def _(pool):
                nc.gpsimd.memset(a_t[:], 0.0).then_inc(a_clear, 1)
                nc.gpsimd.memset(eps[:, 0:1], LN_EPS)
                nc.gpsimd.memset(eps[:, 1:2], HEAD_EPS)
                nc.gpsimd.memset(extremes[:], 0.0)
                nc.gpsimd.memset(sum_aa[:], 0.0)
                nc.gpsimd.memset(ident16[:], 0.0)
                nc.gpsimd.memset(ident32[:], 0.0).then_inc(made, 1)
                pool.wait_ge(made, 1)
                for ident in (ident16, ident32):
                    nc.gpsimd.affine_select(out=ident[:], in_=ident[:], compare_op=ALU.not_equal,
                                            fill=1.0, base=0, pattern=[[-1, P]],
                                            channel_multiplier=1).then_inc(made, 1)

            @block.tensor
            def _(pe):
                pe.wait_ge(loaded, 16 * HEADS)
                pe.wait_ge(made, 3)
                for pair in range(HEADS // 2):
                    for k in range(KC):
                        last = nc.tensor.transpose(w_ps[:, pair, k, :],
                                                   wx[:, k, pair * P:(pair + 1) * P], ident32[:])
                last.then_inc(transposed, 1)
                pe.wait_ge(w_ready, 1)
                pe.wait_ge(a_loaded, 16 * 2 * HEADS)
                for k in range(KC):
                    for pair in range(HEADS // 2):
                        last = nc.tensor.matmul(v_ps[:, k, 0:PROJ], w_t[:, pair, k, :],
                                                a_t[:, pair, :], start=pair == 0,
                                                stop=pair == HEADS // 2 - 1)
                last.then_inc(projected, 1)

            @block.vector
            def _(dve):
                dve.wait_ge(transposed, 1)
                nc.vector.tensor_copy(w_t[:], w_ps[:]).then_inc(w_ready, 1)
                dve.wait_ge(projected, 1)
                nc.vector.tensor_copy(wx[:, :, DIM:DIM + PROJ], v_ps[:, :, 0:PROJ])


def rows_block(nc, sb, ps, sem, batches, tiles, groups, x_rows, adj_rows, wx, ident32, rho, neg_d,
               eps, extremes, h_dram, uv_dram, score_dram, scoreT_dram, hsum_dram, xt, x_loaded,
               degree, casts, uv0):
    pairs = tiles // 2
    steps = batches // 2
    span = tiles * P
    COPY_LAG, ACROSS_LAG, EXP_LAG, HI_LAG = 4, 7, 9, 12
    PRODUCT_LAG, SCORE_LAG, SUM_LAG, UV_LAG = 1, 2, 3, 5
    edge, a_row, edge_loaded, cast_done, a_turned = casts
    with ExitStack() as s:
        haug = [sb(s, f"haug{q}", [P, tiles, HEADS, AUG], F32) for q in (0, 1)]
        score = [sb(s, f"score{q}", [P, tiles, PROJ], F32) for q in (0, 1)]
        scoreT = [sb(s, f"scoreT{q}", [PROJ, span], F32) for q in (0, 1)]
        stats = sb(s, "stats", [P, tiles, 6], F32)
        mean_var = sb(s, "mean_var", [P, tiles, 2], F32)
        deviation = sb(s, "deviation", [P, tiles], F32)
        rstd = [sb(s, f"rstd{q}", [P, tiles], F32) for q in (0, 1)]
        shift = [sb(s, f"shift{q}", [P, tiles], F32) for q in (0, 1)]
        normed = [sb(s, f"normed{i}", [P, DIM], F32) for i in range(4)]
        normed_t = [sb(s, f"normed_t{i}", [P, KC, 4 * P], F32) for i in (0, 1)]
        u_exp = sb(s, "u_exp", [P, tiles, HEADS], F32)
        v_exp = sb(s, "v_exp", [P, tiles, HEADS], F32)
        whole = [sb(s, f"whole{i}", [P, HEADS, 2 * AUG], F32) for i in range(4)]
        ones = sb(s, "ones", [P, 1], F32)
        hsum = sb(s, "hsum", [1, 2, HEADS * AUG], F16)
        tile_sum = [sb(s, f"tile_sum{q}", [P, HEADS * AUG], F32) for q in (0, 1)]
        batch_max = sb(s, "batch_max", [P, 3, HEADS], F32)
        pair_max = sb(s, "pair_max", [P, pairs, HEADS], F32)
        t_ps = [ps(s, f"t_ps{i}", [P, KC, 2 * P], F32) for i in (0, 1)]
        h_ps = [ps(s, f"h_ps{i}", [P, 512], F32) for i in range(4)]
        sT_ps = ps(s, "sT_ps", [P, 4 * P], F32)
        sum_ps = ps(s, "sum_ps", [P, 512], F32)

        ones_made = sem(s, "ones_made")
        stats_done, mv_done, dev_done = sem(s, "stats_done"), sem(s, "mv_done"), sem(s, "dev_done")
        rstd_done, shift_done = sem(s, "rstd_done"), sem(s, "shift_done")
        normed_done, transposed = sem(s, "normed_done"), sem(s, "transposed")
        t_copied, h_made, h_copied = sem(s, "t_copied"), sem(s, "h_made"), sem(s, "h_copied")
        e_copied, sT_made, sT_copied = sem(s, "e_copied"), sem(s, "sT_made"), sem(s, "sT_copied")
        tiles_added, sum_made, sum_copied = (sem(s, "tiles_added"), sem(s, "sum_made"),
                                             sem(s, "sum_copied"))
        exps_done, whole_done = sem(s, "exps_done"), sem(s, "whole_done")
        hi_done, lo_done, max_done = sem(s, "hi_done"), sem(s, "lo_done"), sem(s, "max_done")
        pair_max_done = sem(s, "pair_max_done")
        rows_stored = [sem(s, f"rows_stored{q}") for q in (0, 1)]
        uv_stored = [sem(s, f"uv_stored{g}") for g in range(groups)]
        sum_stored, passed = sem(s, "sum_stored"), sem(s, "passed")
        STORES = HEADS + 2

        parts = [uv0[:, 4 * g:4 * g + 4, :, :].rearrange("p t h (l e) -> p t h l e", l=2)
                 for g in range(groups)]

        def at(b):
            return batches - 1 - b

        def lagging(b, q, slot, lag, slots):
            if slot >= lag:
                return None if isinstance(b, int) and b == batches else (b, q, slot - lag)
            return None if isinstance(b, int) and b == 0 else (b - 1, 1 - q, slot - lag + slots)

        def all_batches(engine, slots_of_batch):
            for q in (0, 1):
                slots_of_batch(q, q)
            if steps > 2:
                with engine.Fori(1, steps - 1) as i:
                    for q in (0, 1):
                        slots_of_batch(2 * i + q, q)
            if steps > 1:
                for q in (0, 1):
                    slots_of_batch(batches - 2 + q, q)
            slots_of_batch(batches, 0)

        def is_at(b, last):
            return isinstance(b, int) and b == last

        with nc.Block() as block:

            @block.gpsimd
            def _(pool):
                for one in (stats_done, mv_done, dev_done, rstd_done, shift_done, normed_done,
                            transposed, t_copied, h_made, h_copied, e_copied, sT_made, sT_copied,
                            tiles_added, sum_made, sum_copied, exps_done, whole_done, hi_done, lo_done, max_done,
                            pair_max_done, cast_done, a_turned):
                    pool.sem_inc(one, START)
                for one in (*x_loaded, *rows_stored, *uv_stored, sum_stored, *edge_loaded):
                    pool.sem_inc(one, 16 * START)
                nc.gpsimd.memset(ones[:], 1.0)
                for q in (0, 1):
                    last = nc.gpsimd.memset(haug[q][:, :, :, HEAD_DIM:AUG], 1.0)
                last.then_inc(ones_made, 1)

                def split_lo(b, q, t):
                    pool.wait_ge(hi_done, done(tiles * b + t))
                    nc.gpsimd.tensor_tensor(parts[t // 4][:, t % 4, :, 1, :], whole[t % 4][:],
                                            parts[t // 4][:, t % 4, :, 0, :],
                                            ALU.subtract).then_inc(lo_done, 1)

                def add_tile(b, q, t):
                    rows = haug[q][:].rearrange("p t h e -> p t (h e)")
                    pool.wait_ge(h_copied, done(tiles * b + t))
                    if t == 0:
                        return
                    if t == 1:
                        pool.wait_ge(sum_made, freed(b, 2))
                    else:
                        pool.wait_ge(tiles_added, done((tiles - 1) * b + t - 2))
                    nc.gpsimd.tensor_tensor(tile_sum[q][:], rows[:, 0, :] if t == 1 else tile_sum[q][:],
                                            rows[:, t, :], ALU.add).then_inc(tiles_added, 1)

                def slots(b, q):
                    for t in range(tiles):
                        at_sum = lagging(b, q, t, COPY_LAG, tiles)
                        if at_sum:
                            add_tile(*at_sum)
                        at_lo = lagging(b, q, t, HI_LAG, tiles)
                        if at_lo:
                            split_lo(*at_lo)

                all_batches(pool, slots)

            @block.sync
            def _(sp):
                def load(b, q):
                    rows = x_rows[bass.ds(at(b) * span, span), :].rearrange("(t p) d -> p t d", p=P)
                    sp.dma_start(xt[q][:], rows).then_inc(x_loaded[q], 16)

                def store_uv(b, g):
                    if is_at(b, batches - 1):
                        return
                    wait_apart(sp, lo_done, done(tiles * b + 4 * g + 3), passed)
                    four = uv_dram[bass.ds(at(b) * span + g * 4 * P, 4 * P), :]
                    sp.dma_start(four.rearrange("(t p) c -> p t c", p=P),
                                 uv0[:, 4 * g:4 * g + 4, :, :].rearrange("p t h c -> p t (h c)")
                                 ).then_inc(uv_stored[g], 16)

                def store_rows(b, q):
                    rows = bass.ds(at(b) * span, span)
                    wait_apart(sp, h_copied, done(tiles * b + tiles - 1), passed)
                    for h in range(HEADS):
                        cols = slice(h * HEAD_DIM, (h + 1) * HEAD_DIM)
                        sp.dma_start(h_dram[rows, cols].rearrange("(t p) e -> p t e", p=P),
                                     haug[q][:, :, h, 0:HEAD_DIM]).then_inc(rows_stored[q], 16)
                    wait_apart(sp, e_copied, done(tiles * b + tiles - 1), passed)
                    sp.dma_start(score_dram[rows, :].rearrange("(t p) c -> p t c", p=P),
                                 score[q][:]).then_inc(rows_stored[q], 16)
                    wait_apart(sp, sT_copied, done(groups * b + groups - 1), passed)
                    sp.dma_start(scoreT_dram[:, rows], scoreT[q][:]).then_inc(rows_stored[q], 16)

                def store_sum(b):
                    wait_apart(sp, sum_copied, done(b), passed)
                    sp.dma_start(hsum_dram[bass.ds(at(b), 1), :], hsum[:].rearrange("o l c -> o (l c)")
                                 ).then_inc(sum_stored, 16)

                def slots(b, q):
                    if not (is_at(b, batches - 1) or is_at(b, batches)):
                        wait_apart(sp, normed_done, done(tiles * b - 1), passed)
                        load(b + 1, 1 - q)
                    if is_at(b, batches):
                        for m in (0, 1):
                            load_edge_tile(sp, adj_rows, edge, edge_loaded, m, m)
                    if not is_at(b, 0):
                        store_uv(b - 1, 0)
                        store_rows(b - 1, 1 - q)
                        store_uv(b - 1, 1)
                        store_sum(b - 1)
                        for g in range(2, groups):
                            store_uv(b - 1, g)
                    if is_at(b, batches):
                        for m in (2, 3):
                            sp.wait_ge(cast_done, done(m - 2))
                            load_edge_tile(sp, adj_rows, edge, edge_loaded, m, m % 2)

                all_batches(sp, slots)
                for q in (0, 1):
                    sp.wait_ge(rows_stored[q], 16 * (START + STORES * steps))
                for g in range(groups):
                    sp.wait_ge(uv_stored[g], 16 * (START + batches - 1))
                sp.wait_ge(sum_stored, 16 * (START + batches))

            @block.scalar
            def _(act):
                def take_deviation(b):
                    act.wait_ge(mv_done, done(b))
                    act.wait_ge(rstd_done, freed(b, 1))
                    nc.scalar.activation(deviation[:], mean_var[:, :, 1], ACT.Sqrt,
                                         bias=eps[:, 0:1]).then_inc(dev_done, 1)

                def norm(b, q, t):
                    if t == 0:
                        act.wait_ge(shift_done, done(b))
                    act.wait_ge(transposed, freed(pairs * b + t // 2, 2))
                    nc.scalar.activation(normed[t % 4][:], xt[q][:, t, :], ACT.Relu,
                                         scale=rstd[q][:, t:t + 1], bias=shift[q][:, t:t + 1]
                                         ).then_inc(normed_done, 1)

                def copy_h(b, q, t):
                    if t == 0:
                        act.wait_ge(rows_stored[q], 16 * (b // 2 * STORES + START))
                        act.wait_ge(sum_made, freed(b, 2))
                    act.wait_ge(h_made, done(tiles * b + t))
                    nc.scalar.activation(
                        haug[q][:, t, :, 0:HEAD_DIM],
                        h_ps[t % 4][:, 0:DIM].rearrange("p (h e) -> p h e", h=HEADS),
                        ACT.Copy).then_inc(h_copied, 1)

                def copy_across(b, q, g):
                    if g == 0:
                        act.wait_ge(rows_stored[q], 16 * (b // 2 * STORES + START))
                    act.wait_ge(sT_made, done(groups * b + g))
                    nc.scalar.activation(scoreT[q][:, g * 4 * P:(g + 1) * 4 * P], sT_ps[0:PROJ, :],
                                         ACT.Copy).then_inc(sT_copied, 1)

                def exponentials(b, q, t):
                    act.wait_ge(e_copied, done(tiles * b + t + 3))
                    act.wait_ge(whole_done, freed(tiles * b + t + 3, tiles))
                    for first, scale, to in (
                            (DST, 1.0, u_exp[:, t:t + 4, :]), (DST, 0.01, v_exp[:, t:t + 4, :]),
                            (SRC, 0.99, rho[:, bass.ds(at(b) * tiles + t, 4), :])):
                        last = nc.scalar.activation(
                            to, score[q][:, t:t + 4, first:first + HEADS * TYPES:TYPES], ACT.Exp,
                            scale=scale)
                    last.then_inc(exps_done, 1)

                def split_hi(b, q, t):
                    if t % 4 == 0:
                        act.wait_ge(uv_stored[t // 4], 16 * (b + START))
                    act.wait_ge(whole_done, done(tiles * b + t))
                    nc.scalar.activation(parts[t // 4][:, t % 4, :, 0, :],
                                         whole[t % 4][:], ACT.Copy).then_inc(hi_done, 1)

                def slots(b, q):
                    for t in range(tiles):
                        if not is_at(b, batches):
                            norm(b, q, t)
                        at_h = lagging(b, q, t, COPY_LAG, tiles)
                        if at_h:
                            copy_h(*at_h)
                        at_across = lagging(b, q, t, ACROSS_LAG, tiles)
                        if at_across and at_across[2] % 4 == 0:
                            copy_across(at_across[0], at_across[1], at_across[2] // 4)
                        at_exp = lagging(b, q, t, EXP_LAG, tiles)
                        if at_exp and at_exp[2] % 4 == 0:
                            exponentials(*at_exp)
                        at_hi = lagging(b, q, t, HI_LAG, tiles)
                        if at_hi:
                            split_hi(*at_hi)
                        if t == tiles - 2 and not (is_at(b, batches - 1) or is_at(b, batches)):
                            take_deviation(b + 1)

                take_deviation(0)
                all_batches(act, slots)
                for m in (0, 1):
                    cast_edge_tile(nc, act, edge, a_row, edge_loaded, degree, cast_done, m, m)

            @block.tensor
            def _(pe):
                def transpose_pair(b, r):
                    pe.wait_ge(normed_done, done(tiles * b + 2 * r + 1))
                    pe.wait_ge(t_copied, freed(pairs * b + r, 2))
                    for t in (0, 1):
                        for k in range(KC):
                            last = nc.tensor.transpose(
                                t_ps[r % 2][:, k, t * P:(t + 1) * P],
                                normed[(2 * r + t) % 4][:, k * P:(k + 1) * P], ident32[:])
                    last.then_inc(transposed, 1)

                def product(b, t):
                    pe.wait_ge(t_copied, done(pairs * b + t // 2))
                    pe.wait_ge(e_copied, freed(tiles * b + t, 4))
                    for k in range(KC):
                        last = nc.tensor.matmul(
                            h_ps[t % 4][:, 0:DIM + PROJ],
                            normed_t[t // 4 % 2][:, k, t % 4 * P:(t % 4 + 1) * P],
                            wx[:, k, :], start=k == 0, stop=k == KC - 1)
                    last.then_inc(h_made, 1)

                def scores_across(b, g):
                    pe.wait_ge(sT_copied, freed(groups * b + g, 1))
                    for k in range(KC):
                        last = nc.tensor.matmul(sT_ps[0:PROJ, :], wx[:, k, DIM:DIM + PROJ],
                                                normed_t[g % 2][:, k, :], start=k == 0,
                                                stop=k == KC - 1)
                    last.then_inc(sT_made, 1)

                def add_rows(b, q):
                    pe.wait_ge(tiles_added, done((tiles - 1) * b + tiles - 2))
                    pe.wait_ge(sum_copied, freed(b, 1))
                    nc.tensor.matmul(sum_ps[0:1, 0:HEADS * AUG], ones[:], tile_sum[q][:], start=True,
                                     stop=True).then_inc(sum_made, 1)

                def slots(b, q):
                    for r in range(pairs):
                        if not is_at(b, batches):
                            transpose_pair(b, r)
                        at_h = lagging(b, q, r, PRODUCT_LAG, pairs)
                        if at_h:
                            for t in (2 * at_h[2], 2 * at_h[2] + 1):
                                product(at_h[0], t)
                            if at_h[2] % 2 == 1:
                                scores_across(at_h[0], at_h[2] // 2)
                        if r == SUM_LAG and not is_at(b, 0):
                            add_rows(b - 1, 1 - q)

                pe.wait_ge(ones_made, 1)
                all_batches(pe, slots)

            @block.vector
            def _(dve):
                def take_stats(b, q, t):
                    if t == 0:
                        dve.wait_ge(x_loaded[q], 16 * done(b // 2))
                    for one in range(t, t + 4):
                        last = nc.vector.bn_stats(stats[:, one, :], xt[q][:, one, :])
                    last.then_inc(stats_done, 1)

                def take_mean_var(b, t):
                    wait_apart(dve, stats_done, done(groups * b + t // 4), passed)
                    for one in range(t, t + 4):
                        last = nc.vector.bn_aggr(mean_var[:, one, :], stats[:, one, :])
                    if t == tiles - 4:
                        last.then_inc(mv_done, 1)

                def invert_deviation(b, q):
                    dve.wait_ge(dev_done, done(b))
                    dve.wait_ge(normed_done, freed(tiles * b, tiles + 1))
                    nc.vector.reciprocal(rstd[q][:], deviation[:]).then_inc(rstd_done, 1)

                def take_shift(b, q):
                    dve.wait_ge(rstd_done, done(b))
                    nc.vector.scalar_tensor_tensor(
                        out=shift[q][:], in0=mean_var[:, :, 0], scalar=-1.0, in1=rstd[q][:],
                        op0=ALU.mult, op1=ALU.mult).then_inc(shift_done, 1)

                def copy_transposed(b, r):
                    g = r // 2
                    dve.wait_ge(transposed, done(pairs * b + r))
                    dve.wait_ge(sT_made, freed(groups * b + g, 2))
                    nc.vector.tensor_copy(normed_t[g % 2][:, :, r % 2 * 2 * P:(r % 2 + 1) * 2 * P],
                                          t_ps[r % 2][:]).then_inc(t_copied, 1)

                def copy_score(b, q, t):
                    if t == 0:
                        dve.wait_ge(rows_stored[q], 16 * (b // 2 * STORES + START))
                    dve.wait_ge(h_copied, done(tiles * b + t))
                    nc.vector.tensor_copy(score[q][:, t, :], h_ps[t % 4][:, DIM:DIM + PROJ]
                                          ).then_inc(e_copied, 1)

                def make_uv(b, q, t):
                    if t % 4 == 0:
                        dve.wait_ge(exps_done, done(groups * b + t // 4))
                    dve.wait_ge(lo_done, freed(tiles * b + t, 4))
                    for n, factor in ((0, u_exp), (1, v_exp)):
                        last = nc.vector.scalar_tensor_tensor(
                            out=whole[t % 4][:, :, n * AUG:(n + 1) * AUG], in0=haug[q][:, t, :, :],
                            scalar=SCALE, in1=factor[:, t, :].unsqueeze(2).to_broadcast([P, HEADS, AUG]),
                            op0=ALU.mult, op1=ALU.mult)
                    last.then_inc(whole_done, 1)

                def take_pair_max(b, q, r):
                    dve.wait_ge(h_copied, done(tiles * b + 2 * r + 1))
                    if r == 0:
                        dve.wait_ge(max_done, done(3 * b - 3))
                    nc.vector.tensor_reduce(
                        pair_max[:, r, :],
                        haug[q][:, 2 * r:2 * r + 2, :, 0:HEAD_DIM].rearrange("p t h e -> p h t e"),
                        axis=AX.XY, op=ALU.max, apply_absolute_value=True).then_inc(pair_max_done, 1)

                def take_sum(b):
                    dve.wait_ge(sum_made, done(b))
                    dve.wait_ge(sum_stored, 16 * (b + START))
                    nc.vector.tensor_copy(hsum[:, 0, :], sum_ps[0:1, 0:HEADS * AUG]).then_inc(max_done, 1)

                def take_sum_lo(b):
                    dve.wait_ge(max_done, done(3 * b + 1))
                    nc.vector.tensor_tensor(hsum[:, 1, :], sum_ps[0:1, 0:HEADS * AUG], hsum[:, 0, :],
                                            ALU.subtract).then_inc(sum_copied, 1)

                def take_batch_max(b, q):
                    dve.wait_ge(e_copied, done(tiles * b + tiles - 1))
                    dve.wait_ge(max_done, done(3 * b - 1))
                    wait_apart(dve, pair_max_done, done(pairs * b + pairs - 1), passed)
                    nc.vector.tensor_scalar(
                        neg_d[:, bass.ds(at(b) * (HEADS * tiles), HEADS * tiles)].rearrange(
                            "p (h t) -> p h t", h=HEADS),
                        score[q][:, :, DST:DST + HEADS * TYPES:TYPES].rearrange("p t h -> p h t"),
                        -1.0, None, ALU.mult)
                    nc.vector.tensor_reduce(
                        batch_max[:, 0, :], pair_max[:].rearrange("p r h -> p h r"), axis=AX.X, op=ALU.max)
                    for n, first in ((1, DST), (2, SRC)):
                        last = nc.vector.tensor_reduce(
                            batch_max[:, n, :],
                            score[q][:, :, first:first + HEADS * TYPES:TYPES].rearrange("p t h -> p h t"),
                            axis=AX.X, op=ALU.max, apply_absolute_value=True)
                    last.then_inc(max_done, 1)

                def take_extremes(b):
                    dve.wait_ge(max_done, done(3 * b))
                    nc.vector.tensor_tensor(extremes[:], extremes[:], batch_max[:], ALU.max
                                            ).then_inc(max_done, 1)

                def slots(b, q):
                    inside = not is_at(b, batches)
                    next_too = inside and not is_at(b, batches - 1)
                    for r in range(pairs):
                        if inside:
                            copy_transposed(b, r)
                        if r == SUM_LAG + 1 and not is_at(b, 0):
                            take_sum(b - 1)
                        at_score = lagging(b, q, r, SCORE_LAG, pairs)
                        if at_score:
                            for t in (2 * at_score[2], 2 * at_score[2] + 1):
                                copy_score(at_score[0], at_score[1], t)
                        if r == SUM_LAG and not is_at(b, 0):
                            take_batch_max(b - 1, 1 - q)
                        at_max = lagging(b, q, r, SUM_LAG, pairs)
                        if at_max:
                            take_pair_max(*at_max)
                        at_uv = lagging(b, q, r, UV_LAG, pairs)
                        if at_uv:
                            for t in (2 * at_uv[2], 2 * at_uv[2] + 1):
                                make_uv(at_uv[0], at_uv[1], t)
                        if r == SUM_LAG + 1 and not is_at(b, 0):
                            take_extremes(b - 1)
                            take_sum_lo(b - 1)
                        if next_too:
                            if r >= 2 and r - 2 < groups:
                                take_stats(b + 1, 1 - q, 4 * (r - 2))
                            if r >= 3 and r - 3 < groups:
                                take_mean_var(b + 1, 4 * (r - 3))
                            if r == pairs - 1:
                                invert_deviation(b + 1, 1 - q)
                    if next_too:
                        take_shift(b + 1, 1 - q)

                for g in range(groups):
                    take_stats(0, 0, 4 * g)
                for g in range(groups):
                    take_mean_var(0, 4 * g)
                invert_deviation(0, 0)
                take_shift(0, 0)
                all_batches(dve, slots)


def load_edge_tile(sp, adj_rows, edge, edge_loaded, m, slot):
    sp.dma_start(edge[slot][:], adj_rows[bass.ds(m * P, P), :]).then_inc(edge_loaded[slot], 16)


def cast_edge_tile(nc, act, edge, a_row, edge_loaded, degree, cast_done, m, slot):
    act.wait_ge(edge_loaded[slot], 16 * done(m // 2))
    nc.scalar.activation(a_row[slot][:].rearrange("p t c -> p (t c)"), edge[slot][:], ACT.Copy,
                         accum_out=degree[:, bass.ds(m, 1)]).then_inc(cast_done, 1)


def edges_block(nc, sb, ps, sem, batches, tiles, units, batch_units, x_rows, adj_rows, out_rows,
                h_dram, uv_dram, scoreT_dram, hsum_dram, ident16, bias_b, gamma_b, beta_b,
                rho, neg_d, eps, degree, sum_aa, casts, uv0):
    all_tiles = UNIT_TILES * units
    passes = all_tiles
    chunks = tiles // 4
    by_act = (1, 3)
    T_AHEAD, AV_AHEAD, CAST_AHEAD = 5, 3, 6
    half_tiles = tiles // 2
    body = 2 * UNIT_TILES
    edge, a_row, edge_loaded, cast_done, a_turned = casts
    with ExitStack() as s:
        at = [sb(s, f"at{i}", [P, tiles, UNIT], BF16) for i in (0, 1)]
        mask = [sb(s, f"mask{i}", [P, tiles, UNIT], BF16) for i in (0, 1)]
        step = [sb(s, f"step{i}", [P, 4, UNIT], BF16) for i in range(len(by_act))]
        uv = [uv0, sb(s, "uv1", [P, tiles, HEADS, 4 * AUG], F16)]
        hsum = sb(s, "hsum_b", [P, 2 * 2 * HEADS * AUG], F16)
        s_row = sb(s, "s_row", [P, HEADS, UNIT], F32)
        h_own = [sb(s, f"h_own{i}", [P, UNIT_TILES, DIM], F32) for i in (0, 1)]
        y = [sb(s, f"y{i}", [P, UNIT_TILES, DIM], F32) for i in (0, 1)]
        seg = [sb(s, f"seg{i}", [P, UNIT_TILES, 4 * AUG], F32) for i in (0, 1)]
        av = [sb(s, f"av{i}", [P, UNIT_TILES, HEADS, AUG], F32) for i in (0, 1)]
        both = sb(s, "both", [P, UNIT_TILES, 2 * AUG], F32)
        num = sb(s, "num", [P, UNIT_TILES, AUG], F32)
        v_part = sb(s, "v_part", [P, UNIT_TILES, AUG], F32)
        rden = sb(s, "rden", [P, UNIT_TILES], F32)
        o = [sb(s, f"o{i}", [P, UNIT_TILES, HEAD_DIM], F32) for i in (0, 1)]
        sq = sb(s, "sq", [P, UNIT_TILES, HEAD_DIM], F32)
        stat = sb(s, "stat", [P, 4, UNIT_TILES], F32)
        squares = [sb(s, f"squares{i}", [P, 2 * UNIT_TILES], F32) for i in (0, 1)]
        neg_now = [sb(s, f"neg_now{i}", [P, HEADS * tiles], F32) for i in (0, 1)]
        step_now = [sb(s, f"step_now{i}", [P, HEADS * tiles], F32) for i in (0, 1)]
        neg_degree = [sb(s, f"neg_degree{i}", [P, 1], F32) for i in (0, 1)]
        lone = [sb(s, f"lone{i}", [P, P], BF16) for i in (0, 1)]
        scaled = sb(s, "scaled", [P, UNIT_TILES, HEAD_DIM], F32)
        m_ps = [ps(s, f"m_ps{i}", [P, 2, 512], F32) for i in (0, 1)]
        a_ps = [ps(s, f"a_ps{i}", [P, half_tiles, P], BF16) for i in (0, 1)]
        av_ps = [ps(s, f"av_ps{i}", [P, 512], F32) for i in (0, 1)]

        own_loaded = [sem(s, f"own_loaded{i}") for i in (0, 1)]
        s_loaded = [sem(s, f"s_loaded{h}") for h in range(HEADS)]
        y_stored = [sem(s, f"y_stored{i}") for i in (0, 1)]
        uv_loaded, passed = sem(s, "uv_loaded"), sem(s, "passed")
        at_done, unit_ready, degree_done = (sem(s, "at_done"), sem(s, "unit_ready"),
                                            sem(s, "degree_done"))
        lone_done, av_made, av_copied = sem(s, "lone_done"), sem(s, "av_made"), sem(s, "av_copied")
        step_done, masks_done = sem(s, "step_done"), sem(s, "masks_done")
        m_made, chunk_used, m_copied = sem(s, "m_made"), sem(s, "chunk_used"), sem(s, "m_copied")
        fin_step, folded, av_used = sem(s, "fin_step"), sem(s, "folded"), sem(s, "av_used")
        h_used, centred, squared = sem(s, "h_used"), sem(s, "centred"), sem(s, "squared")
        var_done, dev_done = sem(s, "var_done"), sem(s, "dev_done")
        rstd_done, scale_done, gamma_done = (sem(s, "rstd_done"), sem(s, "scale_done"),
                                             sem(s, "gamma_done"))
        y_based, y_done = sem(s, "y_based"), sem(s, "y_done")

        def over(t, n=HEAD_DIM):
            return t.unsqueeze(2).to_broadcast([P, UNIT_TILES, n])

        def row_of_head(row, h):
            cols = row[:, h * HEAD_DIM:(h + 1) * HEAD_DIM]
            return cols.unsqueeze(1).to_broadcast([P, UNIT_TILES, HEAD_DIM])

        with nc.Block() as block:

            @block.gpsimd
            def _(pool):
                for one in (at_done, unit_ready, degree_done, lone_done, av_made,
                            av_copied, step_done, masks_done, m_made, chunk_used, m_copied, folded,
                            av_used, h_used, centred, squared, var_done, dev_done, y_based, y_done,
                            rstd_done, scale_done, gamma_done):
                    pool.sem_inc(one, START)
                for one in (*own_loaded, *s_loaded, *y_stored, uv_loaded):
                    pool.sem_inc(one, 16 * START)

                def add_beta(k, q):
                    pool.wait_ge(own_loaded[q], 16 * (2 * (k // 2) + 2 + START))
                    nc.gpsimd.tensor_tensor(y[q][:], y[q][:],
                                            beta_b[:].unsqueeze(1).to_broadcast([P, UNIT_TILES, DIM]),
                                            ALU.add).then_inc(y_based, 1)

                def take_v_part(g, i):
                    h, q = i % HEADS, i // HEADS % 2
                    if h == 0:
                        pool.wait_ge(av_copied, done(g + UNIT_TILES - 1))
                    pool.wait_ge(folded, done(g))
                    nc.gpsimd.tensor_tensor(v_part[:], av[q][:, :, h, :], both[:, :, AUG:2 * AUG],
                                            ALU.subtract).then_inc(av_used, 1)

                def square(g, i):
                    pool.wait_ge(centred, done(g))
                    nc.gpsimd.tensor_tensor(sq[:], o[i % 2][:], o[i % 2][:], ALU.mult).then_inc(squared, 1)

                def add_to_y(g, i):
                    h, q = i % HEADS, i // HEADS % 2
                    pool.wait_ge(scale_done, done(g))
                    nc.gpsimd.tensor_tensor(scaled[:], scaled[:], row_of_head(gamma_b, h), ALU.mult
                                            ).then_inc(gamma_done, 1)
                    pool.wait_ge(gamma_done, done(g))
                    if h == 0:
                        pool.wait_ge(y_based, done(g // HEADS))
                    cols = y[q][:, :, h * HEAD_DIM:(h + 1) * HEAD_DIM]
                    nc.gpsimd.tensor_tensor(cols, cols, scaled[:], ALU.add).then_inc(y_done, 1)

                def turn(g, i, first):
                    take_v_part(g, i)
                    if i % HEADS == 0:
                        add_beta(g // HEADS, i // HEADS % 2)
                    square(g, i)
                    if not first:
                        add_to_y(g - 1, i - 1)

                for i in range(body):
                    turn(i, i, i == 0)
                with pool.Fori(1, passes // body) as r:
                    for i in range(body):
                        turn(r * body + i, i, False)
                add_to_y(passes - 1, body - 1)

            @block.sync
            def _(sp):
                def load_scores(p, unit, h):
                    row = SRC + h * TYPES
                    cols = bass.ds(unit % units * UNIT, UNIT)
                    sp.dma_start(s_row[:, h, :], scoreT_dram[row:row + 1, cols].to_broadcast([P, UNIT])
                                 ).then_inc(s_loaded[h], 16)

                def load_sums(g, q, part):
                    width = 2 * HEADS * AUG // batch_units
                    row = hsum_dram[bass.ds(g // batch_units % batches, 1), part * width:(part + 1) * width]
                    first = (q * batch_units + part) * width
                    sp.dma_start(hsum[:, first:first + width], row.to_broadcast([P, width])
                                 ).then_inc(uv_loaded, 16)

                def load_uv(g, q, part):
                    at = (g - batch_units) % (units - batch_units) + batch_units
                    rows = uv_dram[bass.ds(at * UNIT, UNIT), :]
                    sp.dma_start(uv[q][:, part * UNIT_TILES:(part + 1) * UNIT_TILES, :, :].rearrange(
                        "p t h c -> p t (h c)"),
                        rows.rearrange("(t p) c -> p t c", p=P)).then_inc(uv_loaded, 16)

                def unit_rows(dram, k):
                    return dram[bass.ds(k * UNIT, UNIT), :].rearrange("(t p) d -> p t d", p=P)

                def store(k, q):
                    sp.wait_ge(y_done, done(HEADS * k + HEADS - 1))
                    sp.dma_start(unit_rows(out_rows, k), y[q][:]).then_inc(y_stored[q], 16)

                def unit(k, u, first):
                    q = u % 2
                    sp.wait_ge(m_made, done(2 * (k // batch_units * tiles) - 1))
                    wait_apart(sp, uv_loaded, 16 * (2 * (k + batch_units) + START), passed)
                    load_uv(k + batch_units, 1 - u // batch_units, u % batch_units)
                    load_sums(k + batch_units, 1 - u // batch_units, u % batch_units)
                    sp.wait_ge(h_used, freed(HEADS * k, HEADS + 1))
                    sp.dma_start(h_own[q][:], unit_rows(h_dram, k)).then_inc(own_loaded[q], 16)
                    sp.wait_ge(y_stored[q], 16 * (k // 2 + START))
                    sp.dma_start(y[q][:], unit_rows(x_rows, k)).then_inc(own_loaded[q], 16)
                    for h in range(HEADS):
                        p = HEADS * k + h
                        wait_apart(sp, masks_done, done(chunks * p - 1), passed)
                        load_scores(p + 3, k + (h + 3) // HEADS, (h + 3) % HEADS)
                        sp.wait_ge(cast_done, done(p + CAST_AHEAD - 1))
                        load_edge_tile(sp, adj_rows, edge, edge_loaded, (p + CAST_AHEAD + 1) % all_tiles,
                                       (h + CAST_AHEAD + 1) % 2)
                        if h == 3 and not first:
                            store(k - 1, 1 - q)

                for h in range(3):
                    load_scores(h, 0, h)
                for part in range(batch_units):
                    load_sums(0, 0, part)
                    sp.sem_inc(uv_loaded, 16)
                for m in range(4, CAST_AHEAD + 1):
                    sp.wait_ge(cast_done, done(m - 2))
                    load_edge_tile(sp, adj_rows, edge, edge_loaded, m, m % 2)
                for u in range(2 * batch_units):
                    unit(u, u, u == 0)
                if batches > 2:
                    with sp.Fori(1, batches // 2) as i:
                        for u in range(2 * batch_units):
                            unit(2 * batch_units * i + u, u, False)
                store(units - 1, 1)
                for q in (0, 1):
                    sp.wait_ge(y_stored[q], 16 * (START + units // 2))

            @block.scalar
            def _(act):
                def cast(m, slot):
                    act.wait_ge(a_turned, freed(2 * m + 1, 4))
                    cast_edge_tile(nc, act, edge, a_row, edge_loaded, degree, cast_done, m, slot)

                def take_at(m, parity, it, half):
                    if it == 0 and half == 0:
                        act.wait_ge(masks_done, freed(chunks * m, chunks * HEADS + 1))
                    act.wait_ge(a_turned, done(2 * m + half))
                    nc.scalar.activation(
                        at[parity][:, half_tiles * half:half_tiles * (half + 1), it * P:(it + 1) * P],
                        a_ps[half][:], ACT.Square,
                        accum_out=squares[parity][:, 2 * it + half:2 * it + half + 1]
                    ).then_inc(at_done, 1)

                def mark_lone(n, slot):
                    act.wait_ge(degree_done, done(n))
                    act.wait_ge(av_made, freed(n, 2))
                    nc.scalar.activation(lone[slot][:], ident16[:], ACT.Relu, bias=neg_degree[slot][:]
                                         ).then_inc(lone_done, 1)

                def take_av(n, parity, it):
                    if it == 0:
                        act.wait_ge(av_used, freed(n, HEADS + 1))
                    act.wait_ge(av_made, done(n))
                    nc.scalar.activation(av[parity][:, it, :, :].rearrange("p h e -> p (h e)"),
                                         av_ps[it % 2][:, 0:HEADS * AUG], ACT.Copy
                                         ).then_inc(av_copied, 1)

                def compare(p, parity, h, c):
                    slot = by_act.index(c)
                    if slot == 0:
                        act.wait_ge(s_loaded[h], 16 * done(p // HEADS))
                        act.wait_ge(unit_ready, done(p // HEADS))
                    act.wait_ge(masks_done, freed(chunks * p + c, chunks))
                    for j in range(4):
                        col = h * tiles + 4 * c + j
                        last = nc.scalar.activation(step[slot][:, j, :], s_row[:, h, :], ACT.Relu,
                                                    scale=STEP, bias=step_now[parity][:, col:col + 1])
                    last.then_inc(step_done, 1)

                def take_products(p, h, pair):
                    act.wait_ge(m_made, done(2 * p + pair))
                    if pair == 0:
                        act.wait_ge(folded, freed(p, 2))
                    nc.scalar.activation(seg[h % 2][:, 2 * pair:2 * pair + 2, :],
                                         m_ps[pair][:, :, 0:4 * AUG], ACT.Copy).then_inc(m_copied, 1)

                def head_deviation(g):
                    act.wait_ge(var_done, done(g))
                    nc.scalar.activation(stat[:, 2, :], stat[:, 1, :], ACT.Sqrt, bias=eps[:, 1:2],
                                         scale=1.0 / HEAD_DIM).then_inc(dev_done, 1)

                def turn(p, i, first, last):
                    h = i % HEADS
                    m, n = i + T_AHEAD, i + AV_AHEAD
                    ahead = (p + 1, (i + 1) // HEADS % 2, (i + 1) % HEADS)
                    if not last:
                        compare(*ahead, by_act[0])
                    cast(p + CAST_AHEAD, (i + CAST_AHEAD) % 2)
                    take_products(p, h, 0)
                    take_av(p + AV_AHEAD, n // UNIT_TILES % 2, n % UNIT_TILES)
                    mark_lone(p + AV_AHEAD + 1, (n + 1) % 2)
                    if not first:
                        head_deviation(p - 2)
                    if not last:
                        compare(*ahead, by_act[1])
                    take_at(p + T_AHEAD, m // UNIT_TILES % 2, m % UNIT_TILES, 0)
                    take_products(p, h, 1)
                    take_at(p + T_AHEAD, m // UNIT_TILES % 2, m % UNIT_TILES, 1)

                for n in (0, 1):
                    mark_lone(n, n)
                for m in range(UNIT_TILES):
                    for half in (0, 1):
                        take_at(m, 0, m, half)
                    if m < 2:
                        cast(m + 2, m % 2)
                for c in by_act:
                    compare(0, 0, 0, c)
                for n in range(AV_AHEAD):
                    take_av(n, 0, n)
                    if n + 2 <= AV_AHEAD:
                        mark_lone(n + 2, n % 2)
                        cast(n + 4, n % 2)
                for half in (0, 1):
                    take_at(4, 1, 0, half)
                for i in range(body):
                    turn(i, i, i < 2, False)
                if passes > 2 * body:
                    with act.Fori(1, passes // body - 1) as r:
                        for i in range(body):
                            turn(r * body + i, i, False, False)
                for i in range(body):
                    turn(passes - body + i, i, False, i == body - 1)
                head_deviation(passes - 2)
                head_deviation(passes - 1)

            @block.tensor
            def _(pe):
                def transpose(m, i, half):
                    if half == 0:
                        pe.wait_ge(cast_done, done(m))
                    pe.wait_ge(at_done, freed(2 * m + half, 2))
                    for j in range(half_tiles):
                        last = nc.tensor.transpose(a_ps[half][:, j, :],
                                                   a_row[i % 2][:, half_tiles * half + j, :], ident16[:])
                    last.then_inc(a_turned, 1)

                def multiply_a(n, i, q, c):
                    parity, it = i // UNIT_TILES % 2, i % UNIT_TILES
                    out = av_ps[it % 2][:, 0:HEADS * AUG]
                    if c == 0:
                        pe.wait_ge(av_copied, freed(n, 2))
                        pe.wait_ge(at_done, done(2 * n + 1))
                    for j in range(4 * c, 4 * c + 4):
                        for part in (0, 1):
                            v = slice((2 * part + 1) * AUG, (2 * part + 2) * AUG)
                            nc.tensor.matmul(out, at[parity][:, j, it * P:(it + 1) * P],
                                             uv[q][:, j, :, v], start=j == 0 and part == 0,
                                             stop=False)
                    if c == chunks - 1:
                        pe.wait_ge(lone_done, done(n))
                        for part in (0, 1):
                            first = (2 * q + part) * HEADS * AUG
                            last = nc.tensor.matmul(out, lone[it % 2][:], hsum[:, first:first + HEADS * AUG],
                                                    start=False, stop=part == 1)
                        last.then_inc(av_made, 1)

                def multiply_m(p, i, pair, q, c):
                    h = i % HEADS
                    if c == 0:
                        pe.wait_ge(m_copied, freed(2 * p + pair, 2))
                    if pair == 0:
                        pe.wait_ge(masks_done, done(chunks * p + c))
                    for it in (2 * pair, 2 * pair + 1):
                        for j in range(4 * c, 4 * c + 4):
                            last = nc.tensor.matmul(m_ps[pair][:, it % 2, 0:4 * AUG],
                                                    mask[i % 2][:, j, it * P:(it + 1) * P],
                                                    uv[q][:, j, h, :], start=j == 0,
                                                    stop=j == tiles - 1)
                    if c == chunks - 1:
                        last.then_inc(m_made, 1)
                    elif pair == 1:
                        last.then_inc(chunk_used, 1)

                for m in range(UNIT_TILES):
                    for half in (0, 1):
                        transpose(m, m, half)
                pe.wait_ge(uv_loaded, 16 * (2 * batch_units + START))
                for n in range(AV_AHEAD):
                    for c in range(chunks):
                        multiply_a(n, n, 0, c)
                for half in (0, 1):
                    transpose(UNIT_TILES, UNIT_TILES, half)
                with pe.Fori(0, batches // 2) as r:
                    for i in range(2 * tiles):
                        p = 2 * tiles * r + i
                        q = i // tiles
                        q_ahead = (i + AV_AHEAD) // tiles % 2
                        if (i + AV_AHEAD) % tiles == 0:
                            pe.wait_ge(uv_loaded, 16 * (2 * batch_units * (2 * r + q + 2) + START))
                        for c in range(chunks):
                            multiply_m(p, i, 0, q, c)
                            multiply_a(p + AV_AHEAD, i + AV_AHEAD, q_ahead, c)
                        for c in range(chunks):
                            multiply_m(p, i, 1, q, c)
                            if c % 2 == 0:
                                transpose(p + T_AHEAD, i + T_AHEAD, c // 2)

            @block.vector
            def _(dve):
                def prepare_unit(k, parity):
                    now = neg_d[:, bass.ds(k % units // batch_units * (HEADS * tiles), HEADS * tiles)]
                    nc.vector.tensor_copy(neg_now[parity][:], now)
                    nc.vector.tensor_scalar(step_now[parity][:], now, -STEP, None, ALU.mult
                                            ).then_inc(unit_ready, 1)

                def finish_steps(g, i):
                    STEPS = 6
                    h, parity = i % HEADS, i // HEADS % 2

                    def own(done_steps):
                        dve.wait_ge(fin_step, STEPS * g + done_steps)

                    def fold_parts():
                        dve.wait_ge(m_copied, done(2 * g + 1))
                        nc.vector.tensor_tensor(both[:], seg[h % 2][:, :, 0:2 * AUG],
                                                seg[h % 2][:, :, 2 * AUG:4 * AUG], ALU.add
                                                ).then_inc(folded, 1)

                    def times_rho():
                        dve.wait_ge(folded, done(g))
                        rows = rho[:, bass.ds(g // HEADS * UNIT_TILES, UNIT_TILES), h]
                        nc.vector.tensor_tensor(num[:], both[:, :, 0:AUG], over(rows, AUG), ALU.mult
                                                ).then_inc(fin_step, 1)

                    def add_v_part():
                        own(1)
                        dve.wait_ge(av_used, done(g))
                        nc.vector.tensor_tensor(num[:], num[:], v_part[:], ALU.add).then_inc(fin_step, 1)

                    def invert():
                        own(2)
                        nc.vector.reciprocal(rden[:], num[:, :, HEAD_DIM]).then_inc(fin_step, 1)

                    def divide():
                        own(3)
                        dve.wait_ge(scale_done, done(g - 2))
                        nc.vector.tensor_tensor(o[i % 2][:], num[:, :, 0:HEAD_DIM], over(rden[:]), ALU.mult
                                                ).then_inc(fin_step, 1)

                    def add_bias():
                        own(4)
                        nc.vector.tensor_tensor(o[i % 2][:], o[i % 2][:], row_of_head(bias_b, h), ALU.add
                                                ).then_inc(fin_step, 1)

                    def relu_add_h():
                        own(5)
                        if h == 0:
                            dve.wait_ge(own_loaded[parity], 16 * (2 * (g // body) + 2 + START))
                        nc.vector.scalar_tensor_tensor(
                            out=o[i % 2][:], in0=o[i % 2][:], scalar=0.0,
                            in1=h_own[parity][:, :, h * HEAD_DIM:(h + 1) * HEAD_DIM],
                            op0=ALU.max, op1=ALU.add).then_inc(h_used, 1)

                    def head_sum():
                        dve.wait_ge(h_used, done(g))
                        nc.vector.tensor_reduce(stat[:, 0, :], o[i % 2][:], axis=AX.X, op=ALU.add
                                                ).then_inc(fin_step, 1)

                    def centre():
                        own(6)
                        nc.vector.scalar_tensor_tensor(out=o[i % 2][:], in0=over(stat[:, 0, :]),
                                                       scalar=1.0 / HEAD_DIM, in1=o[i % 2][:],
                                                       op0=ALU.mult, op1=ALU.subtract).then_inc(centred, 1)

                    return [[fold_parts], [lambda: variance(g - 1)], [times_rho], [add_v_part],
                            [invert], [divide],
                            [add_bias], [relu_add_h], [head_sum], [lambda: invert_deviation(g - 1)],
                            [centre], [lambda: scale(g - 1, i - 1)]]

                def variance(g):
                    if isinstance(g, int) and g < 0:
                        return
                    dve.wait_ge(squared, done(g))
                    nc.vector.tensor_reduce(stat[:, 1, :], sq[:], axis=AX.X, op=ALU.add
                                            ).then_inc(var_done, 1)

                def invert_deviation(g):
                    if isinstance(g, int) and g < 0:
                        return
                    dve.wait_ge(dev_done, done(g))
                    nc.vector.reciprocal(stat[:, 3, :], stat[:, 2, :]).then_inc(rstd_done, 1)

                def scale(g, i):
                    if isinstance(g, int) and g < 0:
                        return
                    dve.wait_ge(rstd_done, done(g))
                    dve.wait_ge(y_done, done(g - 1))
                    nc.vector.scalar_tensor_tensor(out=scaled[:], in0=o[i % 2][:], scalar=-1.0,
                                                   in1=over(stat[:, 3, :]), op0=ALU.mult,
                                                   op1=ALU.mult).then_inc(scale_done, 1)

                def turn(p, i, finish):
                    h, parity = i % HEADS, i // HEADS % 2
                    k = p // HEADS
                    if h == 2:
                        prepare_unit(k + 1, 1 - parity)
                    if h == 0:
                        dve.wait_ge(at_done, done(2 * (UNIT_TILES * k + UNIT_TILES - 1) + 1))
                        nc.vector.tensor_tensor(sum_aa[:], sum_aa[:], squares[parity][:], ALU.add)
                    if finish:
                        negate_degree(p + AV_AHEAD + 1, (i + AV_AHEAD + 1) % 2)
                    steps = finish_steps(p - 2, i - 2) if finish else [[]] * 12
                    at_step = iter(steps)
                    for c in range(chunks):
                        if c < chunks - 1:
                            dve.wait_ge(chunk_used, freed((chunks - 1) * p + c, 2 * (chunks - 1)))
                        else:
                            dve.wait_ge(m_made, freed(2 * p + 1, 4))
                        if c in by_act:
                            dve.wait_ge(step_done, done(len(by_act) * p + by_act.index(c)))
                            nc.vector.tensor_tensor(mask[i % 2][:, 4 * c:4 * c + 4, :],
                                                    step[by_act.index(c)][:],
                                                    at[parity][:, 4 * c:4 * c + 4, :], ALU.min
                                                    ).then_inc(masks_done, 1)
                            for one in next(at_step) + next(at_step):
                                one()
                            if not finish:
                                n = 2 + len(by_act) * i + by_act.index(c)
                                negate_degree(n, n % 2)
                            continue
                        if c == 0:
                            dve.wait_ge(s_loaded[h], 16 * done(k))
                        for j in range(4 * c, 4 * c + 4):
                            last = nc.vector.scalar_tensor_tensor(
                                out=mask[i % 2][:, j, :], in0=s_row[:, h, :],
                                scalar=neg_now[parity][:, h * tiles + j:h * tiles + j + 1],
                                in1=at[parity][:, j, :], op0=ALU.is_gt, op1=ALU.mult)
                            if j % 4 == 3:
                                last.then_inc(masks_done, 1)
                            for one in next(at_step):
                                one()

                def negate_degree(n, slot):
                    dve.wait_ge(cast_done, done(n))
                    dve.wait_ge(lone_done, freed(n, 2))
                    nc.vector.tensor_scalar(neg_degree[slot][:], degree[:, bass.ds(n, 1)], -1.0, None,
                                            ALU.mult).then_inc(degree_done, 1)

                prepare_unit(0, 0)
                dve.wait_ge(unit_ready, done(0))
                for n in (0, 1):
                    negate_degree(n, n % 2)
                for i in range(body):
                    turn(i, i, i >= 2)
                with dve.Fori(1, passes // body) as r:
                    for i in range(body):
                        turn(r * body + i, i, True)
                for g in (passes - 2, passes - 1):
                    for steps in finish_steps(g, g % body):
                        for one in steps:
                            one()
                variance(passes - 1)
                invert_deviation(passes - 1)
                scale(passes - 1, body - 1)


def verdict_block(nc, sb, ps, sem, all_tiles, extremes, degree, sum_aa, verdict):
    with ExitStack() as s:
        sums = sb(s, "sums", [P, 2], F32)
        total = sb(s, "total", [P, 2], F32)
        most = sb(s, "most", [P, 3, HEADS], F32)
        good = sb(s, "good", [P, 5, HEADS], F32)
        all_good = sb(s, "all_good", [P, 1], F32)
        summed, reduced, step = sem(s, "summed"), sem(s, "reduced"), sem(s, "verdict_step")
        with nc.Block() as block:

            @block.vector
            def _(dve):
                nc.vector.tensor_reduce(sums[:, 0:1], degree[:, 0:all_tiles], axis=AX.X, op=ALU.add)
                nc.vector.tensor_reduce(sums[:, 1:2], sum_aa[:], axis=AX.X, op=ALU.add).then_inc(summed, 1)
                dve.wait_ge(reduced, 1)
                for n, bound, op in ((0, MAX_H, ALU.is_le), (1, MAX_DST, ALU.is_le),
                                     (2, MAX_SRC, ALU.is_le)):
                    nc.vector.tensor_scalar(good[:, n, :], most[:, n, :], bound, None, op)
                nc.vector.tensor_scalar(good[:, 3, :], most[:, 0, :], MIN_H, None, ALU.is_ge)
                nc.vector.tensor_tensor(good[:, 4, :], total[:, 0:1].to_broadcast([P, HEADS]),
                                        total[:, 1:2].to_broadcast([P, HEADS]), ALU.is_equal
                                        ).then_inc(step, 1)
                dve.wait_ge(step, 1)
                nc.vector.tensor_reduce(all_good[:], good[:], axis=AX.XY, op=ALU.min).then_inc(step, 1)
                dve.wait_ge(step, 2)
                nc.vector.tensor_scalar(verdict[:], all_good[:], 0.0, None, ALU.is_equal)

            @block.gpsimd
            def _(pool):
                pool.wait_ge(summed, 1)
                nc.gpsimd.partition_all_reduce(most[:].rearrange("p a h -> p (a h)"),
                                               extremes[:].rearrange("p a h -> p (a h)"), P,
                                               bass.bass_isa.ReduceOp.max)
                nc.gpsimd.partition_all_reduce(total[:], sums[:], P, bass.bass_isa.ReduceOp.add
                                               ).then_inc(reduced, 1)


def general_block(nc, sb, ps, sem, batches, tiles, all_tiles, x_rows, adj_rows, out_rows, h_dram,
                  score_dram, scoreT_dram, ident32, bias_b, gamma_b, beta_b, eps, verdict):
    span = tiles * P
    with ExitStack() as s:
        edge = sb(s, "g_edge", [P, span], I32)
        target = sb(s, "g_target", [P, TYPES, span], F32)
        match = sb(s, "g_match", [P, span], F32)
        weight = sb(s, "g_weight", [P, span], F32)
        probs_t = sb(s, "g_probs_t", [P, tiles, P], F32)
        h_head = sb(s, "g_h_head", [P, tiles, HEAD_DIM], F32)
        source = sb(s, "g_source", [P, PROJ], F32)
        h_own = sb(s, "g_h_own", [P, DIM], F32)
        x_own = sb(s, "g_x_own", [P, DIM], F32)
        neg_max = sb(s, "g_neg_max", [P, 1], F32)
        row_sum = sb(s, "g_row_sum", [P, 1], F32)
        inv_sum = sb(s, "g_inv_sum", [P, 1], F32)
        o = sb(s, "g_o", [P, DIM], F32)
        sq = sb(s, "g_sq", [P, DIM], F32)
        hstat = sb(s, "g_hstat", [P, 4, HEADS], F32)
        t_ps = ps(s, "g_t_ps", [P, tiles, P], F32)
        o_ps = ps(s, "g_o_ps", [P, 512], F32)
        own_loaded, head_loaded = sem(s, "g_own_loaded"), sem(s, "g_head_loaded")
        weight_done, probs_done = sem(s, "g_weight_done"), sem(s, "g_probs_done")
        turned, turned_copied, product_done = (sem(s, "g_turned"), sem(s, "g_turned_copied"),
                                               sem(s, "g_product_done"))
        head_done, var_done, dev_done = sem(s, "g_head_done"), sem(s, "g_var_done"), sem(s, "g_dev_done")
        y_done, y_stored, chain = sem(s, "g_y_done"), sem(s, "g_y_stored"), sem(s, "g_chain")
        OWN, HEAD = 4, 2

        def by_head(t):
            return t[:].rearrange("p (h e) -> p h e", h=HEADS)

        def over_head(t):
            return t.unsqueeze(2).to_broadcast([P, HEADS, HEAD_DIM])

        with nc.Block() as block:

            @block.sync
            def _(sp):
                wrong = sp.value_load(verdict[0:1, 0:1], min_val=0, max_val=1)
                with sp.If(wrong > 0):
                    for one in (head_done, product_done):
                        sp.sem_inc(one, 1)
                    sp.sem_inc(y_stored, 16)
                    with sp.Fori(0, all_tiles) as n:
                        rows = bass.ds(n * P, P)
                        b = n // tiles
                        sp.wait_ge(y_stored, 16 * n + 16)
                        for to, row in ((edge, adj_rows), (source, score_dram), (h_own, h_dram),
                                        (x_own, x_rows)):
                            sp.dma_start(to[:], row[rows, :]).then_inc(own_loaded, 16)
                        for h in range(HEADS):
                            sp.wait_ge(head_done, HEADS * n + h + 1)
                            first = DST + h * TYPES
                            sp.dma_start(target[:], scoreT_dram[first:first + TYPES,
                                                                bass.ds(b * span, span)]
                                         .rearrange("(o t) n -> o t n", o=1)
                                         .to_broadcast([P, TYPES, span])).then_inc(head_loaded, 16)
                            sp.dma_start(h_head[:],
                                         h_dram[bass.ds(b * span, span), h * HEAD_DIM:(h + 1) * HEAD_DIM]
                                         .rearrange("(t p) e -> p t e", p=P)).then_inc(head_loaded, 16)
                        sp.wait_ge(y_done, n + 1)
                        sp.dma_start(out_rows[rows, :], o[:]).then_inc(y_stored, 16)
                    sp.wait_ge(y_stored, 16 * all_tiles + 16)
                sp.nop()

            @block.scalar
            def _(act):
                wrong = act.value_load(verdict[0:1, 0:1], min_val=0, max_val=1)
                with act.If(wrong > 0):
                    with act.Fori(0, all_tiles) as n:
                        for h in range(HEADS):
                            act.wait_ge(weight_done, HEADS * n + h + 1)
                            nc.scalar.activation(weight[:], weight[:], ACT.Exp, bias=neg_max[:],
                                                 accum_out=row_sum[:]).then_inc(probs_done, 1)
                            act.wait_ge(turned, HEADS * n + h + 1)
                            for quarter in range(tiles // 4):
                                cols = slice(4 * quarter, 4 * quarter + 4)
                                last = nc.scalar.activation(probs_t[:, cols, :], t_ps[:, cols, :], ACT.Copy)
                            last.then_inc(turned_copied, 1)
                        act.wait_ge(var_done, n + 1)
                        nc.scalar.activation(hstat[:, 2, :], hstat[:, 1, :], ACT.Sqrt, bias=eps[:, 1:2],
                                             scale=1.0 / HEAD_DIM).then_inc(dev_done, 1)
                act.nop()

            @block.tensor
            def _(pe):
                wrong = pe.value_load(verdict[0:1, 0:1], min_val=0, max_val=1)
                with pe.If(wrong > 0):
                    with pe.Fori(0, all_tiles) as n:
                        for h in range(HEADS):
                            pe.wait_ge(probs_done, HEADS * n + h + 1)
                            for j in range(tiles):
                                last = nc.tensor.transpose(t_ps[:, j, :], weight[:, j * P:(j + 1) * P],
                                                           ident32[:])
                            last.then_inc(turned, 1)
                            pe.wait_ge(turned_copied, HEADS * n + h + 1)
                            pe.wait_ge(head_loaded, 16 * HEAD * (HEADS * n + h + 1))
                            pe.wait_ge(head_done, HEADS * n + h + 1)
                            for j in range(tiles):
                                last = nc.tensor.matmul(o_ps[:, 0:HEAD_DIM], probs_t[:, j, :],
                                                        h_head[:, j, :], start=j == 0,
                                                        stop=j == tiles - 1)
                            last.then_inc(product_done, 1)
                pe.nop()

            @block.vector
            def _(dve):
                CHAIN = 3 * TYPES + 3
                TAIL = 9
                wrong = dve.value_load(verdict[0:1, 0:1], min_val=0, max_val=1)
                with dve.If(wrong > 0):
                    with dve.Fori(0, all_tiles) as n:
                        links = [0]

                        def link(instruction):
                            links[0] += 1
                            instruction.then_inc(chain, 1)
                            dve.wait_ge(chain, (HEADS * CHAIN + TAIL) * n + links[0])

                        dve.wait_ge(own_loaded, 16 * OWN * (n + 1))
                        for h in range(HEADS):
                            dve.wait_ge(head_loaded, 16 * HEAD * (HEADS * n + h + 1))
                            for t in range(TYPES):
                                link(nc.vector.tensor_scalar(match[:], edge[:], float(t + 1), None,
                                                             ALU.is_equal))
                                col = SRC + h * TYPES + t
                                to = weight if t == 0 else target[:, t, :]
                                link(nc.vector.scalar_tensor_tensor(
                                    out=to[:] if t == 0 else to, in0=target[:, t, :],
                                    scalar=source[:, col:col + 1], in1=match[:], op0=ALU.add, op1=ALU.mult))
                                if t:
                                    link(nc.vector.tensor_tensor(weight[:], weight[:], target[:, t, :],
                                                                 ALU.add))
                            link(nc.vector.scalar_tensor_tensor(out=weight[:], in0=weight[:], scalar=0.01,
                                                                in1=weight[:], op0=ALU.mult, op1=ALU.max))
                            link(nc.vector.tensor_scalar(match[:], edge[:], 0.0, None, ALU.is_equal))
                            link(nc.vector.scalar_tensor_tensor(out=weight[:], in0=match[:],
                                                                scalar=NO_EDGE, in1=weight[:],
                                                                op0=ALU.mult, op1=ALU.add))
                            nc.vector.tensor_reduce(neg_max[:], weight[:], axis=AX.X, op=ALU.max,
                                                    negate=True).then_inc(weight_done, 1)
                            dve.wait_ge(product_done, HEADS * n + h + 2)
                            link(nc.vector.reciprocal(inv_sum[:], row_sum[:]))
                            nc.vector.tensor_scalar(o[:, h * HEAD_DIM:(h + 1) * HEAD_DIM],
                                                    o_ps[:, 0:HEAD_DIM], inv_sum[:], None, ALU.mult
                                                    ).then_inc(head_done, 1)
                        dve.wait_ge(head_done, HEADS * (n + 1) + 1)
                        link(nc.vector.tensor_tensor(o[:], o[:], bias_b[:], ALU.add))
                        link(nc.vector.scalar_tensor_tensor(out=o[:], in0=o[:], scalar=0.0, in1=h_own[:],
                                                            op0=ALU.max, op1=ALU.add))
                        link(nc.vector.tensor_reduce(hstat[:, 0, :], by_head(o), axis=AX.X, op=ALU.add))
                        link(nc.vector.scalar_tensor_tensor(
                            out=by_head(o), in0=over_head(hstat[:, 0, :]), scalar=-1.0 / HEAD_DIM,
                            in1=by_head(o), op0=ALU.mult, op1=ALU.add))
                        link(nc.vector.tensor_tensor(sq[:], o[:], o[:], ALU.mult))
                        nc.vector.tensor_reduce(hstat[:, 1, :], by_head(sq), axis=AX.X, op=ALU.add
                                                ).then_inc(var_done, 1)
                        dve.wait_ge(dev_done, n + 1)
                        link(nc.vector.reciprocal(hstat[:, 3, :], hstat[:, 2, :]))
                        link(nc.vector.tensor_tensor(by_head(o), by_head(o), over_head(hstat[:, 3, :]),
                                                     ALU.mult))
                        link(nc.vector.tensor_tensor(o[:], o[:], gamma_b[:], ALU.mult))
                        link(nc.vector.tensor_tensor(o[:], o[:], beta_b[:], ALU.add))
                        nc.vector.tensor_tensor(o[:], o[:], x_own[:], ALU.add).then_inc(y_done, 1)
                        assert links[0] == HEADS * CHAIN + TAIL
                dve.nop()


_INS = ("x", "adj", "L0_gnn_W", "L0_gnn_a_src", "L0_gnn_a_dst", "L0_gnn_bias", "L0_gnn_ln_gamma",
        "L0_gnn_ln_beta")


def kernel(**inputs):
    import numpy as _np
    import concourse.bacc as _bacc
    from concourse import mybir as _mybir
    from concourse.bass_utils import run_bass_kernel_spmd as _run

    nc = _bacc.Bacc("TRN2", target_bir_lowering=False, num_devices=1, dynamic_dma_scratch_size=1024)
    arrays, args = {}, []
    for name in _INS:
        a = _np.ascontiguousarray(inputs[name])
        arrays[name + "_dram"] = a
        args.append(nc.dram_tensor(name + "_dram", a.shape, _mybir.dt.from_np(a.dtype),
                                   kind="ExternalInput").ap())
    shape = inputs["x"].shape
    args.append(nc.dram_tensor("out_dram", shape, _mybir.dt.float32, kind="ExternalOutput").ap())
    build(nc, *args)
    return _run(nc, [arrays], core_ids=[0]).results[0]["out_dram"]
```

```python
from contextlib import ExitStack

import concourse.bass as bass
from concourse import mybir

P = 128
HEADS, HEAD_DIM, TYPES = 4, 64, 5
DIM = HEADS * HEAD_DIM
KC = DIM // P
AUG = HEAD_DIM + 1
PROJ = 2 * HEADS * TYPES
SRC, DST = 0, HEADS * TYPES
GCOLS = HEADS * 4 * AUG
UNIT_TILES = 4
UNIT = UNIT_TILES * P
SCALE = 64.0
LN_EPS, HEAD_EPS = 1e-5, 1e-6
NO_EDGE = -1e9
MAX_DST, MAX_SRC, MAX_H, MIN_H = 4.0, 40.0, 16.0, 0.25

START = 24


def done(n):
    return n + START + 1


def freed(n, depth):
    return n + START + 1 - depth


def wait_apart(engine, semaphore, value, passed):
    engine.wait_ge(semaphore, value)
    engine.sem_inc(passed, 1)


F32, F16, BF16, I32 = mybir.dt.float32, mybir.dt.float16, mybir.dt.bfloat16, mybir.dt.int32
STEP = 2.0 ** 100
ALU = mybir.AluOpType
ACT = mybir.ActivationFunctionType
AX = mybir.AxisListType


def build(nc, x, adj, W, a_src, a_dst, bias, gamma, beta, out):
    batches, nodes, _ = x.shape
    tiles = nodes // P
    all_tiles = batches * tiles
    units = all_tiles // UNIT_TILES
    batch_units = tiles // UNIT_TILES
    groups = tiles // 4

    x_rows = x.rearrange("b n d -> (b n) d")
    adj_rows = adj.rearrange("b n m -> (b n) m")
    out_rows = out.rearrange("b n d -> (b n) d")
    h_dram = nc.dram_tensor("h_rows", (batches * nodes, HEADS * AUG), F32).ap()
    uv_dram = nc.dram_tensor("uv_rows", (batches * nodes, GCOLS), F16).ap()
    score_dram = nc.dram_tensor("score_rows", (batches * nodes, PROJ), F32).ap()
    scoreT_dram = nc.dram_tensor("score_cols", (PROJ, batches * nodes), F32).ap()
    hsum_dram = nc.dram_tensor("h_sum", (batches, 2 * HEADS * AUG), F16).ap()

    keep = ExitStack()
    with keep:
        def sb(stack, name, shape, dt):
            return stack.enter_context(nc.sbuf_tensor(name, shape, dt))

        def ps(stack, name, shape, dt):
            return stack.enter_context(nc.psum_tensor(name, shape, dt))

        def sem(stack, name):
            return stack.enter_context(nc.semaphore(name))

        ident16 = sb(keep, "ident16", [P, P], BF16)
        ident32 = sb(keep, "ident32", [P, P], F32)
        bias_b = sb(keep, "bias_b", [P, DIM], F32)
        gamma_b = sb(keep, "gamma_b", [P, DIM], F32)
        beta_b = sb(keep, "beta_b", [P, DIM], F32)
        rho = sb(keep, "rho", [P, all_tiles, HEADS], F32)
        neg_d = sb(keep, "neg_d", [P, batches * HEADS * tiles], F32)
        eps = sb(keep, "eps", [P, 2], F32)
        extremes = sb(keep, "extremes", [P, 3, HEADS], F32)
        degree = sb(keep, "degree", [P, all_tiles + 8], F32)
        sum_aa = sb(keep, "sum_aa", [P, 2 * UNIT_TILES], F32)
        verdict = sb(keep, "verdict", [P, 1], I32)

        edge = [sb(keep, f"edge{i}", [P, tiles * P], I32) for i in (0, 1)]
        a_row = [sb(keep, f"a_row{i}", [P, tiles, P], BF16) for i in (0, 1)]
        edge_loaded = [sem(keep, f"edge_loaded{i}") for i in (0, 1)]
        cast_done, a_turned = sem(keep, "cast_done"), sem(keep, "a_turned")
        uv0 = sb(keep, "uv0", [P, tiles, HEADS, 4 * AUG], F16)
        casts = (edge, a_row, edge_loaded, cast_done, a_turned)
        with ExitStack() as early:
            wx = sb(early, "wx", [P, KC, DIM + PROJ], F32)
            xt = [sb(early, f"xt{q}", [P, tiles, DIM], F32) for q in (0, 1)]
            stats = sb(early, "stats", [P, tiles, 6], F32)
            x_loaded = [sem(early, f"x_loaded{q}") for q in (0, 1)]
            setup_block(nc, sb, ps, sem, W, a_src, a_dst, bias, gamma, beta, wx, ident16, ident32,
                        bias_b, gamma_b, beta_b, eps, extremes, sum_aa, x_rows, xt, x_loaded,
                        stats)
            rows_block(nc, sb, ps, sem, batches, tiles, groups, x_rows, adj_rows, wx, ident32, rho,
                       neg_d, eps, extremes, h_dram, uv_dram, score_dram, scoreT_dram, hsum_dram,
                       xt, stats, x_loaded, degree, casts, uv0)
        edges_block(nc, sb, ps, sem, batches, tiles, units, batch_units, x_rows, adj_rows, out_rows,
                    h_dram, uv_dram, scoreT_dram, hsum_dram, ident16, bias_b, gamma_b, beta_b,
                    rho, neg_d, eps, degree, sum_aa, casts, uv0)
        verdict_block(nc, sb, ps, sem, all_tiles, extremes, degree, sum_aa, verdict)
        general_block(nc, sb, ps, sem, batches, tiles, all_tiles, x_rows, adj_rows, out_rows, h_dram,
                      score_dram, scoreT_dram, ident32, bias_b, gamma_b, beta_b, eps, verdict)


def setup_block(nc, sb, ps, sem, W, a_src, a_dst, bias, gamma, beta, wx, ident16, ident32,
                bias_b, gamma_b, beta_b, eps, extremes, sum_aa, x_rows, xt, x_loaded, stats):
    tiles = xt[0].shape[1]
    with ExitStack() as s:
        a_t = sb(s, "a_t", [P, HEADS // 2, PROJ], F32)
        w_t = sb(s, "w_t", [P, HEADS // 2, KC, P], F32)
        w_ps = ps(s, "w_ps", [P, HEADS // 2, KC, P], F32)
        v_ps = ps(s, "v_ps", [P, KC, 256], F32)
        loaded, broadcast = sem(s, "loaded"), sem(s, "broadcast")
        a_loaded, a_clear = sem(s, "a_loaded"), sem(s, "a_clear")
        made, transposed, w_ready = sem(s, "made"), sem(s, "transposed"), sem(s, "w_ready")
        projected = sem(s, "projected")
        with nc.Block() as block:

            @block.sync
            def _(sp):
                for h in range(HEADS):
                    sp.dma_start(wx[:, :, h * HEAD_DIM:(h + 1) * HEAD_DIM],
                                 W[h].rearrange("(k p) e -> p k e", p=P)).then_inc(loaded, 16)
                last_batch = x_rows[x_rows.shape[0] - tiles * P:, :]
                sp.dma_start(xt[0][:], last_batch.rearrange("(t p) d -> p t d", p=P)
                             ).then_inc(x_loaded[0], 16)
                sp.wait_ge(a_clear, 1)
                for first, a in ((SRC, a_src), (DST, a_dst)):
                    for h in range(HEADS):
                        row, col = (h % 2) * HEAD_DIM, first + h * TYPES
                        with nc.allow_non_contiguous_dma(reason="1280 numbers, once"):
                            sp.dma_start(a_t[row:row + HEAD_DIM, h // 2, col:col + TYPES],
                                         a[h].rearrange("t e -> e t")).then_inc(a_loaded, 16)
                for row, to in ((bias, bias_b), (gamma, gamma_b), (beta, beta_b)):
                    flat = row.rearrange("h e -> (h e)").rearrange("(o n) -> o n", o=1)
                    sp.dma_start(to[:, :], flat.to_broadcast([P, DIM])).then_inc(broadcast, 16)
                sp.wait_ge(broadcast, 48)

            @block.gpsimd
            def _(pool):
                nc.gpsimd.memset(a_t[:], 0.0).then_inc(a_clear, 1)
                nc.gpsimd.memset(eps[:, 0:1], LN_EPS)
                nc.gpsimd.memset(eps[:, 1:2], HEAD_EPS)
                nc.gpsimd.memset(extremes[:], 0.0)
                nc.gpsimd.memset(sum_aa[:], 0.0)
                nc.gpsimd.memset(ident16[:], 0.0)
                nc.gpsimd.memset(ident32[:], 0.0).then_inc(made, 1)
                pool.wait_ge(made, 1)
                for ident in (ident16, ident32):
                    nc.gpsimd.affine_select(out=ident[:], in_=ident[:], compare_op=ALU.not_equal,
                                            fill=1.0, base=0, pattern=[[-1, P]],
                                            channel_multiplier=1).then_inc(made, 1)

            @block.tensor
            def _(pe):
                pe.wait_ge(loaded, 16 * HEADS)
                pe.wait_ge(made, 3)
                for pair in range(HEADS // 2):
                    for k in range(KC):
                        last = nc.tensor.transpose(w_ps[:, pair, k, :],
                                                   wx[:, k, pair * P:(pair + 1) * P], ident32[:])
                last.then_inc(transposed, 1)
                pe.wait_ge(w_ready, 1)
                pe.wait_ge(a_loaded, 16 * 2 * HEADS)
                for k in range(KC):
                    for pair in range(HEADS // 2):
                        last = nc.tensor.matmul(v_ps[:, k, 0:PROJ], w_t[:, pair, k, :],
                                                a_t[:, pair, :], start=pair == 0,
                                                stop=pair == HEADS // 2 - 1)
                last.then_inc(projected, 1)

            @block.vector
            def _(dve):
                dve.wait_ge(transposed, 1)
                nc.vector.tensor_copy(w_t[:], w_ps[:]).then_inc(w_ready, 1)
                dve.wait_ge(x_loaded[0], 16)
                for t in range(tiles):
                    nc.vector.bn_stats(stats[:, t, :], xt[0][:, t, :])
                dve.wait_ge(projected, 1)
                nc.vector.tensor_copy(wx[:, :, DIM:DIM + PROJ], v_ps[:, :, 0:PROJ])


def rows_block(nc, sb, ps, sem, batches, tiles, groups, x_rows, adj_rows, wx, ident32, rho, neg_d,
               eps, extremes, h_dram, uv_dram, score_dram, scoreT_dram, hsum_dram, xt, stats, x_loaded,
               degree, casts, uv0):
    pairs = tiles // 2
    steps = batches // 2
    span = tiles * P
    COPY_LAG, ACROSS_LAG, EXP_LAG, HI_LAG = 4, 7, 9, 13
    PRODUCT_LAG, SCORE_LAG, SUM_LAG, UV_LAG = 1, 2, 3, 5
    edge, a_row, edge_loaded, cast_done, a_turned = casts
    WHOLES = 8
    with ExitStack() as s:
        haug = [sb(s, f"haug{q}", [P, tiles, HEADS, AUG], F32) for q in (0, 1)]
        score = [sb(s, f"score{q}", [P, tiles, PROJ], F32) for q in (0, 1)]
        scoreT = [sb(s, f"scoreT{q}", [PROJ, span], F32) for q in (0, 1)]
        mean_var = sb(s, "mean_var", [P, tiles, 2], F32)
        deviation = sb(s, "deviation", [P, tiles], F32)
        rstd = [sb(s, f"rstd{q}", [P, tiles], F32) for q in (0, 1)]
        shift = [sb(s, f"shift{q}", [P, tiles], F32) for q in (0, 1)]
        normed = [sb(s, f"normed{i}", [P, DIM], F32) for i in range(4)]
        normed_t = [sb(s, f"normed_t{i}", [P, KC, 4 * P], F32) for i in (0, 1)]
        u_exp = sb(s, "u_exp", [P, tiles, HEADS], F32)
        v_exp = sb(s, "v_exp", [P, tiles, HEADS], F32)
        whole = [sb(s, f"whole{i}", [P, HEADS, 2 * AUG], F32) for i in range(WHOLES)]
        hsum = sb(s, "hsum", [1, 2, HEADS * AUG], F16)
        pair_sum = [sb(s, f"pair_sum{q}", [P, KC, pairs], F32) for q in (0, 1)]
        batch_sum = sb(s, "batch_sum", [P, KC], F32)
        batch_max = sb(s, "batch_max", [P, 3, HEADS], F32)
        pair_max = sb(s, "pair_max", [P, pairs, HEADS], F32)
        t_ps = [ps(s, f"t_ps{i}", [P, KC, 2 * P], F32) for i in (0, 1)]
        h_ps = [ps(s, f"h_ps{i}", [P, 512], F32) for i in range(4)]
        sT_ps = ps(s, "sT_ps", [P, 4 * P], F32)
        sum_ps = ps(s, "sum_ps", [P, 512], F32)

        ones_made = sem(s, "ones_made")
        stats_done, mv_done, dev_done = sem(s, "stats_done"), sem(s, "mv_done"), sem(s, "dev_done")
        rstd_done, shift_done = sem(s, "rstd_done"), sem(s, "shift_done")
        normed_done, transposed = sem(s, "normed_done"), sem(s, "transposed")
        t_copied, h_made, h_copied = sem(s, "t_copied"), sem(s, "h_made"), sem(s, "h_copied")
        e_copied, sT_made, sT_copied = sem(s, "e_copied"), sem(s, "sT_made"), sem(s, "sT_copied")
        pairs_added, sum_made, sum_copied = (sem(s, "pairs_added"), sem(s, "sum_made"),
                                             sem(s, "sum_copied"))
        exps_done, whole_done = sem(s, "exps_done"), sem(s, "whole_done")
        hi_done, lo_done, max_done = sem(s, "hi_done"), sem(s, "lo_done"), sem(s, "max_done")
        pair_max_done = sem(s, "pair_max_done")
        rows_stored = [sem(s, f"rows_stored{q}") for q in (0, 1)]
        uv_stored = [sem(s, f"uv_stored{g}") for g in range(groups)]
        sum_stored, passed = sem(s, "sum_stored"), sem(s, "passed")
        STORES = 3

        parts = [uv0[:, 4 * g:4 * g + 4, :, :].rearrange("p t h (l e) -> p t h l e", l=2)
                 for g in range(groups)]

        def at(b):
            return batches - 1 - b

        def lagging(b, q, slot, lag, slots):
            if slot >= lag:
                return None if isinstance(b, int) and b == batches else (b, q, slot - lag)
            return None if isinstance(b, int) and b == 0 else (b - 1, 1 - q, slot - lag + slots)

        def all_batches(engine, slots_of_batch):
            for q in (0, 1):
                slots_of_batch(q, q)
            if steps > 2:
                with engine.Fori(1, steps - 1) as i:
                    for q in (0, 1):
                        slots_of_batch(2 * i + q, q)
            if steps > 1:
                for q in (0, 1):
                    slots_of_batch(batches - 2 + q, q)
            slots_of_batch(batches, 0)

        def is_at(b, last):
            return isinstance(b, int) and b == last

        with nc.Block() as block:

            @block.gpsimd
            def _(pool):
                for one in (stats_done, mv_done, dev_done, rstd_done, shift_done, normed_done,
                            transposed, t_copied, h_made, h_copied, e_copied, sT_made, sT_copied,
                            pairs_added, sum_made, sum_copied, exps_done, whole_done, hi_done, lo_done, max_done,
                            pair_max_done, cast_done, a_turned):
                    pool.sem_inc(one, START)
                for one in (*x_loaded, *rows_stored, *uv_stored, sum_stored, *edge_loaded):
                    pool.sem_inc(one, 16 * START)
                nc.gpsimd.memset(hsum[:, 0, :], float(span))
                nc.gpsimd.memset(hsum[:, 1, :], 0.0)
                for q in (0, 1):
                    last = nc.gpsimd.memset(haug[q][:, :, :, HEAD_DIM:AUG], 1.0)
                last.then_inc(ones_made, 1)

                def split_lo(b, q, t):
                    pool.wait_ge(hi_done, done(tiles * b + t))
                    nc.gpsimd.tensor_tensor(parts[t // 4][:, t % 4, :, 1, :], whole[t % WHOLES][:],
                                            parts[t // 4][:, t % 4, :, 0, :],
                                            ALU.subtract).then_inc(lo_done, 1)

                def slots(b, q):
                    for t in range(tiles):
                        at_lo = lagging(b, q, t, HI_LAG, tiles)
                        if at_lo:
                            split_lo(*at_lo)

                all_batches(pool, slots)

            @block.sync
            def _(sp):
                def load(b, q):
                    rows = x_rows[bass.ds(at(b) * span, span), :].rearrange("(t p) d -> p t d", p=P)
                    sp.dma_start(xt[q][:], rows).then_inc(x_loaded[q], 16)

                def store_uv(b, g):
                    if is_at(b, batches - 1):
                        return
                    wait_apart(sp, lo_done, done(tiles * b + 4 * g + 3), passed)
                    four = uv_dram[bass.ds(at(b) * span + g * 4 * P, 4 * P), :]
                    sp.dma_start(four.rearrange("(t p) c -> p t c", p=P),
                                 uv0[:, 4 * g:4 * g + 4, :, :].rearrange("p t h c -> p t (h c)")
                                 ).then_inc(uv_stored[g], 16)

                def store_rows(b, q):
                    rows = bass.ds(at(b) * span, span)
                    wait_apart(sp, h_copied, done(tiles * b + tiles - 1), passed)
                    sp.dma_start(h_dram[rows, :].rearrange("(t p) c -> p t c", p=P),
                                 haug[q][:].rearrange("p t h e -> p t (h e)")
                                 ).then_inc(rows_stored[q], 16)
                    wait_apart(sp, e_copied, done(tiles * b + tiles - 1), passed)
                    sp.dma_start(score_dram[rows, :].rearrange("(t p) c -> p t c", p=P),
                                 score[q][:]).then_inc(rows_stored[q], 16)
                    wait_apart(sp, sT_copied, done(groups * b + groups - 1), passed)
                    sp.dma_start(scoreT_dram[:, rows], scoreT[q][:]).then_inc(rows_stored[q], 16)

                def store_sum(b):
                    wait_apart(sp, sum_copied, done(b), passed)
                    sp.dma_start(hsum_dram[bass.ds(at(b), 1), :], hsum[:].rearrange("o l c -> o (l c)")
                                 ).then_inc(sum_stored, 16)

                def slots(b, q):
                    if not (is_at(b, batches - 1) or is_at(b, batches)):
                        wait_apart(sp, normed_done, done(tiles * b - 1), passed)
                        load(b + 1, 1 - q)
                    if is_at(b, batches):
                        for m in (0, 1):
                            load_edge_tile(sp, adj_rows, edge, edge_loaded, m, m)
                    if not is_at(b, 0):
                        store_uv(b - 1, 0)
                        store_rows(b - 1, 1 - q)
                        store_uv(b - 1, 1)
                        store_sum(b - 1)
                        for g in range(2, groups):
                            store_uv(b - 1, g)
                    if is_at(b, batches):
                        for m in (2, 3):
                            sp.wait_ge(cast_done, done(m - 2))
                            load_edge_tile(sp, adj_rows, edge, edge_loaded, m, m % 2)

                all_batches(sp, slots)
                for q in (0, 1):
                    sp.wait_ge(rows_stored[q], 16 * (START + STORES * steps))
                for g in range(groups):
                    sp.wait_ge(uv_stored[g], 16 * (START + batches - 1))
                sp.wait_ge(sum_stored, 16 * (START + batches))

            @block.scalar
            def _(act):
                def take_deviation(b):
                    act.wait_ge(mv_done, done(b))
                    act.wait_ge(rstd_done, freed(b, 1))
                    nc.scalar.activation(deviation[:], mean_var[:, :, 1], ACT.Sqrt,
                                         bias=eps[:, 0:1]).then_inc(dev_done, 1)

                def norm(b, q, t):
                    if t == 0:
                        act.wait_ge(shift_done, done(b))
                    act.wait_ge(transposed, freed(pairs * b + t // 2, 2))
                    nc.scalar.activation(normed[t % 4][:], xt[q][:, t, :], ACT.Relu,
                                         scale=rstd[q][:, t:t + 1], bias=shift[q][:, t:t + 1]
                                         ).then_inc(normed_done, 1)

                def copy_h(b, q, t):
                    if t == 0:
                        act.wait_ge(rows_stored[q], 16 * (b // 2 * STORES + START))
                    act.wait_ge(h_made, done(tiles * b + t))
                    nc.scalar.activation(
                        haug[q][:, t, :, 0:HEAD_DIM],
                        h_ps[t % 4][:, 0:DIM].rearrange("p (h e) -> p h e", h=HEADS),
                        ACT.Copy).then_inc(h_copied, 1)

                def copy_across(b, q, g):
                    if g == 0:
                        act.wait_ge(rows_stored[q], 16 * (b // 2 * STORES + START))
                    act.wait_ge(sT_made, done(groups * b + g))
                    nc.scalar.activation(scoreT[q][:, g * 4 * P:(g + 1) * 4 * P], sT_ps[0:PROJ, :],
                                         ACT.Copy).then_inc(sT_copied, 1)

                def exponentials(b, q, t):
                    act.wait_ge(e_copied, done(tiles * b + t + 3))
                    act.wait_ge(whole_done, freed(tiles * b + t + 3, tiles))
                    for first, scale, to in (
                            (DST, 1.0, u_exp[:, t:t + 4, :]), (DST, 0.01, v_exp[:, t:t + 4, :]),
                            (SRC, 0.99, rho[:, bass.ds(at(b) * tiles + t, 4), :])):
                        last = nc.scalar.activation(
                            to, score[q][:, t:t + 4, first:first + HEADS * TYPES:TYPES], ACT.Exp,
                            scale=scale)
                    last.then_inc(exps_done, 1)

                def split_hi(b, q, t):
                    if t % 4 == 0:
                        act.wait_ge(uv_stored[t // 4], 16 * (b + START))
                    act.wait_ge(whole_done, done(tiles * b + t))
                    nc.scalar.activation(parts[t // 4][:, t % 4, :, 0, :],
                                         whole[t % WHOLES][:], ACT.Copy).then_inc(hi_done, 1)

                def slots(b, q):
                    for t in range(tiles):
                        if not is_at(b, batches):
                            norm(b, q, t)
                        at_h = lagging(b, q, t, COPY_LAG, tiles)
                        if at_h:
                            copy_h(*at_h)
                        at_across = lagging(b, q, t, ACROSS_LAG, tiles)
                        if at_across and at_across[2] % 4 == 0:
                            copy_across(at_across[0], at_across[1], at_across[2] // 4)
                        at_exp = lagging(b, q, t, EXP_LAG, tiles)
                        if at_exp and at_exp[2] % 4 == 0:
                            exponentials(*at_exp)
                        at_hi = lagging(b, q, t, HI_LAG, tiles)
                        if at_hi:
                            split_hi(*at_hi)
                        if t == tiles - 3 and not (is_at(b, batches - 1) or is_at(b, batches)):
                            take_deviation(b + 1)

                take_deviation(0)
                all_batches(act, slots)
                for m in (0, 1):
                    cast_edge_tile(nc, act, edge, a_row, edge_loaded, degree, cast_done, m, m)

            @block.tensor
            def _(pe):
                def transpose_pair(b, r):
                    pe.wait_ge(normed_done, done(tiles * b + 2 * r + 1))
                    pe.wait_ge(t_copied, freed(pairs * b + r, 2))
                    for t in (0, 1):
                        for k in range(KC):
                            last = nc.tensor.transpose(
                                t_ps[r % 2][:, k, t * P:(t + 1) * P],
                                normed[(2 * r + t) % 4][:, k * P:(k + 1) * P], ident32[:])
                    last.then_inc(transposed, 1)

                def product(b, t):
                    pe.wait_ge(t_copied, done(pairs * b + t // 2))
                    pe.wait_ge(e_copied, freed(tiles * b + t, 4))
                    for k in range(KC):
                        last = nc.tensor.matmul(
                            h_ps[t % 4][:, 0:DIM + PROJ],
                            normed_t[t // 4 % 2][:, k, t % 4 * P:(t % 4 + 1) * P],
                            wx[:, k, :], start=k == 0, stop=k == KC - 1)
                    last.then_inc(h_made, 1)

                def scores_across(b, g):
                    pe.wait_ge(sT_copied, freed(groups * b + g, 1))
                    for k in range(KC):
                        last = nc.tensor.matmul(sT_ps[0:PROJ, :], wx[:, k, DIM:DIM + PROJ],
                                                normed_t[g % 2][:, k, :], start=k == 0,
                                                stop=k == KC - 1)
                    last.then_inc(sT_made, 1)

                def sum_of_h(b):
                    pe.wait_ge(pairs_added, done(b))
                    pe.wait_ge(sum_copied, freed(b, 1))
                    for k in range(KC):
                        last = nc.tensor.matmul(sum_ps[0:1, 0:DIM], batch_sum[:, k:k + 1],
                                                wx[:, k, 0:DIM], start=k == 0, stop=k == KC - 1)
                    last.then_inc(sum_made, 1)

                def slots(b, q):
                    for r in range(pairs):
                        if not is_at(b, batches):
                            transpose_pair(b, r)
                        at_h = lagging(b, q, r, PRODUCT_LAG, pairs)
                        if at_h:
                            for t in (2 * at_h[2], 2 * at_h[2] + 1):
                                product(at_h[0], t)
                            if at_h[2] % 2 == 1:
                                scores_across(at_h[0], at_h[2] // 2)
                        if r == SUM_LAG and not is_at(b, 0):
                            sum_of_h(b - 1)

                all_batches(pe, slots)

            @block.vector
            def _(dve):
                def take_stats(b, q, t):
                    if t == 0:
                        dve.wait_ge(x_loaded[q], 16 * done(b // 2))
                    for one in range(t, t + 4):
                        last = nc.vector.bn_stats(stats[:, one, :], xt[q][:, one, :])
                    last.then_inc(stats_done, 1)

                def take_mean_var(b, t):
                    wait_apart(dve, stats_done, done(groups * b + t // 4), passed)
                    for one in range(t, t + 4):
                        last = nc.vector.bn_aggr(mean_var[:, one, :], stats[:, one, :])
                    if t == tiles - 4:
                        last.then_inc(mv_done, 1)

                def invert_deviation(b, q):
                    dve.wait_ge(dev_done, done(b))
                    dve.wait_ge(normed_done, freed(tiles * b, tiles + 1))
                    nc.vector.reciprocal(rstd[q][:], deviation[:]).then_inc(rstd_done, 1)

                def take_shift(b, q):
                    dve.wait_ge(rstd_done, done(b))
                    nc.vector.scalar_tensor_tensor(
                        out=shift[q][:], in0=mean_var[:, :, 0], scalar=-1.0, in1=rstd[q][:],
                        op0=ALU.mult, op1=ALU.mult).then_inc(shift_done, 1)

                def copy_transposed(b, q, r):
                    g = r // 2
                    dve.wait_ge(transposed, done(pairs * b + r))
                    dve.wait_ge(sT_made, freed(groups * b + g, 2))
                    if r == 0:
                        dve.wait_ge(pairs_added, freed(b, 2))
                    for k in range(KC):
                        last = nc.vector.tensor_scalar(
                            normed_t[g % 2][:, k, r % 2 * 2 * P:(r % 2 + 1) * 2 * P],
                            t_ps[r % 2][:, k, :], 1.0, None, ALU.mult, ALU.add,
                            accum_out=pair_sum[q][:, k, r:r + 1])
                    last.then_inc(t_copied, 1)

                def add_pairs(b, q):
                    wait_apart(dve, t_copied, done(pairs * b + pairs - 1), passed)
                    nc.vector.tensor_reduce(batch_sum[:], pair_sum[q][:], axis=AX.X, op=ALU.add
                                            ).then_inc(pairs_added, 1)

                def copy_score(b, q, t):
                    if t == 0:
                        dve.wait_ge(rows_stored[q], 16 * (b // 2 * STORES + START))
                    dve.wait_ge(h_copied, done(tiles * b + t))
                    nc.vector.tensor_copy(score[q][:, t, :], h_ps[t % 4][:, DIM:DIM + PROJ]
                                          ).then_inc(e_copied, 1)

                def make_uv(b, q, t):
                    if is_at(b, 0) and t == 0:
                        dve.wait_ge(ones_made, 1)
                    if t % 4 == 0:
                        dve.wait_ge(exps_done, done(groups * b + t // 4))
                    dve.wait_ge(lo_done, freed(tiles * b + t, WHOLES))
                    for n, factor in ((0, u_exp), (1, v_exp)):
                        last = nc.vector.scalar_tensor_tensor(
                            out=whole[t % WHOLES][:, :, n * AUG:(n + 1) * AUG], in0=haug[q][:, t, :, :],
                            scalar=SCALE, in1=factor[:, t, :].unsqueeze(2).to_broadcast([P, HEADS, AUG]),
                            op0=ALU.mult, op1=ALU.mult)
                    last.then_inc(whole_done, 1)

                def take_pair_max(b, q, r):
                    dve.wait_ge(h_copied, done(tiles * b + 2 * r + 1))
                    if r == 0:
                        dve.wait_ge(max_done, done(3 * b - 3))
                    nc.vector.tensor_reduce(
                        pair_max[:, r, :],
                        haug[q][:, 2 * r:2 * r + 2, :, 0:HEAD_DIM].rearrange("p t h e -> p h t e"),
                        axis=AX.XY, op=ALU.max, apply_absolute_value=True).then_inc(pair_max_done, 1)

                def heads_of(row):
                    return row.rearrange("o (h e) -> o h e", h=HEADS)

                def take_sum(b):
                    dve.wait_ge(sum_made, done(b))
                    dve.wait_ge(sum_stored, 16 * (b + START))
                    nc.vector.tensor_copy(heads_of(hsum[:, 0, :])[:, :, 0:HEAD_DIM],
                                          heads_of(sum_ps[0:1, 0:DIM])).then_inc(max_done, 1)

                def take_sum_lo(b):
                    dve.wait_ge(max_done, done(3 * b + 1))
                    nc.vector.tensor_tensor(heads_of(hsum[:, 1, :])[:, :, 0:HEAD_DIM],
                                            heads_of(sum_ps[0:1, 0:DIM]),
                                            heads_of(hsum[:, 0, :])[:, :, 0:HEAD_DIM],
                                            ALU.subtract).then_inc(sum_copied, 1)

                def take_batch_max(b, q):
                    dve.wait_ge(e_copied, done(tiles * b + tiles - 1))
                    dve.wait_ge(max_done, done(3 * b - 1))
                    wait_apart(dve, pair_max_done, done(pairs * b + pairs - 1), passed)
                    nc.vector.tensor_scalar(
                        neg_d[:, bass.ds(at(b) * (HEADS * tiles), HEADS * tiles)].rearrange(
                            "p (h t) -> p h t", h=HEADS),
                        score[q][:, :, DST:DST + HEADS * TYPES:TYPES].rearrange("p t h -> p h t"),
                        -1.0, None, ALU.mult)
                    nc.vector.tensor_reduce(
                        batch_max[:, 0, :], pair_max[:].rearrange("p r h -> p h r"), axis=AX.X, op=ALU.max)
                    for n, first in ((1, DST), (2, SRC)):
                        last = nc.vector.tensor_reduce(
                            batch_max[:, n, :],
                            score[q][:, :, first:first + HEADS * TYPES:TYPES].rearrange("p t h -> p h t"),
                            axis=AX.X, op=ALU.max, apply_absolute_value=True)
                    last.then_inc(max_done, 1)

                def take_extremes(b):
                    dve.wait_ge(max_done, done(3 * b))
                    nc.vector.tensor_tensor(extremes[:], extremes[:], batch_max[:], ALU.max
                                            ).then_inc(max_done, 1)

                def slots(b, q):
                    inside = not is_at(b, batches)
                    next_too = inside and not is_at(b, batches - 1)
                    for r in range(pairs):
                        if inside:
                            copy_transposed(b, q, r)
                        if r == 0 and not is_at(b, 0):
                            add_pairs(b - 1, 1 - q)
                        if r == SUM_LAG + 1 and not is_at(b, 0):
                            take_sum(b - 1)
                        at_score = lagging(b, q, r, SCORE_LAG, pairs)
                        if at_score:
                            for t in (2 * at_score[2], 2 * at_score[2] + 1):
                                copy_score(at_score[0], at_score[1], t)
                        if r == SUM_LAG and not is_at(b, 0):
                            take_batch_max(b - 1, 1 - q)
                        at_max = lagging(b, q, r, SUM_LAG, pairs)
                        if at_max:
                            take_pair_max(*at_max)
                        at_uv = lagging(b, q, r, UV_LAG, pairs)
                        if at_uv:
                            for t in (2 * at_uv[2], 2 * at_uv[2] + 1):
                                make_uv(at_uv[0], at_uv[1], t)
                        if r == SUM_LAG + 1 and not is_at(b, 0):
                            take_extremes(b - 1)
                            take_sum_lo(b - 1)
                        if next_too:
                            for g in range(groups):
                                if r == min(g + 2, 4):
                                    take_stats(b + 1, 1 - q, 4 * g)
                                if r == min(g + 3, 5):
                                    take_mean_var(b + 1, 4 * g)
                            if r == pairs - 1:
                                invert_deviation(b + 1, 1 - q)
                    if next_too:
                        take_shift(b + 1, 1 - q)

                dve.sem_inc(stats_done, groups)
                for g in range(groups):
                    take_mean_var(0, 4 * g)
                invert_deviation(0, 0)
                take_shift(0, 0)
                all_batches(dve, slots)


def load_edge_tile(sp, adj_rows, edge, edge_loaded, m, slot):
    sp.dma_start(edge[slot][:], adj_rows[bass.ds(m * P, P), :]).then_inc(edge_loaded[slot], 16)


def cast_edge_tile(nc, act, edge, a_row, edge_loaded, degree, cast_done, m, slot):
    act.wait_ge(edge_loaded[slot], 16 * done(m // 2))
    nc.scalar.activation(a_row[slot][:].rearrange("p t c -> p (t c)"), edge[slot][:], ACT.Copy,
                         accum_out=degree[:, bass.ds(m, 1)]).then_inc(cast_done, 1)


def edges_block(nc, sb, ps, sem, batches, tiles, units, batch_units, x_rows, adj_rows, out_rows,
                h_dram, uv_dram, scoreT_dram, hsum_dram, ident16, bias_b, gamma_b, beta_b,
                rho, neg_d, eps, degree, sum_aa, casts, uv0):
    all_tiles = UNIT_TILES * units
    passes = all_tiles
    chunks = tiles // 4
    by_act = (1, 3)
    T_AHEAD, AV_AHEAD, CAST_AHEAD = 5, 3, 6
    half_tiles = tiles // 2
    body = 2 * UNIT_TILES
    edge, a_row, edge_loaded, cast_done, a_turned = casts
    with ExitStack() as s:
        at = [sb(s, f"at{i}", [P, tiles, UNIT], BF16) for i in (0, 1)]
        mask = [sb(s, f"mask{i}", [P, tiles, UNIT], BF16) for i in (0, 1)]
        step = [sb(s, f"step{i}", [P, 4, UNIT], BF16) for i in range(len(by_act))]
        uv = [uv0, sb(s, "uv1", [P, tiles, HEADS, 4 * AUG], F16)]
        hsum = sb(s, "hsum_b", [P, 2 * 2 * HEADS * AUG], F16)
        s_row = sb(s, "s_row", [P, HEADS, UNIT], F32)
        h_own = [sb(s, f"h_own{i}", [P, UNIT_TILES, HEADS * AUG], F32) for i in (0, 1)]
        y = [sb(s, f"y{i}", [P, UNIT_TILES, DIM], F32) for i in (0, 1)]
        seg = [sb(s, f"seg{i}", [P, UNIT_TILES, 4 * AUG], F32) for i in (0, 1)]
        av = [sb(s, f"av{i}", [P, UNIT_TILES, HEADS, AUG], F32) for i in (0, 1)]
        both = sb(s, "both", [P, UNIT_TILES, 2 * AUG], F32)
        num = sb(s, "num", [P, UNIT_TILES, AUG], F32)
        v_part = sb(s, "v_part", [P, UNIT_TILES, AUG], F32)
        rden = sb(s, "rden", [P, UNIT_TILES], F32)
        o = [sb(s, f"o{i}", [P, UNIT_TILES, HEAD_DIM], F32) for i in (0, 1)]
        sq = sb(s, "sq", [P, UNIT_TILES, HEAD_DIM], F32)
        stat = sb(s, "stat", [P, 4, UNIT_TILES], F32)
        squares = [sb(s, f"squares{i}", [P, 2 * UNIT_TILES], F32) for i in (0, 1)]
        neg_now = [sb(s, f"neg_now{i}", [P, HEADS * tiles], F32) for i in (0, 1)]
        step_now = [sb(s, f"step_now{i}", [P, HEADS * tiles], F32) for i in (0, 1)]
        neg_degree = [sb(s, f"neg_degree{i}", [P, 1], F32) for i in (0, 1)]
        lone = [sb(s, f"lone{i}", [P, P], BF16) for i in (0, 1)]
        scaled = sb(s, "scaled", [P, UNIT_TILES, HEAD_DIM], F32)
        m_ps = [ps(s, f"m_ps{i}", [P, 2, 512], F32) for i in (0, 1)]
        a_ps = [ps(s, f"a_ps{i}", [P, half_tiles, P], BF16) for i in (0, 1)]
        av_ps = [ps(s, f"av_ps{i}", [P, 512], F32) for i in (0, 1)]

        own_loaded = [sem(s, f"own_loaded{i}") for i in (0, 1)]
        s_loaded = [sem(s, f"s_loaded{h}") for h in range(HEADS)]
        y_stored = [sem(s, f"y_stored{i}") for i in (0, 1)]
        uv_loaded, passed = sem(s, "uv_loaded"), sem(s, "passed")
        at_done, unit_ready, degree_done = (sem(s, "at_done"), sem(s, "unit_ready"),
                                            sem(s, "degree_done"))
        lone_done, av_made, av_copied = sem(s, "lone_done"), sem(s, "av_made"), sem(s, "av_copied")
        step_done, masks_done = sem(s, "step_done"), sem(s, "masks_done")
        m_made, chunk_used, m_copied = sem(s, "m_made"), sem(s, "chunk_used"), sem(s, "m_copied")
        fin_step, folded, av_used = sem(s, "fin_step"), sem(s, "folded"), sem(s, "av_used")
        h_used, centred, squared = sem(s, "h_used"), sem(s, "centred"), sem(s, "squared")
        var_done, dev_done = sem(s, "var_done"), sem(s, "dev_done")
        rstd_done, scale_done, gamma_done = (sem(s, "rstd_done"), sem(s, "scale_done"),
                                             sem(s, "gamma_done"))
        y_based, y_done = sem(s, "y_based"), sem(s, "y_done")

        def over(t, n=HEAD_DIM):
            return t.unsqueeze(2).to_broadcast([P, UNIT_TILES, n])

        def row_of_head(row, h):
            cols = row[:, h * HEAD_DIM:(h + 1) * HEAD_DIM]
            return cols.unsqueeze(1).to_broadcast([P, UNIT_TILES, HEAD_DIM])

        with nc.Block() as block:

            @block.gpsimd
            def _(pool):
                for one in (at_done, unit_ready, degree_done, lone_done, av_made,
                            av_copied, step_done, masks_done, m_made, chunk_used, m_copied, folded,
                            av_used, h_used, centred, squared, var_done, dev_done, y_based, y_done,
                            rstd_done, scale_done, gamma_done):
                    pool.sem_inc(one, START)
                for one in (*own_loaded, *s_loaded, *y_stored, uv_loaded):
                    pool.sem_inc(one, 16 * START)

                def add_beta(k, q):
                    pool.wait_ge(own_loaded[q], 16 * (2 * (k // 2) + 2 + START))
                    nc.gpsimd.tensor_tensor(y[q][:], y[q][:],
                                            beta_b[:].unsqueeze(1).to_broadcast([P, UNIT_TILES, DIM]),
                                            ALU.add).then_inc(y_based, 1)

                def take_v_part(g, i):
                    h, q = i % HEADS, i // HEADS % 2
                    if h == 0:
                        pool.wait_ge(av_copied, done(g + UNIT_TILES - 1))
                    pool.wait_ge(folded, done(g))
                    nc.gpsimd.tensor_tensor(v_part[:], av[q][:, :, h, :], both[:, :, AUG:2 * AUG],
                                            ALU.subtract).then_inc(av_used, 1)

                def square(g, i):
                    pool.wait_ge(centred, done(g))
                    nc.gpsimd.tensor_tensor(sq[:], o[i % 2][:], o[i % 2][:], ALU.mult).then_inc(squared, 1)

                def add_to_y(g, i):
                    h, q = i % HEADS, i // HEADS % 2
                    pool.wait_ge(scale_done, done(g))
                    nc.gpsimd.tensor_tensor(scaled[:], scaled[:], row_of_head(gamma_b, h), ALU.mult
                                            ).then_inc(gamma_done, 1)
                    pool.wait_ge(gamma_done, done(g))
                    if h == 0:
                        pool.wait_ge(y_based, done(g // HEADS))
                    cols = y[q][:, :, h * HEAD_DIM:(h + 1) * HEAD_DIM]
                    nc.gpsimd.tensor_tensor(cols, cols, scaled[:], ALU.add).then_inc(y_done, 1)

                def turn(g, i, first):
                    take_v_part(g, i)
                    if i % HEADS == 0:
                        add_beta(g // HEADS, i // HEADS % 2)
                    square(g, i)
                    if not first:
                        add_to_y(g - 1, i - 1)

                for i in range(body):
                    turn(i, i, i == 0)
                with pool.Fori(1, passes // body) as r:
                    for i in range(body):
                        turn(r * body + i, i, False)
                add_to_y(passes - 1, body - 1)

            @block.sync
            def _(sp):
                def load_scores(unit, h):
                    row = SRC + h * TYPES
                    cols = bass.ds(unit % units * UNIT, UNIT)
                    sp.dma_start(s_row[:, h, :], scoreT_dram[row:row + 1, cols].to_broadcast([P, UNIT])
                                 ).then_inc(s_loaded[h], 16)

                def load_sums(g, q, part):
                    width = 2 * HEADS * AUG // batch_units
                    row = hsum_dram[bass.ds(g // batch_units % batches, 1), part * width:(part + 1) * width]
                    first = (q * batch_units + part) * width
                    sp.dma_start(hsum[:, first:first + width], row.to_broadcast([P, width])
                                 ).then_inc(uv_loaded, 16)

                def load_uv(g, q, part):
                    at = (g - batch_units) % (units - batch_units) + batch_units
                    rows = uv_dram[bass.ds(at * UNIT, UNIT), :]
                    sp.dma_start(uv[q][:, part * UNIT_TILES:(part + 1) * UNIT_TILES, :, :].rearrange(
                        "p t h c -> p t (h c)"),
                        rows.rearrange("(t p) c -> p t c", p=P)).then_inc(uv_loaded, 16)

                def unit_rows(dram, k):
                    return dram[bass.ds(k * UNIT, UNIT), :].rearrange("(t p) d -> p t d", p=P)

                def store(k, q):
                    sp.wait_ge(y_done, done(HEADS * k + HEADS - 1))
                    sp.dma_start(unit_rows(out_rows, k), y[q][:]).then_inc(y_stored[q], 16)

                def unit(k, u, first):
                    q = u % 2
                    sp.wait_ge(m_made, done(2 * (k // batch_units * tiles) - 1))
                    wait_apart(sp, uv_loaded, 16 * (2 * (k + batch_units) + START), passed)
                    load_uv(k + batch_units, 1 - u // batch_units, u % batch_units)
                    load_sums(k + batch_units, 1 - u // batch_units, u % batch_units)
                    sp.wait_ge(h_used, freed(HEADS * k, HEADS + 1))
                    sp.dma_start(h_own[q][:], unit_rows(h_dram, k)).then_inc(own_loaded[q], 16)
                    sp.wait_ge(y_stored[q], 16 * (k // 2 + START))
                    sp.dma_start(y[q][:], unit_rows(x_rows, k)).then_inc(own_loaded[q], 16)
                    for h in range(HEADS):
                        p = HEADS * k + h
                        wait_apart(sp, masks_done, done(chunks * p - 1), passed)
                        load_scores(k + (h + 3) // HEADS, (h + 3) % HEADS)
                        sp.wait_ge(cast_done, done(p + CAST_AHEAD - 1))
                        load_edge_tile(sp, adj_rows, edge, edge_loaded, (p + CAST_AHEAD + 1) % all_tiles,
                                       (h + CAST_AHEAD + 1) % 2)
                        if h == 3 and not first:
                            store(k - 1, 1 - q)

                for h in range(3):
                    load_scores(0, h)
                for part in range(batch_units):
                    load_sums(0, 0, part)
                    sp.sem_inc(uv_loaded, 16)
                for m in range(4, CAST_AHEAD + 1):
                    sp.wait_ge(cast_done, done(m - 2))
                    load_edge_tile(sp, adj_rows, edge, edge_loaded, m, m % 2)
                for u in range(2 * batch_units):
                    unit(u, u, u == 0)
                if batches > 2:
                    with sp.Fori(1, batches // 2) as i:
                        for u in range(2 * batch_units):
                            unit(2 * batch_units * i + u, u, False)
                store(units - 1, 1)
                for q in (0, 1):
                    sp.wait_ge(y_stored[q], 16 * (START + units // 2))

            @block.scalar
            def _(act):
                def cast(m, slot):
                    act.wait_ge(a_turned, freed(2 * m + 1, 4))
                    cast_edge_tile(nc, act, edge, a_row, edge_loaded, degree, cast_done, m, slot)

                def take_at(m, parity, it, half):
                    if it == 0 and half == 0:
                        act.wait_ge(masks_done, freed(chunks * m, chunks * HEADS + 1))
                    act.wait_ge(a_turned, done(2 * m + half))
                    nc.scalar.activation(
                        at[parity][:, half_tiles * half:half_tiles * (half + 1), it * P:(it + 1) * P],
                        a_ps[half][:], ACT.Square,
                        accum_out=squares[parity][:, 2 * it + half:2 * it + half + 1]
                    ).then_inc(at_done, 1)

                def mark_lone(n, slot):
                    act.wait_ge(degree_done, done(n))
                    act.wait_ge(av_made, freed(n, 2))
                    nc.scalar.activation(lone[slot][:], ident16[:], ACT.Relu, bias=neg_degree[slot][:]
                                         ).then_inc(lone_done, 1)

                def take_av(n, parity, it):
                    if it == 0:
                        act.wait_ge(av_used, freed(n, HEADS + 1))
                    act.wait_ge(av_made, done(n))
                    nc.scalar.activation(av[parity][:, it, :, :].rearrange("p h e -> p (h e)"),
                                         av_ps[it % 2][:, 0:HEADS * AUG], ACT.Copy
                                         ).then_inc(av_copied, 1)

                def compare(p, parity, h, c):
                    slot = by_act.index(c)
                    if slot == 0:
                        act.wait_ge(s_loaded[h], 16 * done(p // HEADS))
                        act.wait_ge(unit_ready, done(p // HEADS))
                    act.wait_ge(masks_done, freed(chunks * p + c, chunks))
                    for j in range(4):
                        col = h * tiles + 4 * c + j
                        last = nc.scalar.activation(step[slot][:, j, :], s_row[:, h, :], ACT.Relu,
                                                    scale=STEP, bias=step_now[parity][:, col:col + 1])
                    last.then_inc(step_done, 1)

                def take_products(p, h, pair):
                    act.wait_ge(m_made, done(2 * p + pair))
                    if pair == 0:
                        act.wait_ge(folded, freed(p, 2))
                    nc.scalar.activation(seg[h % 2][:, 2 * pair:2 * pair + 2, :],
                                         m_ps[pair][:, :, 0:4 * AUG], ACT.Copy).then_inc(m_copied, 1)

                def head_deviation(g):
                    act.wait_ge(var_done, done(g))
                    nc.scalar.activation(stat[:, 2, :], stat[:, 1, :], ACT.Sqrt, bias=eps[:, 1:2],
                                         scale=1.0 / HEAD_DIM).then_inc(dev_done, 1)

                def turn(p, i, first, last):
                    h = i % HEADS
                    m, n = i + T_AHEAD, i + AV_AHEAD
                    ahead = (p + 1, (i + 1) // HEADS % 2, (i + 1) % HEADS)
                    if not last:
                        compare(*ahead, by_act[0])
                    cast(p + CAST_AHEAD, (i + CAST_AHEAD) % 2)
                    take_products(p, h, 0)
                    take_av(p + AV_AHEAD, n // UNIT_TILES % 2, n % UNIT_TILES)
                    mark_lone(p + AV_AHEAD + 1, (n + 1) % 2)
                    if not first:
                        head_deviation(p - 2)
                    if not last:
                        compare(*ahead, by_act[1])
                    take_at(p + T_AHEAD, m // UNIT_TILES % 2, m % UNIT_TILES, 0)
                    take_products(p, h, 1)
                    take_at(p + T_AHEAD, m // UNIT_TILES % 2, m % UNIT_TILES, 1)

                for n in (0, 1):
                    mark_lone(n, n)
                for m in range(UNIT_TILES):
                    for half in (0, 1):
                        take_at(m, 0, m, half)
                    if m < 2:
                        cast(m + 2, m % 2)
                for c in by_act:
                    compare(0, 0, 0, c)
                for n in range(AV_AHEAD):
                    take_av(n, 0, n)
                    if n + 2 <= AV_AHEAD:
                        mark_lone(n + 2, n % 2)
                        cast(n + 4, n % 2)
                for half in (0, 1):
                    take_at(4, 1, 0, half)
                for i in range(body):
                    turn(i, i, i < 2, False)
                if passes > 2 * body:
                    with act.Fori(1, passes // body - 1) as r:
                        for i in range(body):
                            turn(r * body + i, i, False, False)
                for i in range(body):
                    turn(passes - body + i, i, False, i == body - 1)
                head_deviation(passes - 2)
                head_deviation(passes - 1)

            @block.tensor
            def _(pe):
                def transpose(m, i, half):
                    if half == 0:
                        pe.wait_ge(cast_done, done(m))
                    pe.wait_ge(at_done, freed(2 * m + half, 2))
                    for j in range(half_tiles):
                        last = nc.tensor.transpose(a_ps[half][:, j, :],
                                                   a_row[i % 2][:, half_tiles * half + j, :], ident16[:])
                    last.then_inc(a_turned, 1)

                def multiply_a(n, i, q, c):
                    parity, it = i // UNIT_TILES % 2, i % UNIT_TILES
                    out = av_ps[it % 2][:, 0:HEADS * AUG]
                    if c == 0:
                        pe.wait_ge(av_copied, freed(n, 2))
                        pe.wait_ge(at_done, done(2 * n + 1))
                    for j in range(4 * c, 4 * c + 4):
                        for part in (0, 1):
                            v = slice((2 * part + 1) * AUG, (2 * part + 2) * AUG)
                            nc.tensor.matmul(out, at[parity][:, j, it * P:(it + 1) * P],
                                             uv[q][:, j, :, v], start=j == 0 and part == 0,
                                             stop=False)
                    if c == chunks - 1:
                        pe.wait_ge(lone_done, done(n))
                        for part in (0, 1):
                            first = (2 * q + part) * HEADS * AUG
                            last = nc.tensor.matmul(out, lone[it % 2][:], hsum[:, first:first + HEADS * AUG],
                                                    start=False, stop=part == 1)
                        last.then_inc(av_made, 1)

                def multiply_m(p, i, pair, q, c):
                    h = i % HEADS
                    if c == 0:
                        pe.wait_ge(m_copied, freed(2 * p + pair, 2))
                    if pair == 0:
                        pe.wait_ge(masks_done, done(chunks * p + c))
                    for it in (2 * pair, 2 * pair + 1):
                        for j in range(4 * c, 4 * c + 4):
                            last = nc.tensor.matmul(m_ps[pair][:, it % 2, 0:4 * AUG],
                                                    mask[i % 2][:, j, it * P:(it + 1) * P],
                                                    uv[q][:, j, h, :], start=j == 0,
                                                    stop=j == tiles - 1)
                    if c == chunks - 1:
                        last.then_inc(m_made, 1)
                    elif pair == 1:
                        last.then_inc(chunk_used, 1)

                for m in range(UNIT_TILES):
                    for half in (0, 1):
                        transpose(m, m, half)
                pe.wait_ge(uv_loaded, 16 * (2 * batch_units + START))
                for n in range(AV_AHEAD):
                    for c in range(chunks):
                        multiply_a(n, n, 0, c)
                for half in (0, 1):
                    transpose(UNIT_TILES, UNIT_TILES, half)
                with pe.Fori(0, batches // 2) as r:
                    for i in range(2 * tiles):
                        p = 2 * tiles * r + i
                        q = i // tiles
                        q_ahead = (i + AV_AHEAD) // tiles % 2
                        if (i + AV_AHEAD) % tiles == 0:
                            pe.wait_ge(uv_loaded, 16 * (2 * batch_units * (2 * r + q + 2) + START))
                        for c in range(chunks):
                            multiply_m(p, i, 0, q, c)
                            multiply_a(p + AV_AHEAD, i + AV_AHEAD, q_ahead, c)
                        for c in range(chunks):
                            multiply_m(p, i, 1, q, c)
                            if c % 2 == 0:
                                transpose(p + T_AHEAD, i + T_AHEAD, c // 2)

            @block.vector
            def _(dve):
                def prepare_unit(k, parity):
                    now = neg_d[:, bass.ds(k % units // batch_units * (HEADS * tiles), HEADS * tiles)]
                    nc.vector.tensor_copy(neg_now[parity][:], now)
                    nc.vector.tensor_scalar(step_now[parity][:], now, -STEP, None, ALU.mult
                                            ).then_inc(unit_ready, 1)

                STEPS = 6

                def own(g, steps):
                    dve.wait_ge(fin_step, STEPS * g + steps)

                def fold_parts(g, i):
                    dve.wait_ge(m_copied, done(2 * g + 1))
                    nc.vector.tensor_tensor(both[:], seg[i % 2][:, :, 0:2 * AUG],
                                            seg[i % 2][:, :, 2 * AUG:4 * AUG], ALU.add
                                            ).then_inc(folded, 1)

                def times_rho(g, i):
                    dve.wait_ge(folded, done(g))
                    rows = rho[:, bass.ds(g // HEADS * UNIT_TILES, UNIT_TILES), i % HEADS]
                    nc.vector.tensor_tensor(num[:], both[:, :, 0:AUG], over(rows, AUG), ALU.mult
                                            ).then_inc(fin_step, 1)

                def add_v_part(g):
                    own(g, 1)
                    dve.wait_ge(av_used, done(g))
                    nc.vector.tensor_tensor(num[:], num[:], v_part[:], ALU.add).then_inc(fin_step, 1)

                def divide(g, i):
                    own(g, 2)
                    nc.vector.reciprocal(rden[:], num[:, :, HEAD_DIM]).then_inc(fin_step, 1)
                    own(g, 3)
                    dve.wait_ge(scale_done, done(g - 2))
                    nc.vector.tensor_tensor(o[i % 2][:], num[:, :, 0:HEAD_DIM], over(rden[:]), ALU.mult
                                            ).then_inc(fin_step, 1)

                def add_bias(g, i):
                    own(g, 4)
                    nc.vector.tensor_tensor(o[i % 2][:], o[i % 2][:], row_of_head(bias_b, i % HEADS),
                                            ALU.add).then_inc(fin_step, 1)

                def relu_add_h(g, i):
                    h, parity = i % HEADS, i // HEADS % 2
                    own(g, 5)
                    if h == 0:
                        dve.wait_ge(own_loaded[parity], 16 * (2 * (g // body) + 2 + START))
                    nc.vector.scalar_tensor_tensor(
                        out=o[i % 2][:], in0=o[i % 2][:], scalar=0.0,
                        in1=h_own[parity][:, :, h * AUG:h * AUG + HEAD_DIM],
                        op0=ALU.max, op1=ALU.add).then_inc(h_used, 1)

                def head_sum(g, i):
                    dve.wait_ge(h_used, done(g))
                    nc.vector.tensor_reduce(stat[:, 0, :], o[i % 2][:], axis=AX.X, op=ALU.add
                                            ).then_inc(fin_step, 1)

                def centre(g, i):
                    own(g, 6)
                    nc.vector.scalar_tensor_tensor(out=o[i % 2][:], in0=over(stat[:, 0, :]),
                                                   scalar=1.0 / HEAD_DIM, in1=o[i % 2][:],
                                                   op0=ALU.mult, op1=ALU.subtract).then_inc(centred, 1)

                def variance(g):
                    dve.wait_ge(squared, done(g))
                    nc.vector.tensor_reduce(stat[:, 1, :], sq[:], axis=AX.X, op=ALU.add
                                            ).then_inc(var_done, 1)

                def invert_deviation(g):
                    dve.wait_ge(dev_done, done(g))
                    nc.vector.reciprocal(stat[:, 3, :], stat[:, 2, :]).then_inc(rstd_done, 1)

                def scale(g, i):
                    dve.wait_ge(rstd_done, done(g))
                    dve.wait_ge(y_done, done(g - 1))
                    nc.vector.scalar_tensor_tensor(out=scaled[:], in0=o[i % 2][:], scalar=-1.0,
                                                   in1=over(stat[:, 3, :]), op0=ALU.mult,
                                                   op1=ALU.mult).then_inc(scale_done, 1)

                def mask_free(p, c):
                    if c < chunks - 1:
                        dve.wait_ge(chunk_used, freed((chunks - 1) * p + c, 2 * (chunks - 1)))
                    else:
                        dve.wait_ge(m_made, freed(2 * p + 1, 4))

                def mask_tile(p, i, j):
                    h, parity = i % HEADS, i // HEADS % 2
                    if j % 4 == 0:
                        mask_free(p, j // 4)
                    if j == 0:
                        dve.wait_ge(s_loaded[h], 16 * done(p // HEADS))
                    one = nc.vector.scalar_tensor_tensor(
                        out=mask[i % 2][:, j, :], in0=s_row[:, h, :],
                        scalar=neg_now[parity][:, h * tiles + j:h * tiles + j + 1],
                        in1=at[parity][:, j, :], op0=ALU.is_gt, op1=ALU.mult)
                    if j % 4 == 3:
                        one.then_inc(masks_done, 1)

                def mask_chunk(p, i, c):
                    slot = by_act.index(c)
                    mask_free(p, c)
                    dve.wait_ge(step_done, done(len(by_act) * p + slot))
                    nc.vector.tensor_tensor(mask[i % 2][:, 4 * c:4 * c + 4, :], step[slot][:],
                                            at[i // HEADS % 2][:, 4 * c:4 * c + 4, :], ALU.min
                                            ).then_inc(masks_done, 1)

                def negate_degree(n, slot):
                    dve.wait_ge(cast_done, done(n))
                    dve.wait_ge(lone_done, freed(n, 2))
                    nc.vector.tensor_scalar(neg_degree[slot][:], degree[:, bass.ds(n, 1)], -1.0, None,
                                            ALU.mult).then_inc(degree_done, 1)

                def begin(p, i):
                    h, parity = i % HEADS, i // HEADS % 2
                    k = p // HEADS
                    if h == 2:
                        prepare_unit(k + 1, 1 - parity)
                    if h == 0:
                        dve.wait_ge(at_done, done(2 * (UNIT_TILES * k + UNIT_TILES - 1) + 1))
                        nc.vector.tensor_tensor(sum_aa[:], sum_aa[:], squares[parity][:], ALU.add)

                def first_turn(p):
                    begin(p, p)
                    for c in range(chunks):
                        if c in by_act:
                            mask_chunk(p, p, c)
                            n = 2 + len(by_act) * p + by_act.index(c)
                            negate_degree(n, n % 2)
                        else:
                            for j in range(4 * c, 4 * c + 4):
                                mask_tile(p, p, j)

                def turn(p, i, older):
                    g, ig = p - 2, i - 2
                    begin(p, i)
                    negate_degree(p + AV_AHEAD + 1, (i + AV_AHEAD + 1) % 2)
                    mask_tile(p, i, 0)
                    fold_parts(g, ig)
                    mask_tile(p, i, 1)
                    if older:
                        variance(g - 1)
                    mask_tile(p, i, 2)
                    times_rho(g, ig)
                    mask_tile(p, i, 3)
                    add_v_part(g)
                    mask_chunk(p, i, 1)
                    divide(g, ig)
                    mask_tile(p, i, 8)
                    add_bias(g, ig)
                    mask_tile(p, i, 9)
                    relu_add_h(g, ig)
                    mask_tile(p, i, 10)
                    head_sum(g, ig)
                    mask_tile(p, i, 11)
                    if older:
                        invert_deviation(g - 1)
                    mask_chunk(p, i, 3)
                    centre(g, ig)
                    if older:
                        scale(g - 1, ig - 1)

                def last_turn(g, i):
                    fold_parts(g, i)
                    variance(g - 1)
                    times_rho(g, i)
                    add_v_part(g)
                    divide(g, i)
                    add_bias(g, i)
                    relu_add_h(g, i)
                    head_sum(g, i)
                    invert_deviation(g - 1)
                    centre(g, i)
                    scale(g - 1, i - 1)

                prepare_unit(0, 0)
                dve.wait_ge(unit_ready, done(0))
                for n in (0, 1):
                    negate_degree(n, n % 2)
                for p in (0, 1):
                    first_turn(p)
                for i in range(2, body):
                    turn(i, i, i > 2)
                with dve.Fori(1, passes // body) as r:
                    for i in range(body):
                        turn(r * body + i, i, True)
                for g in (passes - 2, passes - 1):
                    last_turn(g, g % body)
                variance(passes - 1)
                invert_deviation(passes - 1)
                scale(passes - 1, body - 1)


def verdict_block(nc, sb, ps, sem, all_tiles, extremes, degree, sum_aa, verdict):
    with ExitStack() as s:
        sums = sb(s, "sums", [P, 2], F32)
        total = sb(s, "total", [P, 2], F32)
        most = sb(s, "most", [P, 3, HEADS], F32)
        good = sb(s, "good", [P, 5, HEADS], F32)
        all_good = sb(s, "all_good", [P, 1], F32)
        summed, reduced, step = sem(s, "summed"), sem(s, "reduced"), sem(s, "verdict_step")
        with nc.Block() as block:

            @block.vector
            def _(dve):
                nc.vector.tensor_reduce(sums[:, 0:1], degree[:, 0:all_tiles], axis=AX.X, op=ALU.add)
                nc.vector.tensor_reduce(sums[:, 1:2], sum_aa[:], axis=AX.X, op=ALU.add).then_inc(summed, 1)
                dve.wait_ge(reduced, 1)
                for n, bound, op in ((0, MAX_H, ALU.is_le), (1, MAX_DST, ALU.is_le),
                                     (2, MAX_SRC, ALU.is_le)):
                    nc.vector.tensor_scalar(good[:, n, :], most[:, n, :], bound, None, op)
                nc.vector.tensor_scalar(good[:, 3, :], most[:, 0, :], MIN_H, None, ALU.is_ge)
                nc.vector.tensor_tensor(good[:, 4, :], total[:, 0:1].to_broadcast([P, HEADS]),
                                        total[:, 1:2].to_broadcast([P, HEADS]), ALU.is_equal
                                        ).then_inc(step, 1)
                dve.wait_ge(step, 1)
                nc.vector.tensor_reduce(all_good[:], good[:], axis=AX.XY, op=ALU.min).then_inc(step, 1)
                dve.wait_ge(step, 2)
                nc.vector.tensor_scalar(verdict[:], all_good[:], 0.0, None, ALU.is_equal)

            @block.gpsimd
            def _(pool):
                pool.wait_ge(summed, 1)
                nc.gpsimd.partition_all_reduce(most[:].rearrange("p a h -> p (a h)"),
                                               extremes[:].rearrange("p a h -> p (a h)"), P,
                                               bass.bass_isa.ReduceOp.max)
                nc.gpsimd.partition_all_reduce(total[:], sums[:], P, bass.bass_isa.ReduceOp.add
                                               ).then_inc(reduced, 1)


def general_block(nc, sb, ps, sem, batches, tiles, all_tiles, x_rows, adj_rows, out_rows, h_dram,
                  score_dram, scoreT_dram, ident32, bias_b, gamma_b, beta_b, eps, verdict):
    span = tiles * P
    with ExitStack() as s:
        edge = sb(s, "g_edge", [P, span], I32)
        target = sb(s, "g_target", [P, TYPES, span], F32)
        match = sb(s, "g_match", [P, span], F32)
        weight = sb(s, "g_weight", [P, span], F32)
        probs_t = sb(s, "g_probs_t", [P, tiles, P], F32)
        h_head = sb(s, "g_h_head", [P, tiles, HEAD_DIM], F32)
        source = sb(s, "g_source", [P, PROJ], F32)
        h_own = sb(s, "g_h_own", [P, DIM], F32)
        x_own = sb(s, "g_x_own", [P, DIM], F32)
        neg_max = sb(s, "g_neg_max", [P, 1], F32)
        row_sum = sb(s, "g_row_sum", [P, 1], F32)
        inv_sum = sb(s, "g_inv_sum", [P, 1], F32)
        o = sb(s, "g_o", [P, DIM], F32)
        sq = sb(s, "g_sq", [P, DIM], F32)
        hstat = sb(s, "g_hstat", [P, 4, HEADS], F32)
        t_ps = ps(s, "g_t_ps", [P, tiles, P], F32)
        o_ps = ps(s, "g_o_ps", [P, 512], F32)
        own_loaded, head_loaded = sem(s, "g_own_loaded"), sem(s, "g_head_loaded")
        weight_done, probs_done = sem(s, "g_weight_done"), sem(s, "g_probs_done")
        turned, turned_copied, product_done = (sem(s, "g_turned"), sem(s, "g_turned_copied"),
                                               sem(s, "g_product_done"))
        head_done, var_done, dev_done = sem(s, "g_head_done"), sem(s, "g_var_done"), sem(s, "g_dev_done")
        y_done, y_stored, chain = sem(s, "g_y_done"), sem(s, "g_y_stored"), sem(s, "g_chain")
        OWN, HEAD = 4, 2

        def by_head(t):
            return t[:].rearrange("p (h e) -> p h e", h=HEADS)

        def over_head(t):
            return t.unsqueeze(2).to_broadcast([P, HEADS, HEAD_DIM])

        with nc.Block() as block:

            @block.sync
            def _(sp):
                wrong = sp.value_load(verdict[0:1, 0:1], min_val=0, max_val=1)
                with sp.If(wrong > 0):
                    for one in (head_done, product_done):
                        sp.sem_inc(one, 1)
                    sp.sem_inc(y_stored, 16)
                    with sp.Fori(0, all_tiles) as n:
                        rows = bass.ds(n * P, P)
                        b = n // tiles
                        sp.wait_ge(y_stored, 16 * n + 16)
                        for to, row in ((edge, adj_rows), (source, score_dram), (x_own, x_rows)):
                            sp.dma_start(to[:], row[rows, :]).then_inc(own_loaded, 16)
                        sp.dma_start(by_head(h_own), h_dram[rows, :].rearrange(
                            "p (h e) -> p h e", h=HEADS)[:, :, 0:HEAD_DIM]).then_inc(own_loaded, 16)
                        for h in range(HEADS):
                            sp.wait_ge(head_done, HEADS * n + h + 1)
                            first = DST + h * TYPES
                            sp.dma_start(target[:], scoreT_dram[first:first + TYPES,
                                                                bass.ds(b * span, span)]
                                         .rearrange("(o t) n -> o t n", o=1)
                                         .to_broadcast([P, TYPES, span])).then_inc(head_loaded, 16)
                            sp.dma_start(h_head[:],
                                         h_dram[bass.ds(b * span, span), h * AUG:h * AUG + HEAD_DIM]
                                         .rearrange("(t p) e -> p t e", p=P)).then_inc(head_loaded, 16)
                        sp.wait_ge(y_done, n + 1)
                        sp.dma_start(out_rows[rows, :], o[:]).then_inc(y_stored, 16)
                    sp.wait_ge(y_stored, 16 * all_tiles + 16)
                sp.nop()

            @block.scalar
            def _(act):
                wrong = act.value_load(verdict[0:1, 0:1], min_val=0, max_val=1)
                with act.If(wrong > 0):
                    with act.Fori(0, all_tiles) as n:
                        for h in range(HEADS):
                            act.wait_ge(weight_done, HEADS * n + h + 1)
                            nc.scalar.activation(weight[:], weight[:], ACT.Exp, bias=neg_max[:],
                                                 accum_out=row_sum[:]).then_inc(probs_done, 1)
                            act.wait_ge(turned, HEADS * n + h + 1)
                            for quarter in range(tiles // 4):
                                cols = slice(4 * quarter, 4 * quarter + 4)
                                last = nc.scalar.activation(probs_t[:, cols, :], t_ps[:, cols, :], ACT.Copy)
                            last.then_inc(turned_copied, 1)
                        act.wait_ge(var_done, n + 1)
                        nc.scalar.activation(hstat[:, 2, :], hstat[:, 1, :], ACT.Sqrt, bias=eps[:, 1:2],
                                             scale=1.0 / HEAD_DIM).then_inc(dev_done, 1)
                act.nop()

            @block.tensor
            def _(pe):
                wrong = pe.value_load(verdict[0:1, 0:1], min_val=0, max_val=1)
                with pe.If(wrong > 0):
                    with pe.Fori(0, all_tiles) as n:
                        for h in range(HEADS):
                            pe.wait_ge(probs_done, HEADS * n + h + 1)
                            for j in range(tiles):
                                last = nc.tensor.transpose(t_ps[:, j, :], weight[:, j * P:(j + 1) * P],
                                                           ident32[:])
                            last.then_inc(turned, 1)
                            pe.wait_ge(turned_copied, HEADS * n + h + 1)
                            pe.wait_ge(head_loaded, 16 * HEAD * (HEADS * n + h + 1))
                            pe.wait_ge(head_done, HEADS * n + h + 1)
                            for j in range(tiles):
                                last = nc.tensor.matmul(o_ps[:, 0:HEAD_DIM], probs_t[:, j, :],
                                                        h_head[:, j, :], start=j == 0,
                                                        stop=j == tiles - 1)
                            last.then_inc(product_done, 1)
                pe.nop()

            @block.vector
            def _(dve):
                CHAIN = 3 * TYPES + 3
                TAIL = 9
                wrong = dve.value_load(verdict[0:1, 0:1], min_val=0, max_val=1)
                with dve.If(wrong > 0):
                    with dve.Fori(0, all_tiles) as n:
                        links = [0]

                        def link(instruction):
                            links[0] += 1
                            instruction.then_inc(chain, 1)
                            dve.wait_ge(chain, (HEADS * CHAIN + TAIL) * n + links[0])

                        dve.wait_ge(own_loaded, 16 * OWN * (n + 1))
                        for h in range(HEADS):
                            dve.wait_ge(head_loaded, 16 * HEAD * (HEADS * n + h + 1))
                            for t in range(TYPES):
                                link(nc.vector.tensor_scalar(match[:], edge[:], float(t + 1), None,
                                                             ALU.is_equal))
                                col = SRC + h * TYPES + t
                                to = weight if t == 0 else target[:, t, :]
                                link(nc.vector.scalar_tensor_tensor(
                                    out=to[:] if t == 0 else to, in0=target[:, t, :],
                                    scalar=source[:, col:col + 1], in1=match[:], op0=ALU.add, op1=ALU.mult))
                                if t:
                                    link(nc.vector.tensor_tensor(weight[:], weight[:], target[:, t, :],
                                                                 ALU.add))
                            link(nc.vector.scalar_tensor_tensor(out=weight[:], in0=weight[:], scalar=0.01,
                                                                in1=weight[:], op0=ALU.mult, op1=ALU.max))
                            link(nc.vector.tensor_scalar(match[:], edge[:], 0.0, None, ALU.is_equal))
                            link(nc.vector.scalar_tensor_tensor(out=weight[:], in0=match[:],
                                                                scalar=NO_EDGE, in1=weight[:],
                                                                op0=ALU.mult, op1=ALU.add))
                            nc.vector.tensor_reduce(neg_max[:], weight[:], axis=AX.X, op=ALU.max,
                                                    negate=True).then_inc(weight_done, 1)
                            dve.wait_ge(product_done, HEADS * n + h + 2)
                            link(nc.vector.reciprocal(inv_sum[:], row_sum[:]))
                            nc.vector.tensor_scalar(o[:, h * HEAD_DIM:(h + 1) * HEAD_DIM],
                                                    o_ps[:, 0:HEAD_DIM], inv_sum[:], None, ALU.mult
                                                    ).then_inc(head_done, 1)
                        dve.wait_ge(head_done, HEADS * (n + 1) + 1)
                        link(nc.vector.tensor_tensor(o[:], o[:], bias_b[:], ALU.add))
                        link(nc.vector.scalar_tensor_tensor(out=o[:], in0=o[:], scalar=0.0, in1=h_own[:],
                                                            op0=ALU.max, op1=ALU.add))
                        link(nc.vector.tensor_reduce(hstat[:, 0, :], by_head(o), axis=AX.X, op=ALU.add))
                        link(nc.vector.scalar_tensor_tensor(
                            out=by_head(o), in0=over_head(hstat[:, 0, :]), scalar=-1.0 / HEAD_DIM,
                            in1=by_head(o), op0=ALU.mult, op1=ALU.add))
                        link(nc.vector.tensor_tensor(sq[:], o[:], o[:], ALU.mult))
                        nc.vector.tensor_reduce(hstat[:, 1, :], by_head(sq), axis=AX.X, op=ALU.add
                                                ).then_inc(var_done, 1)
                        dve.wait_ge(dev_done, n + 1)
                        link(nc.vector.reciprocal(hstat[:, 3, :], hstat[:, 2, :]))
                        link(nc.vector.tensor_tensor(by_head(o), by_head(o), over_head(hstat[:, 3, :]),
                                                     ALU.mult))
                        link(nc.vector.tensor_tensor(o[:], o[:], gamma_b[:], ALU.mult))
                        link(nc.vector.tensor_tensor(o[:], o[:], beta_b[:], ALU.add))
                        nc.vector.tensor_tensor(o[:], o[:], x_own[:], ALU.add).then_inc(y_done, 1)
                        assert links[0] == HEADS * CHAIN + TAIL
                dve.nop()


_INS = ("x", "adj", "L0_gnn_W", "L0_gnn_a_src", "L0_gnn_a_dst", "L0_gnn_bias", "L0_gnn_ln_gamma",
        "L0_gnn_ln_beta")


def kernel(**inputs):
    import numpy as _np
    import concourse.bacc as _bacc
    from concourse import mybir as _mybir
    from concourse.bass_utils import run_bass_kernel_spmd as _run

    nc = _bacc.Bacc("TRN2", target_bir_lowering=False, num_devices=1, dynamic_dma_scratch_size=1024)
    arrays, args = {}, []
    for name in _INS:
        a = _np.ascontiguousarray(inputs[name])
        arrays[name + "_dram"] = a
        args.append(nc.dram_tensor(name + "_dram", a.shape, _mybir.dt.from_np(a.dtype),
                                   kind="ExternalInput").ap())
    shape = inputs["x"].shape
    args.append(nc.dram_tensor("out_dram", shape, _mybir.dt.float32, kind="ExternalOutput").ap())
    build(nc, *args)
    return _run(nc, [arrays], core_ids=[0]).results[0]["out_dram"]
```
